# Optimizing a Trainium2 kernel written in Bass

```python
import numpy as np
import jax
import jax.numpy as jnp

def _softmax(x, axis=-1):
    return jax.nn.softmax(x, axis=axis)

def _gelu(x):
    return jax.nn.gelu(x, approximate=True)

def _silu(x):
    return jax.nn.silu(x)

def _sigmoid(x):
    return jax.nn.sigmoid(x)

def _layernorm(x, axis=-1, eps=1e-05):
    m = jnp.mean(x, axis=axis, keepdims=True)
    v = jnp.var(x, axis=axis, keepdims=True)
    return (x - m) / jnp.sqrt(v + eps)

def _scatter_add(tgt, idx, src, axis=0):
    return tgt.at[idx].add(src)

def _segment_sum(src, seg, n):
    return jax.ops.segment_sum(src, seg, n)
kernel_name = 'mk_perceiver_d2_seqx_r8_82b5a5'

def setup_inputs(seed: int=0):
    np.random.seed(seed)
    _w = jnp.asarray

    def _rec_inputs():
        import jax
        import jax.numpy as jnp
        _rk = jax.random.key(seed)
        x = 7.22e-05 + 1 * jax.random.normal(jax.random.fold_in(_rk, 1), (2, 128, 128), jnp.float32)
        _lenS = 128 - jax.random.randint(jax.random.fold_in(_rk, 7), (2,), 0, max(1, 128 // 4) + 1, jnp.int32)
        _lenS2 = 2048 - jax.random.randint(jax.random.fold_in(_rk, 8), (2,), 0, max(1, 2048 // 4) + 1, jnp.int32)
        _ctx_1024P = jax.random.normal(jax.random.fold_in(_rk, 11), (2, 16, 128), jnp.float32)
        _ctx_1024c = jax.random.dirichlet(jax.random.fold_in(_rk, 511), 0.3 * jnp.ones((16,), jnp.float32), (2, 2048))
        _ctx_1024t = jnp.einsum('bsk,bkd->bsd', _ctx_1024c, _ctx_1024P)
        _ctx_1024t = _ctx_1024t * jax.lax.rsqrt(jnp.mean(jnp.square(_ctx_1024t)) + 1e-12) * 0.953939
        ctx_1024 = 4.13588e-05 + 0.999923 * (_ctx_1024t + 0.3 * jax.random.normal(jax.random.fold_in(_rk, 611), (2, 2048, 128), jnp.float32))
        fside_BxSxS2_0 = jax.random.uniform(jax.random.fold_in(_rk, 13), (2, 128, 2048), jnp.float32, 0.0, 1)
        _validS = jnp.arange(128)[None, :] < _lenS[:, None]
        _validS2 = jnp.arange(2048)[None, :] < _lenS2[:, None]
        _causal = jnp.tril(jnp.ones((128, 128), dtype=bool))
        mask_1xSxS2_if1 = jnp.where(jnp.ones((1, 128, 2048), dtype=bool), 1, 0).astype(jnp.int32)
        mask_BxSxS2_ik1 = jnp.where(jnp.broadcast_to(_validS2[:, None, :], (2, 128, 2048)), 1, 0).astype(jnp.int32)
        return (x, ctx_1024, fside_BxSxS2_0, mask_1xSxS2_if1, mask_BxSxS2_ik1)
    x, ctx_1024, fside_BxSxS2_0, mask_1xSxS2_if1, mask_BxSxS2_ik1 = _rec_inputs()

    def _L0_xattn_setup():
        import jax, jax.numpy as jnp
        import numpy as np
        D_MODEL = 128
        NEG = -1000000000.0
        key = jax.random.key(seed)
        ks = jax.random.split(key, 12)
        B, S, D = (4, 256, D_MODEL)
        s = 1.0 / np.sqrt(D)
        inp = {'query': jax.random.normal(ks[0], (B, S, D), jnp.float32), 'key': jax.random.normal(ks[1], (B, S, D), jnp.float32), 'value': jax.random.normal(ks[2], (B, S, D), jnp.float32), 'mask': jnp.ones((1, S, S), jnp.int32), 'Wq': jax.random.normal(ks[3], (D, D), jnp.float32) * s, 'bq': jnp.zeros((D,), jnp.float32), 'Wk': jax.random.normal(ks[4], (D, D), jnp.float32) * s, 'bk': jnp.zeros((D,), jnp.float32), 'Wv': jax.random.normal(ks[5], (D, D), jnp.float32) * s, 'bv': jnp.zeros((D,), jnp.float32), 'Wo': jax.random.normal(ks[6], (D, D), jnp.float32) * s, 'bo': jnp.zeros((D,), jnp.float32)}
        return inp
    _L0_xattn_all = _L0_xattn_setup()
    _L0_xattn_in = {k: v for k, v in _L0_xattn_all.items() if k in ('Wq', 'bq', 'Wk', 'bk', 'Wv', 'bv', 'Wo', 'bo')}
    del _L0_xattn_all

    def _L0_attn_setup():
        import jax, jax.numpy as jnp
        import numpy as np
        B, T, D, C = (4, 512, 128, 64)
        key = jax.random.key(seed)
        k1, k2, k3 = jax.random.split(key, 3)
        scale = 1.0 / np.sqrt(D)
        return {'out': jax.random.normal(k1, (B, T, D), dtype=jnp.float32), 'W_write': jax.random.normal(k2, (D, D), dtype=jnp.float32) * scale, 'W_read': jax.random.normal(k3, (D, D), dtype=jnp.float32) * scale, 'decay': jnp.asarray(4.6, dtype=jnp.float32), 'log_alpha': jnp.asarray(np.log(0.03), dtype=jnp.float32)}
    _L0_attn_all = _L0_attn_setup()
    _L0_attn_in = {k: v for k, v in _L0_attn_all.items() if k in ('W_write', 'W_read', 'decay', 'log_alpha')}
    del _L0_attn_all

    def _L0_ffn_setup():
        import jax, jax.numpy as jnp
        import numpy as np
        E = 8
        TOP_K = 2
        H = 128
        I = 64
        B, S = (2, 256)

        def _moe_forward(hidden_states, w_gate, w_fc, w_proj):
            b, s, h = hidden_states.shape
            x = hidden_states.reshape(-1, h)
            T = x.shape[0]
            router_logits = x @ w_gate.T
            topk_vals, topk_idx = jax.lax.top_k(router_logits, TOP_K)
            router_weights = jax.nn.softmax(topk_vals.astype(jnp.float32), axis=-1).astype(x.dtype)
            gates = jnp.zeros((T, E), x.dtype).at[jnp.arange(T)[:, None], topk_idx].add(router_weights)
            hmid = jax.nn.gelu(jnp.einsum('th,eih->tei', x, w_fc), approximate=False)
            y = jnp.einsum('tei,ehi->teh', hmid, w_proj)
            out = jnp.einsum('teh,te->th', y, gates)
            return out.reshape(b, s, h)
        key = jax.random.key(seed)
        k0, k1, k2, k3 = jax.random.split(key, 4)
        std = 0.02
        return {'hidden_states': jax.random.normal(k0, (B, S, H), dtype=jnp.float32), 'w_gate': jax.random.normal(k1, (E, H), dtype=jnp.float32) * std, 'w_fc': jax.random.normal(k2, (E, I, H), dtype=jnp.float32) * std, 'w_proj': jax.random.normal(k3, (E, H, I), dtype=jnp.float32) * (std / np.sqrt(48.0))}
    _L0_ffn_all = _L0_ffn_setup()
    _L0_ffn_in = {k: v for k, v in _L0_ffn_all.items() if k in ('w_gate', 'w_fc', 'w_proj')}
    del _L0_ffn_all

    def _L1_xattn_setup():
        import jax, jax.numpy as jnp
        import numpy as np
        NUM_HEADS = 16
        HIDDEN = 128
        B, S = (2, 256)

        def _split_heads(x, H):
            b, s, d = x.shape
            return x.reshape(b, s, H, d // H).transpose(0, 2, 1, 3)
        key = jax.random.key(seed)
        ks = jax.random.split(key, 14)
        D = HIDDEN
        scale = 1.0 / np.sqrt(D)
        inp = {'query': jax.random.normal(ks[0], (B, S, D), jnp.float32), 'key_in': jax.random.normal(ks[1], (B, S, D), jnp.float32), 'value': jax.random.normal(ks[2], (B, S, D), jnp.float32), 'group_prob': jax.random.uniform(ks[3], (B, S, S), jnp.float32), 'mask': jax.random.randint(ks[4], (B, S, S), 0, 2, jnp.int32), 'wq_k': jax.random.normal(ks[5], (D, D), jnp.float32) * scale, 'wq_b': jnp.zeros((D,), jnp.float32), 'wk_k': jax.random.normal(ks[6], (D, D), jnp.float32) * scale, 'wk_b': jnp.zeros((D,), jnp.float32), 'wv_k': jax.random.normal(ks[7], (D, D), jnp.float32) * scale, 'wv_b': jnp.zeros((D,), jnp.float32), 'wo_k': jax.random.normal(ks[8], (D, D), jnp.float32) * scale, 'wo_b': jnp.zeros((D,), jnp.float32)}
        return inp
    _L1_xattn_all = _L1_xattn_setup()
    _L1_xattn_in = {k: v for k, v in _L1_xattn_all.items() if k in ('wq_k', 'wq_b', 'wk_k', 'wk_b', 'wv_k', 'wv_b', 'wo_k', 'wo_b')}
    del _L1_xattn_all

    def _L1_attn_setup():
        import jax, jax.numpy as jnp
        import numpy as np
        import math
        DIM = 128
        ATTN_DIM = 128
        B, S = (2, 512)
        key = jax.random.key(seed)
        k1, k2, k3 = jax.random.split(key, 3)
        x = jax.random.normal(k1, (B, S, DIM), dtype=jnp.float32)
        W_qkv = jax.random.normal(k2, (3 * ATTN_DIM, DIM), dtype=jnp.float32) * (1.0 / math.sqrt(DIM))
        b_qkv = jax.random.normal(k3, (3 * ATTN_DIM,), dtype=jnp.float32) * 0.01
        return {'x': x, 'W_qkv': W_qkv, 'b_qkv': b_qkv}
    _L1_attn_all = _L1_attn_setup()
    _L1_attn_in = {k: v for k, v in _L1_attn_all.items() if k in ('W_qkv', 'b_qkv')}
    del _L1_attn_all

    def _L1_ffn_setup():
        import jax, jax.numpy as jnp
        import numpy as np
        B, N, D = (4, 512, 128)
        E, S, F = (16, 64, 256)
        DO = 128
        EPS = 1e-05

        def _layernorm(x, g, b):
            mu = jnp.mean(x, axis=-1, keepdims=True)
            var = jnp.mean(jnp.square(x - mu), axis=-1, keepdims=True)
            return (x - mu) * jax.lax.rsqrt(var + EPS) * g + b
        key = jax.random.key(seed)
        ks = jax.random.split(key, 8)
        d = {'x': jax.random.normal(ks[0], (B, N, D), dtype=jnp.float32), 'norm_g': jnp.ones((D,), jnp.float32), 'norm_b': jnp.zeros((D,), jnp.float32), 'slot_g': jnp.ones((D,), jnp.float32), 'slot_b': jnp.zeros((D,), jnp.float32), 'scale': jnp.ones((1,), jnp.float32), 'slot_embeds': jax.random.normal(ks[1], (E, S, D), jnp.float32) / np.sqrt(D), 'Wg': jax.random.normal(ks[2], (E, D, F), jnp.float32) * np.sqrt(2.0 / (D + F)), 'bg': jnp.zeros((E, F), jnp.float32), 'Wu': jax.random.normal(ks[3], (E, D, F), jnp.float32) * np.sqrt(2.0 / (D + F)), 'bu': jnp.zeros((E, F), jnp.float32), 'Wd': jax.random.normal(ks[4], (E, F, DO), jnp.float32) * np.sqrt(2.0 / (F + DO)), 'bd': jnp.zeros((E, DO), jnp.float32)}
        return d
    _L1_ffn_all = _L1_ffn_setup()
    _L1_ffn_in = {k: v for k, v in _L1_ffn_all.items() if k in ('norm_g', 'norm_b', 'slot_g', 'slot_b', 'scale', 'slot_embeds', 'Wg', 'bg', 'Wu', 'bu', 'Wd', 'bd')}
    del _L1_ffn_all
    return {'x': x, 'ctx_1024': ctx_1024, 'fside_BxSxS2_0': fside_BxSxS2_0, 'mask_1xSxS2_if1': mask_1xSxS2_if1, 'mask_BxSxS2_ik1': mask_BxSxS2_ik1, 'L0_xattn_Wq': _L0_xattn_in['Wq'], 'L0_xattn_bq': _L0_xattn_in['bq'], 'L0_xattn_Wk': _L0_xattn_in['Wk'], 'L0_xattn_bk': _L0_xattn_in['bk'], 'L0_xattn_Wv': _L0_xattn_in['Wv'], 'L0_xattn_bv': _L0_xattn_in['bv'], 'L0_xattn_Wo': _L0_xattn_in['Wo'], 'L0_xattn_bo': _L0_xattn_in['bo'], 'L0_attn_W_write': _L0_attn_in['W_write'], 'L0_attn_W_read': _L0_attn_in['W_read'], 'L0_attn_decay': _L0_attn_in['decay'], 'L0_attn_log_alpha': _L0_attn_in['log_alpha'], 'L0_ffn_w_gate': _L0_ffn_in['w_gate'], 'L0_ffn_w_fc': _L0_ffn_in['w_fc'], 'L0_ffn_w_proj': _L0_ffn_in['w_proj'], 'L1_xattn_wq_k': _L1_xattn_in['wq_k'], 'L1_xattn_wq_b': _L1_xattn_in['wq_b'], 'L1_xattn_wk_k': _L1_xattn_in['wk_k'], 'L1_xattn_wk_b': _L1_xattn_in['wk_b'], 'L1_xattn_wv_k': _L1_xattn_in['wv_k'], 'L1_xattn_wv_b': _L1_xattn_in['wv_b'], 'L1_xattn_wo_k': _L1_xattn_in['wo_k'], 'L1_xattn_wo_b': _L1_xattn_in['wo_b'], 'L1_attn_W_qkv': _L1_attn_in['W_qkv'], 'L1_attn_b_qkv': _L1_attn_in['b_qkv'], 'L1_ffn_norm_g': _L1_ffn_in['norm_g'], 'L1_ffn_norm_b': _L1_ffn_in['norm_b'], 'L1_ffn_slot_g': _L1_ffn_in['slot_g'], 'L1_ffn_slot_b': _L1_ffn_in['slot_b'], 'L1_ffn_scale': _L1_ffn_in['scale'], 'L1_ffn_slot_embeds': _L1_ffn_in['slot_embeds'], 'L1_ffn_Wg': _L1_ffn_in['Wg'], 'L1_ffn_bg': _L1_ffn_in['bg'], 'L1_ffn_Wu': _L1_ffn_in['Wu'], 'L1_ffn_bu': _L1_ffn_in['bu'], 'L1_ffn_Wd': _L1_ffn_in['Wd'], 'L1_ffn_bd': _L1_ffn_in['bd']}

def reference(x, ctx_1024, fside_BxSxS2_0, mask_1xSxS2_if1, mask_BxSxS2_ik1, L0_xattn_Wq, L0_xattn_bq, L0_xattn_Wk, L0_xattn_bk, L0_xattn_Wv, L0_xattn_bv, L0_xattn_Wo, L0_xattn_bo, L0_attn_W_write, L0_attn_W_read, L0_attn_decay, L0_attn_log_alpha, L0_ffn_w_gate, L0_ffn_w_fc, L0_ffn_w_proj, L1_xattn_wq_k, L1_xattn_wq_b, L1_xattn_wk_k, L1_xattn_wk_b, L1_xattn_wv_k, L1_xattn_wv_b, L1_xattn_wo_k, L1_xattn_wo_b, L1_attn_W_qkv, L1_attn_b_qkv, L1_ffn_norm_g, L1_ffn_norm_b, L1_ffn_slot_g, L1_ffn_slot_b, L1_ffn_scale, L1_ffn_slot_embeds, L1_ffn_Wg, L1_ffn_bg, L1_ffn_Wu, L1_ffn_bu, L1_ffn_Wd, L1_ffn_bd):
    import jax
    import jax.numpy as jnp

    def _L0_xattn_ref(query, key, value, mask, Wq, bq, Wk, bk, Wv, bv, Wo, bo):
        import jax, jax.numpy as jnp
        import numpy as np
        D_MODEL = 128
        NEG = -1000000000.0
        q = query @ Wq + bq
        k = key @ Wk + bk
        v = value @ Wv + bv
        d_k = q.shape[-1]
        scores = jnp.einsum('bsd,btd->bst', q, k) / jnp.sqrt(jnp.float32(d_k))
        scores = jnp.where(mask == 0, jnp.float32(NEG), scores)
        p_attn = jax.nn.softmax(scores, axis=-1)
        x = jnp.einsum('bst,btd->bsd', p_attn, v)
        return x @ Wo + bo

    def _L0_attn_ref(out, W_write, W_read, decay, log_alpha):
        import jax, jax.numpy as jnp
        import numpy as np
        B, T, D, C = (4, 512, 128, 64)
        Bq, Tq, Dq = out.shape
        n_chunks = Tq // C
        out32 = out.astype(jnp.float32)
        gamma = jax.nn.sigmoid(decay)
        log_gamma = jnp.log(gamma)
        v = jnp.einsum('btd,ed->bte', out32, W_write)
        wk = jnp.pad(out32[:, :-1], ((0, 0), (1, 0), (0, 0)))
        rk = out32

        def to_chunks(x):
            return x.reshape(Bq, n_chunks, C, Dq).transpose(1, 0, 2, 3)
        rk_ch, wk_ch, v_ch = (to_chunks(rk), to_chunks(wk), to_chunks(v))
        p = jnp.arange(C)
        diffs = jnp.clip(p[:, None] - 1 - p[None, :], 0)
        causal = p[:, None] > p[None, :]
        M = jnp.exp(diffs.astype(jnp.float32) * log_gamma) * causal
        gp = gamma ** p
        gw = gamma ** (C - 1 - p)
        gC = gamma ** C

        def step(W, xs):
            rk_c, wk_c, v_c = xs
            inter = jnp.einsum('bij,bcj->bci', W, rk_c) * gp[None, :, None]
            S = jnp.einsum('bcd,bkd->bck', rk_c, wk_c)
            intra = jnp.einsum('bck,bkd->bcd', S * M, v_c)
            reads = inter + intra
            W = gC * W + jnp.einsum('bcd,bce->bde', v_c * gw[None, :, None], wk_c)
            return (W, reads)
        W0 = jnp.zeros((Bq, Dq, Dq), dtype=jnp.float32)
        _, reads = jax.lax.scan(step, W0, (rk_ch, wk_ch, v_ch))
        reads = reads.transpose(1, 0, 2, 3).reshape(Bq, Tq, Dq)
        alpha = jnp.exp(log_alpha)
        read_out = jnp.einsum('btd,ed->bte', reads, W_read)
        return out + alpha * read_out.astype(out.dtype)

    def _L0_ffn_ref(hidden_states, w_gate, w_fc, w_proj):
        import jax, jax.numpy as jnp
        import numpy as np
        E = 8
        TOP_K = 2
        H = 128
        I = 64
        B, S = (2, 256)

        def _moe_forward(hidden_states, w_gate, w_fc, w_proj):
            b, s, h = hidden_states.shape
            x = hidden_states.reshape(-1, h)
            T = x.shape[0]
            router_logits = x @ w_gate.T
            topk_vals, topk_idx = jax.lax.top_k(router_logits, TOP_K)
            router_weights = jax.nn.softmax(topk_vals.astype(jnp.float32), axis=-1).astype(x.dtype)
            gates = jnp.zeros((T, E), x.dtype).at[jnp.arange(T)[:, None], topk_idx].add(router_weights)
            hmid = jax.nn.gelu(jnp.einsum('th,eih->tei', x, w_fc), approximate=False)
            y = jnp.einsum('tei,ehi->teh', hmid, w_proj)
            out = jnp.einsum('teh,te->th', y, gates)
            return out.reshape(b, s, h)
        return _moe_forward(hidden_states, w_gate, w_proj=w_proj, w_fc=w_fc)

    def _L1_xattn_ref(query, key_in, value, group_prob, mask, wq_k, wq_b, wk_k, wk_b, wv_k, wv_b, wo_k, wo_b):
        import jax, jax.numpy as jnp
        import numpy as np
        NUM_HEADS = 16
        HIDDEN = 128
        B, S = (2, 256)

        def _split_heads(x, H):
            b, s, d = x.shape
            return x.reshape(b, s, H, d // H).transpose(0, 2, 1, 3)
        H = NUM_HEADS
        dh = query.shape[-1] // H
        q = _split_heads(query @ wq_k + wq_b, H)
        k = _split_heads(key_in @ wk_k + wk_b, H)
        v = _split_heads(value @ wv_k + wv_b, H)
        logits = jnp.einsum('bhqd,bhkd->bhqk', q, k) / jnp.sqrt(jnp.asarray(dh, q.dtype))
        neg = (1.0 - mask.astype(q.dtype)) * -1000000000.0
        logits = logits + neg[:, None, :, :]
        attn = jax.nn.softmax(logits, axis=-1)
        attn = attn * group_prob[:, None, :, :]
        out = jnp.einsum('bhqk,bhkd->bhqd', attn, v)
        out = out.transpose(0, 2, 1, 3).reshape(query.shape[0], -1, H * dh)
        return out @ wo_k + wo_b

    def _L1_attn_ref(x, W_qkv, b_qkv):
        import jax, jax.numpy as jnp
        import numpy as np
        import math
        DIM = 128
        ATTN_DIM = 128
        B, S = (2, 512)
        b, s, d = x.shape
        qkv = jnp.einsum('bsd,ed->bse', x, W_qkv) + b_qkv
        q, k, v = jnp.split(qkv, 3, axis=-1)
        score = jnp.einsum('bqd,bkd->bqk', q, k)
        causal = jnp.tril(jnp.ones((s, s), dtype=bool))
        score = jnp.where(causal, score, -jnp.inf)
        attn = jax.nn.softmax(score / math.sqrt(ATTN_DIM), axis=-1)
        y = jnp.einsum('bqk,bkd->bqd', attn, v)
        return y

    def _L1_ffn_ref(x, norm_g, norm_b, slot_g, slot_b, scale, slot_embeds, Wg, bg, Wu, bu, Wd, bd):
        import jax, jax.numpy as jnp
        import numpy as np
        B, N, D = (4, 512, 128)
        E, S, F = (16, 64, 256)
        DO = 128
        EPS = 1e-05

        def _layernorm(x, g, b):
            mu = jnp.mean(x, axis=-1, keepdims=True)
            var = jnp.mean(jnp.square(x - mu), axis=-1, keepdims=True)
            return (x - mu) * jax.lax.rsqrt(var + EPS) * g + b
        x = _layernorm(x, norm_g, norm_b)
        se = _layernorm(slot_embeds, slot_g, slot_b) * scale
        logits = jnp.einsum('bnd,esd->bnes', x, se)
        dispatch = jax.nn.softmax(logits, axis=1)
        combine = jax.nn.softmax(logits.reshape(x.shape[0], x.shape[1], -1), axis=-1)
        slots = jnp.einsum('bnd,bnes->besd', x, dispatch)
        gate = jax.nn.gelu(jnp.einsum('besd,edf->besf', slots, Wg) + bg[None, :, None, :], approximate=False)
        up = jnp.einsum('besd,edf->besf', slots, Wu) + bu[None, :, None, :]
        eout = jnp.einsum('besf,efo->beso', gate * up, Wd) + bd[None, :, None, :]
        eout = eout.reshape(eout.shape[0], -1, eout.shape[-1])
        return jnp.einsum('bns,bso->bno', combine, eout)
    x = x + _L0_xattn_ref(_layernorm(x, axis=-1), ctx_1024, ctx_1024, mask_1xSxS2_if1, L0_xattn_Wq, L0_xattn_bq, L0_xattn_Wk, L0_xattn_bk, L0_xattn_Wv, L0_xattn_bv, L0_xattn_Wo, L0_xattn_bo)
    x = x + _L0_attn_ref(_layernorm(x, axis=-1), L0_attn_W_write, L0_attn_W_read, L0_attn_decay, L0_attn_log_alpha)
    x = x + _L0_ffn_ref(_layernorm(x, axis=-1), L0_ffn_w_gate, L0_ffn_w_fc, L0_ffn_w_proj)
    x = x + _L1_xattn_ref(_layernorm(x, axis=-1), ctx_1024, ctx_1024, fside_BxSxS2_0, mask_BxSxS2_ik1, L1_xattn_wq_k, L1_xattn_wq_b, L1_xattn_wk_k, L1_xattn_wk_b, L1_xattn_wv_k, L1_xattn_wv_b, L1_xattn_wo_k, L1_xattn_wo_b)
    x = x + _L1_attn_ref(_layernorm(x, axis=-1), L1_attn_W_qkv, L1_attn_b_qkv)
    x = x + _L1_ffn_ref(_layernorm(x, axis=-1), L1_ffn_norm_g, L1_ffn_norm_b, L1_ffn_slot_g, L1_ffn_slot_b, L1_ffn_scale, L1_ffn_slot_embeds, L1_ffn_Wg, L1_ffn_bg, L1_ffn_Wu, L1_ffn_bu, L1_ffn_Wd, L1_ffn_bd)
    return x

_drawn_inputs = setup_inputs


def setup_inputs(seed=0):
    import zlib

    import numpy as np

    out = dict(_drawn_inputs(seed))
    spreads = {'L0_xattn_bq': (0.0, 0.1),
     'L0_xattn_bk': (0.0, 2.0),
     'L0_xattn_bv': (0.0, 0.1),
     'L0_xattn_bo': (0.0, 0.1),
     'L1_xattn_wq_b': (0.0, 0.8),
     'L1_xattn_wk_b': (0.0, 2.0),
     'L1_xattn_wv_b': (0.0, 0.8),
     'L1_xattn_wo_b': (0.0, 2.0),
     'L1_ffn_norm_g': (1.0, 0.6),
     'L1_ffn_norm_b': (0.0, 2.0),
     'L1_ffn_slot_g': (1.0, 0.6),
     'L1_ffn_slot_b': (0.0, 2.0),
     'L1_ffn_bg': (0.0, 2.0),
     'L1_ffn_bu': (0.0, 2.0),
     'L1_ffn_bd': (0.0, 2.0)}
    factors = {'fside_BxSxS2_0': 8.0,
     'L0_ffn_w_gate': 8.0,
     'L0_ffn_w_fc': 8.0,
     'L0_ffn_w_proj': 8.0,
     'L1_xattn_wq_k': 8.0,
     'L1_xattn_wk_k': 7.814,
     'L1_xattn_wv_k': 3.676,
     'L1_xattn_wo_k': 3.737,
     'L1_attn_b_qkv': 64.0,
     'L1_attn_W_qkv': 7.047,
     'L1_ffn_Wg': 3.505,
     'L1_ffn_Wu': 3.124}
    for name, (base, spread) in spreads.items():
        noise = np.random.default_rng([zlib.crc32(name.encode()), seed]).standard_normal(out[name].shape)
        drawn = base * np.exp(spread * noise) if base else spread * noise
        out[name] = jnp.asarray(drawn.astype(out[name].dtype))
    for name, factor in factors.items():
        out[name] = (out[name] * factor).astype(out[name].dtype)
    return out
```

```python
from contextlib import ExitStack

import concourse.bass as bass
from concourse import mybir

ALU = mybir.AluOpType
ACT = mybir.ActivationFunctionType
AX_X = mybir.AxisListType.X
F32 = mybir.dt.float32
BF16 = mybir.dt.bfloat16
I32 = mybir.dt.int32

B, N, D, T = 2, 128, 128, 2048
C = T // 128
HALF = T // 2
HEADS, DH = 16, 8
PARTS = 3
ROWS = PARTS * PARTS * DH
E0, I0 = 8, 64
E1, SLOTS, F1 = 16, 64, 256
NS = E1 * SLOTS
EPS = 1e-5
MASKED = 1e9
CAUSAL = 1e30
FAR = 3e38
ITEMS = B * HEADS
RING = 4
S0_SCALE = float(D) ** -0.5
S1_SCALE = float(DH) ** -0.5

FIRST = (("ident", 128), ("x", B * D), ("wq_t", 128), ("wk_t", 128), ("wv_t", 128), ("wo", 128), ("bo_rows", 128),
         ("bq", 1), ("bk", 1), ("bv", 1), ("decay", 1), ("log_alpha", 1), ("wk1_b", 1))
SECOND = (("wk1", 128), ("wv1", 128), ("wv1_b_rows", 128), ("steps", 128), ("causal", 128), ("ww_t", 128), ("wr_t", 128),
          ("wgate_t", E0), ("lower", E0 * E0), ("wfc_t", E0 * I0), ("wproj_t", E0 * I0))
THIRD = (("wq1", 128), ("wo1", 128), ("wo1_b_rows", 128), ("wqkv_t", 384), ("bv_rows", 128), ("future", 128),
         ("select", 4 * DH), ("norm_g_rows", 128), ("norm_b_rows", 128), ("bg", 2 * E1), ("bu", 2 * E1),
         ("wq1_b", 1), ("bq_self", 1), ("bk_self", 1), ("norm_g", 1), ("norm_b", 1), ("slot_g", 1), ("slot_b", 1), ("scale", 1))

SIGNALS = """
first_in second_in third_in ctxt_in0 ctxt_in1 ctxr_in mask0_in mask1_in g_in slots_in wg_in wu_in wd_in bd_in
ones_set dve_chain pool_chain
var_ready rstd_ready xn_ready xnt_psum xnt_ready
fold_src fold_psum fold_ready qp_psum qp_ready row_psum xb_ready
mask1_ready s0_psum s0_masked s0_args s0_exp pt0_psum pt0_ready o0_psum o0_ready y0_psum x_ready
kp_psum kp_copied k_parts k_saved keys_in0 keys_in1 keys_in2 keys_in3 vp_psum v_ready
decay_exp decay_one decay_log decay_ready v0_psum v0_ready st_psum sm_ready rd_psum rd_ready ro_psum
h0_psum rl_psum logits_max router_exp gates_ready gelu0_ready hw_ready ht_psum ht_ready f0_psum
q1_psum q_parts q_saved queries_in
scores_psum scores_masked exp_ready pt_psum pt_copied pg_dve pg_pool pv_psum heads_copied heads_psum
at_ready att_psum att_ready wo_psum
q2_psum k2_psum v2_psum q2_ready k2_ready v2_ready cs_psum cs_masked cs_exp pst_psum pst_ready ys_psum
se_rstd se_ready se_psum set_ready xf_ready xft_ready
ln_psum ln_max combine_exp ls_psum ls_shift dispatch_exp dispatch_ready dt_psum dt_dve dt_act ct_psum ct_dve ct_act
sl_psum sl_dve sl_act g_psum u_psum gate_ready hmid_ready eo_psum eo_ready y_psum out_ready out_saved
""".split()


def columns(packed, names):
    views, at = {}, 0
    for name, n in names:
        views[name] = packed[:, at:at + n]
        at += n
    return views


def build(nc, a, out, k_dram, q_dram):
    with ExitStack() as ctx:
        def sb(name, shape, dt=F32):
            return ctx.enter_context(nc.sbuf_tensor(name, shape, dt))

        s = {name: ctx.enter_context(nc.semaphore(name)) for name in SIGNALS}
        keys_in = [s[f"keys_in{i}"] for i in range(RING)]

        first = sb("first", [128, sum(n for _, n in FIRST)])
        second = sb("second", [128, sum(n for _, n in SECOND)])
        third = sb("third", [128, sum(n for _, n in THIRD)])
        w = {**columns(first, FIRST), **columns(second, SECOND), **columns(third, THIRD)}
        ident = w["ident"]
        ones = sb("ones", [128, 128])
        minus_half = sb("minus_half", [128, 8])
        ctx_t = sb("ctx_t", [128, B, T])
        ctx_r = sb("ctx_r", [128, B, C, D])
        g_t = sb("g_t", [128, B, C, N])
        mask1 = sb("mask1", [128, B, T])
        k_parts = sb("k_parts", [128, PARTS, B, T], BF16)
        keys = sb("keys", [ROWS, RING, T], BF16)
        queries = sb("queries", [ROWS, HEADS, B * N], BF16)
        v = sb("v", [128, B, C, D])
        lg = sb("lg", [128, 2, T])
        pg = sb("pg", [128, 2, T])
        pc = sb("pc", [128, 2, 512])
        se_t = sb("se_t", [128, NS])
        mask0 = g_t[:, 1].rearrange("p c n -> p (c n)")
        k_full = g_t[:, 0].rearrange("p (u c) n -> p u (c n)", u=2)
        se = pc[:, :, :].rearrange("p a (k d) -> p (a k) d", d=D)
        wg = ctx_t[:, :, :].rearrange("p b t -> p (b t)").rearrange("p (e f) -> p e f", e=E1)
        wu = ctx_r[:, :, :, :].rearrange("p b c d -> p (b c d)").rearrange("p (e f) -> p e f", e=E1)
        kw = k_parts[:, :, :, :].rearrange("p a b t -> p (a b t)").bitcast(F32)
        wd = kw[:, 0:E1 * 2 * D].rearrange("p (e k o) -> p e k o", e=E1, k=2)
        bd = kw[:, E1 * 2 * D:].rearrange("p (e o) -> p e o", e=E1)

        x = [w["x"].rearrange("p (b d) -> p b d", b=B)] + [sb(f"x{i}", [128, B, D])[:, :, :] for i in range(1, 6)]
        xb = sb("xb", [128, B, D])
        xn = sb("xn", [128, B, D])
        xnt = sb("xnt", [128, B, N + 2])
        stats = sb("stats", [128, 8, 6])
        mv = sb("mv", [128, 8, 2])
        ve = sb("ve", [128, 8])
        rstd = sb("rstd", [128, 8])
        folds = sb("folds", [128, 388])
        wob = sb("wob", [128, 128])
        t0 = sb("t0", [128, B * N])
        t1 = sb("t1", [128, B * N])
        t2 = sb("t2", [128, B * N])
        q_split = sb("q_split", [128, PARTS, B * N], BF16)
        heads_sb = sb("heads_sb", [128, 512])
        cols = sb("cols", [128, 96])
        m0 = cols[:, 0:4]
        flag, nflag, bias0, m0c, den0, rinv0 = (cols[:, 4 + 2 * i:6 + 2 * i] for i in range(6))
        rowc = cols[:, 16:18]
        bqbk = cols[:, 18:19]
        alpha, lgam, e1col = cols[:, 19:20], cols[:, 20:21], cols[:, 21:22]
        m2, den2, rinv2 = cols[:, 22:24], cols[:, 24:26], cols[:, 26:28]
        m_c, den_c, rinv_c = cols[:, 28:30], cols[:, 30:32], cols[:, 32:34]
        sg, sbias = cols[:, 34:35], cols[:, 35:36]
        mn = cols[:, 36:40]
        d_max, d_sum = cols[:, 40:56], cols[:, 56:72]
        den1 = sb("den1", [128, ITEMS])
        rinv1 = sb("rinv1", [128, ITEMS])
        router = sb("router", [128, 8, B * E0])
        versus = sb("versus", [128, 3, B * E0 * E0])

        ps = ctx.enter_context(nc.psum_tensor("ps", [128, 8, 512], F32))

        def wide(slot):
            return ps[:, 2 * slot:2 * slot + 2, :].rearrange("p a n -> p (a n)")

        combine = lg[:, 0, :].rearrange("p (e b n) -> p e b n", e=E1, b=B)
        combine_t = lg[:, 1, :].rearrange("p (e n) -> p e n", e=E1)
        dispatch_t = pg[:, 0, :].rearrange("p (k n) -> p k n", k=16)
        dispatch = pg[:, 1, :].rearrange("p (b n) -> p b n", b=B)
        slots_t = mask1[:, 0, :].rearrange("p (e b n) -> p e b n", e=E1, b=B)
        gate_h = mask1[:, 1, 0:512].rearrange("p (s k n) -> p s k n", s=2, k=2)
        hmid = mask1[:, 1, 512:1024].rearrange("p (s k n) -> p s k n", s=2, k=2)
        eo = mask1[:, 1, 1024:1280].rearrange("p (s n) -> p s n", s=2)
        hid = lg[:, 0, 0:1024]
        hid_t = lg[:, 1, 0:1024].rearrange("p (b k n) -> p b k n", b=B, k=4)

        def xt(b):
            return xnt[:, b, 1:N + 1]

        xt2 = xnt[:, :, 1:N + 1]
        block = ctx.enter_context(nc.Block())

        @block.sync
        def _(sp):
            sp.dma_start(first[:, :], a["first"]).then_inc(s["first_in"], 16)
            sp.dma_start(ctx_t[:, 0, :], a["ctx_t"][:, 0, :]).then_inc(s["ctxt_in0"], 16)
            sp.dma_start(mask0.bitcast(I32), a["mask0"]).then_inc(s["mask0_in"], 16)
            sp.dma_start(ctx_t[:, 1, :], a["ctx_t"][:, 1, :]).then_inc(s["ctxt_in1"], 16)
            sp.dma_start(second[:, :], a["second"]).then_inc(s["second_in"], 16)
            sp.dma_start(ctx_r[:, :, :, :], a["ctx_r"]).then_inc(s["ctxr_in"], 16)
            sp.dma_start(se, a["slots"]).then_inc(s["slots_in"], 16)
            sp.dma_start(third[:, :], a["third"]).then_inc(s["third_in"], 16)
            sp.dma_start(mask1[:, :, :].bitcast(I32), a["mask1"]).then_inc(s["mask1_in"], 16)
            for b in range(B):
                sp.wait_ge(s["k_parts"], 2 * b + 2)
                sp.dma_start(k_dram[b].rearrange("a r t -> r a t"), k_parts[:, :, b, :]).then_inc(s["k_saved"], 16)
            sp.wait_ge(s["s0_masked"], 4)
            sp.dma_start(g_t[:, :, :, :], a["g_t"]).then_inc(s["g_in"], 16)

            def load_keys(i):
                b, h = i // HEADS, i % HEADS
                for r in range(PARTS):
                    sp.dma_start(keys[24 * r:24 * r + 24, i % RING, :], k_dram[b, :, DH * h:DH * h + DH, :])\
                      .then_inc(keys_in[i % RING], 16)

            sp.wait_ge(s["k_saved"], 32)
            for i in range(RING):
                load_keys(i)
            sp.wait_ge(s["q_parts"], 1)
            sp.dma_start(q_dram.rearrange("a r n -> r a n"), q_split[:, :, :]).then_inc(s["q_saved"], 16)
            sp.wait_ge(s["q_saved"], 16)
            for r in range(PARTS):
                for p in range(PARTS):
                    sp.dma_start(queries[24 * r + 8 * p:24 * r + 8 * p + 8, :, :],
                                 q_dram[r].rearrange("(h d) n -> d h n", d=DH)).then_inc(s["queries_in"], 16)
            sp.wait_ge(s["vp_psum"], 4)
            sp.dma_start(wg, a["wg"]).then_inc(s["wg_in"], 16)
            sp.wait_ge(s["o0_psum"], 2)
            sp.dma_start(wu, a["wu"]).then_inc(s["wu_in"], 16)
            sp.dma_start(wd, a["wd"]).then_inc(s["wd_in"], 16)
            sp.dma_start(bd, a["bd"]).then_inc(s["bd_in"], 16)
            for i in range(RING, ITEMS):
                sp.wait_ge(s["scores_psum"], 2 * (i - RING) + 2)
                load_keys(i)
            sp.wait_ge(s["out_ready"], 2)
            sp.dma_start(out.rearrange("b n d -> n b d"), x[4]).then_inc(s["out_saved"], 16)
            sp.wait_ge(s["out_saved"], 16)

        @block.gpsimd
        def _(pool):
            chain = [0]

            def link(ins):
                chain[0] += 1
                ins.then_inc(s["pool_chain"], 1)
                pool.wait_ge(s["pool_chain"], chain[0])

            def inverse_root(k, n=B):
                pool.wait_ge(s["var_ready"], k + 1)
                pool.tensor_tensor(rstd[:, 0:n], ve[:, 0:n], minus_half[:, 0:n], ALU.pow).then_inc(s["rstd_ready"], 1)

            link(pool.memset(minus_half[:, :], -0.5))
            pool.memset(ones[:, :], 1.0).then_inc(s["ones_set"], 1)
            pool.memset(xnt[:, :, 0:1], 0.0).then_inc(s["ones_set"], 1)
            inverse_root(0)
            def split(kb):
                b, half = kb // 2, kb % 2
                part = [k_parts[:, p, b, half * HALF:(half + 1) * HALF] for p in range(PARTS)]
                rest = k_full[:, kb % 2, :]
                pool.wait_ge(s["kp_copied"], kb + 1)
                link(pool.tensor_tensor(rest, rest, part[0], ALU.subtract))
                link(pool.tensor_scalar(part[1], rest, 1.0, 0.0, ALU.mult, ALU.add))
                pool.tensor_tensor(part[2], rest, part[1], ALU.subtract).then_inc(s["k_parts"], 1)
            split(0)
            split(1)
            inverse_root(1)
            split(2)
            inverse_root(2, 8)
            split(3)
            inverse_root(3)
            inverse_root(4)
            pool.wait_ge(s["mask1_in"], 16)
            pool.tensor_scalar(mask1[:, :, :], mask1[:, :, :].bitcast(I32), -MASKED, MASKED, ALU.mult, ALU.add)\
                .then_inc(s["mask1_ready"], 1)
            pool.wait_ge(s["g_in"], 16)
            for i in range(ITEMS):
                for n, q in enumerate((1, 3)):
                    pool.wait_ge(s["pt_copied"], 2 * i + n + 1)
                    if n == 0 and i >= 2:
                        pool.wait_ge(s["pv_psum"], i - 1)
                    g = g_t[:, i // HEADS].rearrange("p c n -> p (c n)")[:, q * 512:(q + 1) * 512]
                    pool.tensor_tensor(pg[:, i % 2, q * 512:(q + 1) * 512], pc[:, n, :], g, ALU.mult)\
                        .then_inc(s["pg_pool"], 1)
            inverse_root(5)
            inverse_root(6)

        @block.scalar
        def _(act):
            act.wait_ge(s["first_in"], 16)
            act.activation(e1col, w["decay"], ACT.Exp, scale=-1.0).then_inc(s["decay_exp"], 1)
            act.activation(alpha, w["log_alpha"], ACT.Exp).then_inc(s["decay_exp"], 1)
            act.wait_ge(s["decay_one"], 1)
            act.activation(lgam, e1col, ACT.Ln).then_inc(s["decay_log"], 1)
            act.wait_ge(s["decay_log"], 1)
            act.wait_ge(s["second_in"], 16)
            act.wait_ge(s["decay_one"], 2)
            act.activation(w["steps"], w["steps"], ACT.Exp, scale=lgam).then_inc(s["decay_log"], 1)
            for b in range(B):
                act.wait_ge(s["s0_args"], b + 1)
                act.activation(lg[:, b, :], lg[:, b, :], ACT.Exp, bias=bias0[:, b:b + 1], scale=nflag[:, b:b + 1],
                               accum_out=den0[:, b:b + 1]).then_inc(s["s0_exp"], 1)
            for kb in range(4):
                b, half = kb // 2, kb % 2
                act.wait_ge(s["kp_psum"], kb + 1)
                if kb >= 2:
                    act.wait_ge(s["k_parts"], kb - 1)
                act.activation(k_full[:, kb % 2, :], wide(kb % 2), ACT.Identity, bias=w["wk1_b"])
                act.activation(k_parts[:, 0, b, half * HALF:(half + 1) * HALF], wide(kb % 2), ACT.Identity,
                               bias=w["wk1_b"]).then_inc(s["kp_copied"], 1)
            act.wait_ge(s["logits_max"], 1)
            act.activation(router[:, 2, :], router[:, 1, :], ACT.Exp).then_inc(s["router_exp"], 1)
            act.wait_ge(s["h0_psum"], 1)
            act.activation(hid, ps[:, 4:6, :].rearrange("p a n -> p (a n)"), ACT.Gelu).then_inc(s["gelu0_ready"], 1)

            def exponentials(i):
                act.wait_ge(s["scores_masked"], 2 * i + 2)
                act.activation(lg[:, i % 2, :], lg[:, i % 2, :], ACT.Exp, bias=mn[:, 2 * (i % 2) + 1:2 * (i % 2) + 2],
                               scale=-1.0, accum_out=den1[:, i:i + 1]).then_inc(s["exp_ready"], 1)

            exponentials(0)
            for i in range(ITEMS):
                for n in range(2):
                    act.wait_ge(s["pt_psum"], 4 * i + 2 * n + 2)
                    if i > 0:
                        act.wait_ge(s["pg_pool"], 2 * (i - 1) + n + 1)
                    act.activation(pc[:, n, :], ps[:, 5, :], ACT.Copy).then_inc(s["pt_copied"], 1)
                if i + 1 < ITEMS:
                    exponentials(i + 1)
                if i % 4 == 0 and i:
                    act.wait_ge(s["pv_psum"], i)
                    act.activation(heads_sb[:, :], ps[:, 6, :], ACT.Copy).then_inc(s["heads_copied"], 1)
            act.wait_ge(s["pv_psum"], ITEMS)
            act.wait_ge(s["heads_psum"], ITEMS // 4 - 1)
            act.activation(heads_sb[:, :], ps[:, 6, :], ACT.Copy).then_inc(s["heads_copied"], 1)
            act.wait_ge(s["k2_psum"], 1)
            act.activation(t1[:, :], ps[:, 5, 0:256], ACT.Identity, bias=w["bk_self"]).then_inc(s["k2_ready"], 1)
            for b in range(B):
                act.wait_ge(s["cs_masked"], b + 1)
                act.activation(lg[:, 0, b * N:(b + 1) * N], lg[:, 0, b * N:(b + 1) * N], ACT.Exp, bias=m2[:, b:b + 1],
                               scale=-1.0, accum_out=den2[:, b:b + 1]).then_inc(s["cs_exp"], 1)
            for b in range(B):
                act.wait_ge(s["ln_max"], b + 1)
                act.activation(combine[:, :, b, :], wide(b).rearrange("p (e n) -> p e n", e=E1), ACT.Exp, bias=m_c[:, b:b + 1],
                               accum_out=den_c[:, b:b + 1]).then_inc(s["combine_exp"], 1)
            act.wait_ge(s["ls_shift"], 1)
            act.activation(pg[:, 0, :], pg[:, 0, :], ACT.Exp).then_inc(s["dispatch_exp"], 1)
            act.wait_ge(s["ct_psum"], 1)
            act.activation(lg[:, 1, 1024:2048], wide(3), ACT.Copy).then_inc(s["ct_act"], 1)
            act.wait_ge(s["dt_psum"], 1)
            act.activation(dispatch[:, 1, :], wide(1), ACT.Copy).then_inc(s["dt_act"], 1)
            act.wait_ge(s["sl_psum"], 2)
            act.activation(slots_t[:, :, 1, :], wide(1).rearrange("p (e n) -> p e n", e=E1), ACT.Copy)\
               .then_inc(s["sl_act"], 1)
            for e in range(E1):
                act.wait_ge(s["g_psum"], e + 1)
                if e >= 2:
                    act.wait_ge(s["hmid_ready"], 2 * (e - 1))
                for k in range(2):
                    act.activation(gate_h[:, e % 2, k, :], ps[:, 4 + e % 2, k * 128:(k + 1) * 128], ACT.Gelu,
                                   bias=w["bg"][:, 2 * e + k:2 * e + k + 1]).then_inc(s["gate_ready"], 1)

        @block.vector
        def _(dve):
            chain = [0]

            def link(ins):
                chain[0] += 1
                ins.then_inc(s["dve_chain"], 1)
                dve.wait_ge(s["dve_chain"], chain[0])

            norms = [0]

            def normalise(xin, xout, k, n=B):
                for b in range(n):
                    link(dve.bn_stats(stats[:, b, :], xin[:, b, :]))
                    link(dve.bn_aggr(mv[:, b, :], stats[:, b, :]))
                dve.tensor_scalar(ve[:, 0:n], mv[:, 0:n, 1:2].rearrange("p b o -> p (b o)"), EPS, None, ALU.add)\
                   .then_inc(s["var_ready"], 1)
                dve.wait_ge(s["rstd_ready"], k + 1)
                for b in range(n):
                    ins = dve.tensor_scalar(xout[:, b, :], xin[:, b, :], mv[:, b, 0:1], rstd[:, b:b + 1],
                                            ALU.subtract, ALU.mult)
                    if n == B:
                        ins.then_inc(s["xn_ready"], 1)
                    else:
                        ins.then_inc(s["se_ready"], 1)

            def keep_transpose(k):
                dve.wait_ge(s["xnt_psum"], k + 1)
                dve.tensor_copy(xt2, ps[:, 6, 0:256].rearrange("p (b n) -> p b n", b=B)).then_inc(s["xnt_ready"], 1)

            dve.wait_ge(s["first_in"], 16)
            dve.tensor_tensor(t2[:, 0:1], w["bq"], w["bk"], ALU.mult).then_inc(s["fold_src"], 1)
            dve.tensor_scalar(wob[:, :], w["wo"], w["bv"], None, ALU.mult).then_inc(s["fold_src"], 1)
            normalise(x[0], xn, 0)
            dve.wait_ge(s["fold_psum"], 1)
            dve.tensor_copy(folds[:, 0:387], ps[:, 7, 0:387]).then_inc(s["fold_ready"], 1)
            dve.wait_ge(s["ones_set"], 2)
            keep_transpose(0)
            dve.wait_ge(s["decay_exp"], 1)
            dve.tensor_scalar(e1col, e1col, 1.0, None, ALU.add).then_inc(s["decay_one"], 1)
            dve.wait_ge(s["fold_ready"], 1)
            dve.wait_ge(s["qp_psum"], 1)
            dve.tensor_scalar(t0[:, :], ps[:, 4, 0:256], folds[:, 384:385], -S0_SCALE, ALU.add, ALU.mult)\
               .then_inc(s["qp_ready"], 1)
            dve.wait_ge(s["row_psum"], 1)
            link(dve.tensor_scalar(rowc, ps[:, 5, 0:2], folds[:, 386:387], -S0_SCALE, ALU.add, ALU.mult))
            link(dve.tensor_tensor(xb[:, :, :], x[0], w["bo_rows"].unsqueeze(1).to_broadcast([128, B, D]), ALU.add))
            link(dve.tensor_tensor(xb[:, :, :], xb[:, :, :],
                                   folds[:, 256:384].unsqueeze(1).to_broadcast([128, B, D]), ALU.add))
            dve.wait_ge(s["mask0_in"], 16)
            link(dve.tensor_scalar(mask0, mask0.bitcast(I32), 0, MASKED, ALU.is_equal, ALU.mult))
            for b in range(B):
                for half in range(2):
                    u = 2 * b + half
                    dve.wait_ge(s["s0_psum"], u + 1)
                    dve.tensor_tensor_reduce(lg[:, b, half * HALF:(half + 1) * HALF], wide(half),
                                             mask0[:, half * HALF:(half + 1) * HALF], 1.0,
                                             FAR if half == 0 else m0[:, u - 1:u], ALU.add, ALU.min, m0[:, u:u + 1])\
                       .then_inc(s["s0_masked"], 1)
                    dve.wait_ge(s["s0_masked"], u + 1)
                m, f, o = m0[:, u:u + 1], flag[:, b:b + 1], slice(b, b + 1)
                link(dve.tensor_tensor(m0c[:, o], m, rowc[:, o], ALU.add))
                link(dve.tensor_scalar(f, m, 0.5 * MASKED, None, ALU.is_lt))
                link(dve.tensor_scalar(nflag[:, o], f, -1.0, None, ALU.mult))
                link(dve.tensor_tensor(m0c[:, o], m0c[:, o], rowc[:, o], ALU.subtract))
                dve.tensor_tensor(bias0[:, o], m0c[:, o], f, ALU.mult).then_inc(s["s0_args"], 1)
            dve.wait_ge(s["decay_log"], 1)
            dve.tensor_scalar(lgam, lgam, -1.0, None, ALU.mult).then_inc(s["decay_one"], 1)
            for b in range(B):
                for q in range(4):
                    t = 4 * b + q
                    dve.wait_ge(s["pt0_psum"], t + 1)
                    dve.tensor_copy(pg[:, b, q * 512:(q + 1) * 512], ps[:, 4 + t % 2, :]).then_inc(s["pt0_ready"], 1)
                link(dve.reciprocal(rinv0[:, b:b + 1], den0[:, b:b + 1]))
                dve.wait_ge(s["o0_psum"], b + 1)
                dve.tensor_copy(t1[:, b * N:(b + 1) * N], ps[:, 6, b * N:(b + 1) * N]).then_inc(s["o0_ready"], 1)
                dve.wait_ge(s["y0_psum"], b + 1)
                link(dve.scalar_tensor_tensor(out=x[1][:, b, :], in0=ps[:, 7, b * N:(b + 1) * N],
                                              scalar=rinv0[:, b:b + 1], in1=xb[:, b, :], op0=ALU.mult, op1=ALU.add))

            normalise(x[1], xn, 1)
            keep_transpose(1)
            dve.wait_ge(s["decay_log"], 2)
            link(dve.tensor_tensor(w["steps"], w["steps"], w["causal"], ALU.mult))

            def keep_values(vb):
                b, half = vb // 2, vb % 2
                dve.wait_ge(s["vp_psum"], vb + 1)
                dve.tensor_tensor(v[:, b, half * 8:half * 8 + 8, :], wide(vb % 2).rearrange("p (c d) -> p c d", c=8),
                                  w["wv1_b_rows"].unsqueeze(1).to_broadcast([128, 8, D]), ALU.add)\
                   .then_inc(s["v_ready"], 1)

            dve.wait_ge(s["v0_psum"], 1)
            dve.tensor_copy(t0[:, :], ps[:, 7, 0:256]).then_inc(s["v0_ready"], 1)
            dve.wait_ge(s["st_psum"], 1)
            dve.tensor_tensor(t1[:, :].rearrange("p (b n) -> p b n", b=B), ps[:, 4, 0:256].rearrange("p (b n) -> p b n", b=B),
                              w["steps"].unsqueeze(1).to_broadcast([128, B, N]), ALU.mult).then_inc(s["sm_ready"], 1)
            keep_values(0)
            dve.wait_ge(s["rd_psum"], 1)
            dve.tensor_copy(t2[:, :], ps[:, 5, 0:256]).then_inc(s["rd_ready"], 1)
            keep_values(1)
            dve.wait_ge(s["ro_psum"], 1)
            link(dve.scalar_tensor_tensor(out=xb[:, :, :].rearrange("p b d -> p (b d)"), in0=ps[:, 6, 0:256], scalar=alpha,
                                          in1=xn[:, :, :].rearrange("p b d -> p (b d)"), op0=ALU.mult, op1=ALU.add))
            link(dve.tensor_tensor(x[2][:, :, :], x[1][:, :, :], xb[:, :, :], ALU.add))

            dve.wait_ge(s["slots_in"], 16)
            dve.wait_ge(s["third_in"], 16)
            normalise(se, se, 2, 8)
            link(dve.tensor_tensor(sg, w["slot_g"], w["scale"], ALU.mult))
            link(dve.tensor_tensor(sbias, w["slot_b"], w["scale"], ALU.mult))

            normalise(x[2], xn, 3)
            keep_transpose(2)
            keep_values(2)
            l, shifted, ex, rank, wts, gates = (router[:, i, :] for i in (0, 1, 2, 3, 4, 5))
            pair, top = router[:, 6, 0:B], router[:, 7, 0:B]

            def by_batch(t):
                return t.rearrange("p (b e) -> p b e", b=B)

            def over_rest(t):
                return t.unsqueeze(2).to_broadcast([128, B, E0])

            dve.wait_ge(s["rl_psum"], 1)
            link(dve.tensor_copy(l, ps[:, 7, 0:16]))
            link(dve.tensor_reduce(top, by_batch(l), AX_X, ALU.max))
            dve.tensor_tensor(by_batch(shifted), by_batch(l), over_rest(top), ALU.subtract).then_inc(s["logits_max"], 1)
            me = by_batch(l).unsqueeze(3).to_broadcast([128, B, E0, E0])
            cube = [versus[:, i, :].rearrange("p (b e j) -> p b e j", b=B, e=E0) for i in range(3)]
            for b in range(B):
                other = by_batch(l)[:, b, :].unsqueeze(1).to_broadcast([128, E0, E0])
                link(dve.tensor_tensor(cube[0][:, b], other, me[:, b], ALU.is_gt))
                link(dve.tensor_tensor(cube[1][:, b], other, me[:, b], ALU.is_equal))
                link(dve.tensor_tensor(cube[1][:, b], cube[1][:, b], w["lower"].rearrange("p (e j) -> p e j", e=E0), ALU.mult))
            link(dve.tensor_tensor(versus[:, 2, :], versus[:, 0, :], versus[:, 1, :], ALU.add))
            link(dve.tensor_reduce(rank, versus[:, 2, :].rearrange("p (e j) -> p e j", j=E0), AX_X, ALU.add))
            dve.wait_ge(s["router_exp"], 1)
            link(dve.scalar_tensor_tensor(out=wts, in0=rank, scalar=1.5, in1=ex, op0=ALU.is_lt, op1=ALU.mult))
            link(dve.tensor_reduce(pair, by_batch(wts), AX_X, ALU.add))
            link(dve.reciprocal(pair, pair))
            link(dve.tensor_tensor(by_batch(gates), by_batch(wts), over_rest(pair), ALU.mult))
            dve.wait_ge(s["gelu0_ready"], 1)
            dve.tensor_tensor(hid.rearrange("p (g i) -> p g i", i=I0), hid.rearrange("p (g i) -> p g i", i=I0),
                              gates.unsqueeze(2).to_broadcast([128, B * E0, I0]), ALU.mult).then_inc(s["hw_ready"], 1)
            keep_values(3)
            for b in range(B):
                dve.wait_ge(s["ht_psum"], b + 1)
                dve.tensor_copy(lg[:, 1, b * 512:(b + 1) * 512], ps[:, 6 + b, :]).then_inc(s["ht_ready"], 1)
            dve.wait_ge(s["f0_psum"], 1)
            link(dve.tensor_tensor(x[3][:, :, :].rearrange("p b d -> p (b d)"), ps[:, 4, 0:256],
                                   x[2][:, :, :].rearrange("p b d -> p (b d)"), ALU.add))

            normalise(x[3], xn, 4)
            keep_transpose(3)
            link(dve.tensor_tensor(xb[:, :, :], x[3][:, :, :], w["wo1_b_rows"].unsqueeze(1).to_broadcast([128, B, D]), ALU.add))
            dve.wait_ge(s["q1_psum"], 1)
            link(dve.tensor_scalar(t0[:, :], ps[:, 5, 0:256], w["wq1_b"], -S1_SCALE, ALU.add, ALU.mult))
            link(dve.tensor_copy(q_split[:, 0, :], t0[:, :]))
            link(dve.tensor_tensor(t0[:, :], t0[:, :], q_split[:, 0, :], ALU.subtract))
            link(dve.tensor_copy(q_split[:, 1, :], t0[:, :]))
            dve.tensor_tensor(q_split[:, 2, :], t0[:, :], q_split[:, 1, :], ALU.subtract).then_inc(s["q_parts"], 1)
            for n in range(2):
                dve.wait_ge(s["se_psum"], n + 1)
                dve.tensor_scalar(se_t[:, n * 512:(n + 1) * 512], ps[:, 6 + n, :], sg, sbias, ALU.mult, ALU.add)\
                   .then_inc(s["set_ready"], 1)
            dve.wait_ge(s["mask1_ready"], 1)
            dve.wait_ge(s["g_in"], 16)

            def mask_scores(i, half):
                b, slot = i // HEADS, 2 * (i % 2) + half
                dve.wait_ge(s["scores_psum"], 2 * i + half + 1)
                if half == 0 and i >= 2:
                    dve.wait_ge(s["pt_psum"], 4 * (i - 1))
                if half:
                    dve.wait_ge(s["scores_masked"], 2 * i + 1)
                dve.tensor_tensor_reduce(lg[:, i % 2, half * HALF:(half + 1) * HALF], wide(half),
                                         mask1[:, b, half * HALF:(half + 1) * HALF], 1.0,
                                         mn[:, slot - 1:slot] if half else FAR, ALU.add, ALU.min, mn[:, slot:slot + 1])\
                   .then_inc(s["scores_masked"], 1)

            def by_group(i, n):
                q = 2 * n
                dve.wait_ge(s["pt_psum"], 4 * i + q + 1)
                if n == 0 and i >= 2:
                    dve.wait_ge(s["pv_psum"], i - 1)
                g = g_t[:, i // HEADS].rearrange("p c n -> p (c n)")[:, q * 512:(q + 1) * 512]
                dve.tensor_tensor(pg[:, i % 2, q * 512:(q + 1) * 512], ps[:, 4, :], g, ALU.mult)\
                   .then_inc(s["pg_dve"], 1)

            mask_scores(0, 0)
            mask_scores(0, 1)
            for i in range(ITEMS):
                for n in range(2):
                    if i + 1 < ITEMS:
                        mask_scores(i + 1, n)
                    by_group(i, n)
            dve.wait_ge(s["exp_ready"], ITEMS)
            link(dve.reciprocal(rinv1[:, :], den1[:, :]))
            dve.wait_ge(s["heads_psum"], ITEMS // 4)
            dve.tensor_tensor(t0[:, :].rearrange("p (i d) -> p i d", d=DH), ps[:, 7, 0:256].rearrange("p (i d) -> p i d", d=DH),
                              rinv1[:, :].unsqueeze(2).to_broadcast([128, ITEMS, DH]), ALU.mult).then_inc(s["at_ready"], 1)
            dve.wait_ge(s["att_psum"], 1)
            dve.tensor_copy(t1[:, :], ps[:, 4, 0:256]).then_inc(s["att_ready"], 1)
            dve.wait_ge(s["wo_psum"], 1)
            link(dve.tensor_tensor(x[4][:, :, :].rearrange("p b d -> p (b d)"), ps[:, 5, 0:256],
                                   xb[:, :, :].rearrange("p b d -> p (b d)"), ALU.add))

            normalise(x[4], xn, 5)
            keep_transpose(4)
            dve.wait_ge(s["q2_psum"], 1)
            dve.tensor_scalar(t0[:, :], ps[:, 7, 0:256], w["bq_self"], -S0_SCALE, ALU.add, ALU.mult).then_inc(s["q2_ready"], 1)
            dve.wait_ge(s["v2_psum"], 1)
            dve.tensor_tensor(t2[:, :].rearrange("p (b n) -> p b n", b=B), ps[:, 3, 0:256].rearrange("p (b n) -> p b n", b=B),
                              w["bv_rows"].unsqueeze(1).to_broadcast([128, B, D]), ALU.add).then_inc(s["v2_ready"], 1)
            dve.wait_ge(s["cs_psum"], 1)
            for b in range(B):
                dve.tensor_tensor_reduce(lg[:, 0, b * N:(b + 1) * N], ps[:, 4, b * N:(b + 1) * N], w["future"], 1.0, FAR,
                                         ALU.add, ALU.min, m2[:, b:b + 1]).then_inc(s["cs_masked"], 1)
            dve.wait_ge(s["pst_psum"], 1)
            dve.tensor_copy(t1[:, :], ps[:, 5, 0:256]).then_inc(s["pst_ready"], 1)
            link(dve.reciprocal(rinv2, den2))
            dve.wait_ge(s["ys_psum"], 1)
            for b in range(B):
                link(dve.scalar_tensor_tensor(out=x[5][:, b, :], in0=ps[:, 6, b * N:(b + 1) * N], scalar=rinv2[:, b:b + 1],
                                              in1=x[4][:, b, :], op0=ALU.mult, op1=ALU.add))

            normalise(x[5], xn, 6)
            dve.wait_ge(s["xnt_psum"], 6)
            dve.tensor_scalar(t0[:, :], ps[:, 6, 0:256], w["norm_g"], w["norm_b"], ALU.mult, ALU.add).then_inc(s["xft_ready"], 1)
            link(dve.tensor_tensor(xb[:, :, :], xn[:, :, :], w["norm_g_rows"].unsqueeze(1).to_broadcast([128, B, D]), ALU.mult))
            dve.tensor_tensor(xb[:, :, :], xb[:, :, :], w["norm_b_rows"].unsqueeze(1).to_broadcast([128, B, D]), ALU.add)\
               .then_inc(s["xf_ready"], 1)
            dve.wait_ge(s["ls_psum"], 1)
            lsp = ps[:, 4:8, :].rearrange("p a (k n) -> p (a k) n", n=N)
            link(dve.tensor_reduce(d_max, lsp, AX_X, ALU.max))
            dve.tensor_tensor(dispatch_t, lsp, d_max.unsqueeze(2).to_broadcast([128, 16, N]), ALU.subtract)\
               .then_inc(s["ls_shift"], 1)
            for b in range(B):
                dve.wait_ge(s["ln_psum"], b + 1)
                dve.tensor_reduce(m_c[:, b:b + 1], wide(b), AX_X, ALU.max, negate=True).then_inc(s["ln_max"], 1)
            dve.wait_ge(s["dispatch_exp"], 1)
            link(dve.tensor_reduce(d_sum, dispatch_t, AX_X, ALU.add))
            link(dve.reciprocal(d_sum, d_sum))
            dve.tensor_tensor(dispatch_t, dispatch_t, d_sum.unsqueeze(2).to_broadcast([128, 16, N]), ALU.mult)\
               .then_inc(s["dispatch_ready"], 1)
            dve.wait_ge(s["ct_psum"], 1)
            dve.tensor_copy(lg[:, 1, 0:1024], wide(2)).then_inc(s["ct_dve"], 1)
            dve.wait_ge(s["dt_psum"], 1)
            dve.tensor_copy(dispatch[:, 0, :], wide(0)).then_inc(s["dt_dve"], 1)
            link(dve.reciprocal(rinv_c, den_c))
            dve.wait_ge(s["sl_psum"], 1)
            dve.tensor_copy(slots_t[:, :, 0, :], wide(0).rearrange("p (e n) -> p e n", e=E1)).then_inc(s["sl_dve"], 1)

            def add_down_bias(e):
                dve.wait_ge(s["eo_psum"], e + 1)
                if e >= 2:
                    dve.wait_ge(s["y_psum"], e - 1)
                dve.tensor_tensor(eo[:, e % 2, :], ps[:, 2 + e % 2, 0:128], bd[:, e, :], ALU.add).then_inc(s["eo_ready"], 1)

            dve.wait_ge(s["bd_in"], 16)
            for e in range(E1):
                dve.wait_ge(s["u_psum"], e + 1)
                if e >= 2:
                    dve.wait_ge(s["eo_psum"], e - 1)
                for k in range(2):
                    dve.wait_ge(s["gate_ready"], 2 * e + k + 1)
                    dve.scalar_tensor_tensor(out=hmid[:, e % 2, k, :], in0=ps[:, 6 + e % 2, k * 128:(k + 1) * 128],
                                             scalar=w["bu"][:, 2 * e + k:2 * e + k + 1], in1=gate_h[:, e % 2, k, :],
                                             op0=ALU.add, op1=ALU.mult).then_inc(s["hmid_ready"], 1)
                if e >= 1:
                    add_down_bias(e - 1)
            add_down_bias(E1 - 1)
            dve.wait_ge(s["y_psum"], E1)
            for b in range(B):
                dve.scalar_tensor_tensor(out=x[4][:, b, :], in0=ps[:, b, 0:128], scalar=rinv_c[:, b:b + 1],
                                         in1=x[5][:, b, :], op0=ALU.mult, op1=ALU.add).then_inc(s["out_ready"], 1)

        @block.tensor
        def _(pe):
            mm, tp = pe.matmul, pe.transpose

            def transpose_rows(k, ready, src=xn):
                for b in range(B):
                    pe.wait_ge(s["xn_ready"], ready + b + 1)
                    ins = tp(ps[:, 6, b * N:(b + 1) * N], src[:, b, :], ident)
                ins.then_inc(s["xnt_psum"], 1)

            pe.wait_ge(s["first_in"], 16)
            pe.wait_ge(s["ones_set"], 1)
            mm(ps[:, 7, 0:128], w["wq_t"], w["wk_t"], start=True, stop=True)
            mm(ps[:, 7, 128:256], w["wv_t"], w["wo"], start=True, stop=True)
            mm(ps[:, 7, 384:385], w["wk_t"], w["bq"], start=True, stop=True)
            mm(ps[:, 7, 385:386], w["wq_t"], w["bk"], start=True, stop=True)
            pe.wait_ge(s["fold_src"], 2)
            mm(ps[:, 7, 256:384], ones[:, :], wob[:, :], start=True, stop=True)
            mm(ps[:, 7, 386:387], ones[:, :], t2[:, 0:1], start=True, stop=True).then_inc(s["fold_psum"], 1)
            transpose_rows(0, 0)
            pe.wait_ge(s["fold_ready"], 1)
            pe.wait_ge(s["xnt_ready"], 1)
            mm(ps[:, 4, 0:256], folds[:, 0:128], xt2, start=True, stop=True).then_inc(s["qp_psum"], 1)
            for b in range(B):
                ins = mm(ps[:, 5, b:b + 1], xt(b), folds[:, 385:386], start=True, stop=True)
            ins.then_inc(s["row_psum"], 1)
            pe.wait_ge(s["qp_ready"], 1)
            for b in range(B):
                pe.wait_ge(s[f"ctxt_in{b}"], 16)
                for half in range(2):
                    if b:
                        pe.wait_ge(s["s0_masked"], half + 1)
                    for n in range(2):
                        ins = mm(ps[:, 2 * half + n, :], t0[:, b * N:(b + 1) * N],
                                 ctx_t[:, b, half * HALF + n * 512:half * HALF + (n + 1) * 512], start=True, stop=True)
                    ins.then_inc(s["s0_psum"], 1)

            def project_keys(kb):
                b, half = kb // 2, kb % 2
                if kb < 2:
                    pe.wait_ge(s["s0_masked"], 3 + kb)
                else:
                    pe.wait_ge(s["kp_copied"], kb - 1)
                for n in range(2):
                    ins = mm(ps[:, 2 * half + n, :], w["wk1"],
                             ctx_t[:, b, half * HALF + n * 512:half * HALF + (n + 1) * 512], start=True, stop=True)
                ins.then_inc(s["kp_psum"], 1)

            def project_values(vb):
                b, half = vb // 2, vb % 2
                if vb < 2:
                    pe.wait_ge(s["kp_copied"], 3 + vb)
                else:
                    pe.wait_ge(s["v_ready"], vb - 1)
                for c in range(8):
                    t = (half * 8 + c) * 128
                    ins = mm(ps[:, 2 * half + c // 4, (c % 4) * 128:(c % 4 + 1) * 128], ctx_t[:, b, t:t + 128], w["wv1"],
                             start=True, stop=True)
                ins.then_inc(s["vp_psum"], 1)

            pe.wait_ge(s["second_in"], 16)
            project_keys(0)
            project_keys(1)
            pe.wait_ge(s["ctxr_in"], 16)
            for b in range(B):
                pe.wait_ge(s["s0_exp"], b + 1)
                for q in range(4):
                    t = 4 * b + q
                    if t >= 2:
                        pe.wait_ge(s["pt0_ready"], t - 1)
                    for n in range(4):
                        c = 4 * q + n
                        ins = tp(ps[:, 4 + t % 2, n * 128:(n + 1) * 128], lg[:, b, c * 128:(c + 1) * 128], ident)
                    ins.then_inc(s["pt0_psum"], 1)
                if b == 0:
                    project_keys(2)
                for c in range(C):
                    if c % 4 == 0:
                        pe.wait_ge(s["pt0_ready"], 4 * b + c // 4 + 1)
                    ins = mm(ps[:, 6, b * N:(b + 1) * N], ctx_r[:, b, c, :], pg[:, b, c * 128:(c + 1) * 128],
                             start=(c == 0), stop=(c == C - 1))
                ins.then_inc(s["o0_psum"], 1)
                pe.wait_ge(s["o0_ready"], b + 1)
                mm(ps[:, 7, b * N:(b + 1) * N], t1[:, b * N:(b + 1) * N], folds[:, 128:256], start=True, stop=True)\
                    .then_inc(s["y0_psum"], 1)
            project_keys(3)
            transpose_rows(1, 2)
            pe.wait_ge(s["xnt_ready"], 2)
            for b in range(B):
                ins = mm(ps[:, 7, b * N:(b + 1) * N], xt(b), w["ww_t"], start=True, stop=True)
            ins.then_inc(s["v0_psum"], 1)
            for b in range(B):
                ins = mm(ps[:, 4, b * N:(b + 1) * N], xnt[:, b, 0:N], xt(b), start=True, stop=True)
            ins.then_inc(s["st_psum"], 1)
            project_values(0)
            pe.wait_ge(s["v0_ready"], 1)
            pe.wait_ge(s["sm_ready"], 1)
            for b in range(B):
                ins = mm(ps[:, 5, b * N:(b + 1) * N], t0[:, b * N:(b + 1) * N], t1[:, b * N:(b + 1) * N], start=True, stop=True)
            ins.then_inc(s["rd_psum"], 1)
            project_values(1)
            pe.wait_ge(s["rd_ready"], 1)
            for b in range(B):
                ins = mm(ps[:, 6, b * N:(b + 1) * N], t2[:, b * N:(b + 1) * N], w["wr_t"], start=True, stop=True)
            ins.then_inc(s["ro_psum"], 1)
            project_values(2)
            transpose_rows(2, 4)
            pe.wait_ge(s["xnt_ready"], 3)
            for b in range(B):
                ins = mm(ps[:, 7, b * E0:(b + 1) * E0], xt(b), w["wgate_t"], start=True, stop=True)
            ins.then_inc(s["rl_psum"], 1)
            for b in range(B):
                ins = mm(ps[:, 4 + b, :], xt(b), w["wfc_t"], start=True, stop=True)
            ins.then_inc(s["h0_psum"], 1)
            project_values(3)
            pe.wait_ge(s["hw_ready"], 1)
            for b in range(B):
                for k in range(4):
                    at = b * 512 + k * 128
                    ins = tp(ps[:, 6 + b, k * 128:(k + 1) * 128], lg[:, 0, at:at + 128], ident)
                ins.then_inc(s["ht_psum"], 1)
            for b in range(B):
                pe.wait_ge(s["ht_ready"], b + 1)
                for k in range(4):
                    ins = mm(ps[:, 4, b * N:(b + 1) * N], hid_t[:, b, k, :], w["wproj_t"][:, k * 128:(k + 1) * 128],
                             start=(k == 0), stop=(k == 3))
            ins.then_inc(s["f0_psum"], 1)
            transpose_rows(3, 6)
            pe.wait_ge(s["xnt_ready"], 4)
            pe.wait_ge(s["third_in"], 16)
            mm(ps[:, 5, 0:256], w["wq1"], xt2, start=True, stop=True).then_inc(s["q1_psum"], 1)
            pe.wait_ge(s["se_ready"], 8)
            for n in range(2):
                for k in range(4):
                    ins = tp(ps[:, 6 + n, k * 128:(k + 1) * 128], se[:, 4 * n + k, :], ident)
                ins.then_inc(s["se_psum"], 1)

            def scores(i, half):
                b, h = i // HEADS, i % HEADS
                if half == 0:
                    pe.wait_ge(keys_in[i % RING], 48 * (i // RING + 1))
                if i >= 1:
                    pe.wait_ge(s["scores_masked"], 2 * i + half - 1)
                for n in range(2):
                    at = half * HALF + n * 512
                    ins = mm(ps[:, 2 * half + n, :], queries[:, h, b * N:(b + 1) * N], keys[:, i % RING, at:at + 512],
                             start=True, stop=True)
                ins.then_inc(s["scores_psum"], 1)

            def transpose_quarter(i, q):
                if q == 0:
                    pe.wait_ge(s["exp_ready"], i + 1)
                t = 2 * i + q // 2
                if t >= 1:
                    pe.wait_ge(s["pt_copied" if q % 2 else "pg_dve"], t)
                for n in range(4):
                    c = 4 * q + n
                    ins = tp(ps[:, 4 + q % 2, n * 128:(n + 1) * 128], lg[:, i % 2, c * 128:(c + 1) * 128], ident)
                ins.then_inc(s["pt_psum"], 1)

            def weigh_values(i):
                b, h = i // HEADS, i % HEADS
                if i % 4 == 0 and i:
                    pe.wait_ge(s["heads_copied"], i // 4)
                for q in range(4):
                    pe.wait_ge(s["pg_pool" if q % 2 else "pg_dve"], 2 * i + q // 2 + 1)
                    for j in range(4):
                        c = 4 * q + j
                        ins = mm(ps[32 * j:32 * j + 32, 6, (h % 4) * 128:(h % 4 + 1) * 128],
                                 v[:, b, c, 32 * (h // 4):32 * (h // 4) + 32], pg[:, i % 2, c * 128:(c + 1) * 128],
                                 start=(q == 0), stop=(q == 3))
                ins.then_inc(s["pv_psum"], 1)

            def gather_heads(g):
                pe.wait_ge(s["heads_copied"], g + 1)
                for n in range(4):
                    i = 4 * g + n
                    ins = mm(ps[:, 7, i * DH:(i + 1) * DH], heads_sb[:, n * 128:(n + 1) * 128],
                             w["select"][:, n * DH:(n + 1) * DH], start=True, stop=True)
                ins.then_inc(s["heads_psum"], 1)

            pe.wait_ge(s["queries_in"], 16 * 9)
            pe.wait_ge(s["v_ready"], 4)
            pe.wait_ge(s["set_ready"], 2)
            scores(0, 0)
            scores(0, 1)
            scores(1, 0)
            scores(1, 1)
            for i in range(ITEMS):
                transpose_quarter(i, 0)
                transpose_quarter(i, 1)
                if i + 2 < ITEMS:
                    scores(i + 2, 0)
                transpose_quarter(i, 2)
                transpose_quarter(i, 3)
                if i + 2 < ITEMS:
                    scores(i + 2, 1)
                if i >= 1:
                    weigh_values(i - 1)
                if i % 4 == 1 and i > 4:
                    gather_heads(i // 4 - 1)
            weigh_values(ITEMS - 1)
            gather_heads(ITEMS // 4 - 1)
            pe.wait_ge(s["at_ready"], 1)
            for b in range(B):
                ins = tp(ps[:, 4, b * N:(b + 1) * N], t0[:, b * N:(b + 1) * N], ident)
            ins.then_inc(s["att_psum"], 1)
            pe.wait_ge(s["att_ready"], 1)
            for b in range(B):
                ins = mm(ps[:, 5, b * N:(b + 1) * N], t1[:, b * N:(b + 1) * N], w["wo1"], start=True, stop=True)
            ins.then_inc(s["wo_psum"], 1)
            transpose_rows(4, 8)
            pe.wait_ge(s["xnt_ready"], 5)
            mm(ps[:, 7, 0:256], w["wqkv_t"][:, 0:128], xt2, start=True, stop=True).then_inc(s["q2_psum"], 1)
            mm(ps[:, 5, 0:256], w["wqkv_t"][:, 128:256], xt2, start=True, stop=True).then_inc(s["k2_psum"], 1)
            for b in range(B):
                ins = mm(ps[:, 3, b * N:(b + 1) * N], xt(b), w["wqkv_t"][:, 256:384], start=True, stop=True)
            ins.then_inc(s["v2_psum"], 1)
            pe.wait_ge(s["q2_ready"], 1)
            pe.wait_ge(s["k2_ready"], 1)
            for b in range(B):
                ins = mm(ps[:, 4, b * N:(b + 1) * N], t0[:, b * N:(b + 1) * N], t1[:, b * N:(b + 1) * N], start=True, stop=True)
            ins.then_inc(s["cs_psum"], 1)
            for b in range(B):
                pe.wait_ge(s["cs_exp"], b + 1)
                ins = tp(ps[:, 5, b * N:(b + 1) * N], lg[:, 0, b * N:(b + 1) * N], ident)
            ins.then_inc(s["pst_psum"], 1)
            pe.wait_ge(s["pst_ready"], 1)
            pe.wait_ge(s["v2_ready"], 1)
            for b in range(B):
                ins = mm(ps[:, 6, b * N:(b + 1) * N], t1[:, b * N:(b + 1) * N], t2[:, b * N:(b + 1) * N], start=True, stop=True)
            ins.then_inc(s["ys_psum"], 1)
            transpose_rows(5, 10)
            pe.wait_ge(s["xft_ready"], 1)
            for k in range(8):
                ins = mm(ps[:, 4 + k // 2, (k % 2) * 256:(k % 2 + 1) * 256], se_t[:, k * 128:(k + 1) * 128], t0[:, :],
                         start=True, stop=True)
            ins.then_inc(s["ls_psum"], 1)
            for b in range(B):
                for n in range(2):
                    ins = mm(ps[:, 2 * b + n, :], t0[:, b * N:(b + 1) * N], se_t[:, n * 512:(n + 1) * 512], start=True, stop=True)
                ins.then_inc(s["ln_psum"], 1)
            pe.wait_ge(s["combine_exp"], 2)
            pe.wait_ge(s["ls_shift"], 1)
            for e in range(E1):
                ins = tp(ps[:, 4 + e // 4, (e % 4) * 128:(e % 4 + 1) * 128], combine[:, e, :, :].rearrange("p b n -> p (b n)"), ident)
            ins.then_inc(s["ct_psum"], 1)
            pe.wait_ge(s["dispatch_ready"], 1)
            for k in range(8):
                for b in range(B):
                    ins = tp(ps[:, 2 * b + k // 4, (k % 4) * 128:(k % 4 + 1) * 128], dispatch_t[:, 2 * k + b, :], ident)
            ins.then_inc(s["dt_psum"], 1)
            pe.wait_ge(s["xf_ready"], 1)
            for b in range(B):
                pe.wait_ge(s["dt_act" if b else "dt_dve"], 1)
                for n in range(2):
                    ins = mm(ps[:, 2 * b + n, :], xb[:, b, :], dispatch[:, b, n * 512:(n + 1) * 512], start=True, stop=True)
                ins.then_inc(s["sl_psum"], 1)

            def up(e):
                rhs = slots_t[:, e, :, :]
                if e >= 2:
                    pe.wait_ge(s["gate_ready"], 2 * (e - 1))
                for k in range(2):
                    ins = mm(ps[:, 4 + e % 2, k * 128:(k + 1) * 128], wg[:, e, k * 128:(k + 1) * 128], rhs, start=True, stop=True)
                ins.then_inc(s["g_psum"], 1)
                if e >= 2:
                    pe.wait_ge(s["hmid_ready"], 2 * (e - 1))
                for k in range(2):
                    ins = mm(ps[:, 6 + e % 2, k * 128:(k + 1) * 128], wu[:, e, k * 128:(k + 1) * 128], rhs, start=True, stop=True)
                ins.then_inc(s["u_psum"], 1)

            def down(e):
                if e >= 2:
                    pe.wait_ge(s["eo_ready"], e - 1)
                for k in range(2):
                    pe.wait_ge(s["hmid_ready"], 2 * e + k + 1)
                    ins = mm(ps[:, 2 + e % 2, 0:128], hmid[:, e % 2, k, :], wd[:, e, k, :], start=(k == 0), stop=(k == 1))
                ins.then_inc(s["eo_psum"], 1)

            def back(e):
                pe.wait_ge(s["eo_ready"], e + 1)
                for b in range(B):
                    r = slice(64 * b, 64 * b + 64)
                    ins = mm(ps[:, b, 0:128], combine_t[r, e, :], eo[r, e % 2, :], start=(e == 0), stop=(e == E1 - 1))
                ins.then_inc(s["y_psum"], 1)

            pe.wait_ge(s["sl_dve"], 1)
            pe.wait_ge(s["sl_act"], 1)
            pe.wait_ge(s["ct_dve"], 1)
            pe.wait_ge(s["ct_act"], 1)
            for name in ("wg_in", "wu_in", "wd_in"):
                pe.wait_ge(s[name], 16)
            up(0)
            for e in range(E1):
                if e + 1 < E1:
                    up(e + 1)
                down(e)
                if e >= 1:
                    back(e - 1)
            back(E1 - 1)


def kernel(**inputs):
    import numpy as np
    import concourse.bacc as bacc
    from concourse.bass_utils import run_bass_kernel_spmd as run

    i = {name: np.asarray(value) for name, value in inputs.items()}

    def rows(vector):
        return np.broadcast_to(vector.reshape(1, -1), (128, vector.size))

    def col(vector):
        return vector.reshape(128, 1)

    f = np.float32
    j, p = np.arange(N)[:, None], np.arange(N)[None, :]
    e, o = np.arange(E0)[:, None], np.arange(E0)[None, :]
    select = np.zeros((128, 4, DH), f)
    for n in range(4):
        for g in range(4):
            for d in range(DH):
                select[32 * g + DH * n + d, n, d] = 1
    qkv_b = i["L1_attn_b_qkv"]
    parts = {
        "ident": np.eye(128, dtype=f), "x": i["x"].transpose(1, 0, 2).reshape(N, B * D),
        "wq_t": i["L0_xattn_Wq"].T, "wk_t": i["L0_xattn_Wk"].T, "wv_t": i["L0_xattn_Wv"].T, "wo": i["L0_xattn_Wo"],
        "bo_rows": rows(i["L0_xattn_bo"]), "bq": col(i["L0_xattn_bq"]), "bk": col(i["L0_xattn_bk"]),
        "bv": col(i["L0_xattn_bv"]), "decay": rows(i["L0_attn_decay"]), "log_alpha": rows(i["L0_attn_log_alpha"]),
        "wk1": i["L1_xattn_wk_k"], "wk1_b": col(i["L1_xattn_wk_b"]), "wv1": i["L1_xattn_wv_k"],
        "wv1_b_rows": rows(i["L1_xattn_wv_b"]),
        "steps": np.maximum(p - 1 - j, 0).astype(f), "causal": (p > j).astype(f),
        "ww_t": i["L0_attn_W_write"].T, "wr_t": i["L0_attn_W_read"].T,
        "wgate_t": i["L0_ffn_w_gate"].T, "lower": rows((o < e).astype(f).reshape(-1)),
        "wfc_t": i["L0_ffn_w_fc"].reshape(E0 * I0, D).T,
        "wproj_t": i["L0_ffn_w_proj"].transpose(0, 2, 1).reshape(4, 128, D).transpose(1, 0, 2).reshape(128, 4 * D),
        "wq1": i["L1_xattn_wq_k"], "wo1": i["L1_xattn_wo_k"], "wo1_b_rows": rows(i["L1_xattn_wo_b"]),
        "wqkv_t": i["L1_attn_W_qkv"].T, "bv_rows": rows(qkv_b[256:384]),
        "future": np.where(p > j, f(CAUSAL), f(0)).astype(f), "select": select.reshape(128, 4 * DH),
        "norm_g_rows": rows(i["L1_ffn_norm_g"]), "norm_b_rows": rows(i["L1_ffn_norm_b"]),
        "bg": i["L1_ffn_bg"].reshape(2 * E1, 128).T, "bu": i["L1_ffn_bu"].reshape(2 * E1, 128).T,
        "wq1_b": col(i["L1_xattn_wq_b"]), "bq_self": col(qkv_b[0:128]), "bk_self": col(qkv_b[128:256]),
        "norm_g": col(i["L1_ffn_norm_g"]), "norm_b": col(i["L1_ffn_norm_b"]), "slot_g": col(i["L1_ffn_slot_g"]),
        "slot_b": col(i["L1_ffn_slot_b"]), "scale": rows(i["L1_ffn_scale"]),
    }
    c = i["ctx_1024"]
    arrays = {
        "first": np.concatenate([parts[n] for n, _ in FIRST], axis=1),
        "second": np.concatenate([parts[n] for n, _ in SECOND], axis=1),
        "third": np.concatenate([parts[n] for n, _ in THIRD], axis=1),
        "ctx_t": c.transpose(2, 0, 1), "ctx_r": c.reshape(B, C, 128, D).transpose(2, 0, 1, 3),
        "g_t": i["fside_BxSxS2_0"].reshape(B, N, C, 128).transpose(3, 0, 2, 1),
        "mask0": i["mask_1xSxS2_if1"][0], "mask1": i["mask_BxSxS2_ik1"].transpose(1, 0, 2),
        "slots": i["L1_ffn_slot_embeds"].reshape(8, 128, D).transpose(1, 0, 2),
        "wg": i["L1_ffn_Wg"].transpose(1, 0, 2), "wu": i["L1_ffn_Wu"].transpose(1, 0, 2),
        "wd": i["L1_ffn_Wd"].reshape(E1, 2, 128, D).transpose(2, 0, 1, 3),
        "bd": np.broadcast_to(i["L1_ffn_bd"][None], (128, E1, D)),
    }
    nc = bacc.Bacc("TRN2", target_bir_lowering=False, num_devices=1)
    feeds, aps = {}, {}
    for name, array in arrays.items():
        feeds[f"in_{name}"] = array = np.ascontiguousarray(array)
        aps[name] = nc.dram_tensor(f"in_{name}", array.shape, mybir.dt.from_np(array.dtype), kind="ExternalInput").ap()
    out = nc.dram_tensor("out_0", (B, N, D), F32, kind="ExternalOutput").ap()
    k_dram = nc.dram_tensor("k_dram", (B, PARTS, 128, T), BF16, kind="Internal").ap()
    q_dram = nc.dram_tensor("q_dram", (PARTS, 128, B * N), BF16, kind="Internal").ap()
    build(nc, aps, out, k_dram, q_dram)
    r = run(nc, [feeds], core_ids=[0])
    return r.results[0]["out_0"]
```

```python
from contextlib import ExitStack

import concourse.bass as bass
from concourse import mybir

ALU = mybir.AluOpType
ACT = mybir.ActivationFunctionType
AX_X = mybir.AxisListType.X
F32 = mybir.dt.float32
BF16 = mybir.dt.bfloat16
I32 = mybir.dt.int32

B, N, D, T = 2, 128, 128, 2048
C = T // 128
HALF = T // 2
HEADS, DH = 16, 8
PARTS = 3
ROWS = PARTS * PARTS * DH
E0, I0 = 8, 64
E1, SLOTS, F1 = 16, 64, 256
NS = E1 * SLOTS
PAIRS = E1 // 2
EPS = 1e-5
MASKED = 1e9
CAUSAL = 1e30
FAR = 3e38
ITEMS = B * HEADS
WARM_UP = 10
F0, F1, F2, F3, F4, F5 = 2,2,2,8,2,10
SE_ITEM = 18
RING = 4
S0_SCALE = float(D) ** -0.5
S1_SCALE = float(DH) ** -0.5

START = (("ident", 128), ("x", B * D))
FIRST = (("wq_t", 128), ("wk_t", 128), ("wv_t", 128), ("wo", 128), ("bo_rows", 128),
         ("bq", 1), ("bk", 1), ("bv", 1), ("decay", 1), ("log_alpha", 1), ("wk1_b", 1))
SECOND = (("wk1", 128), ("wv1", 128), ("steps", 128), ("causal", 128), ("ww_t", 128), ("wr_t", 128),
          ("wgate_t", E0), ("lower", E0 * E0), ("wfc_t", E0 * I0), ("wproj_t", E0 * I0))
THIRD = (("wv1_b_rows", 128), ("wq1", 128), ("wo1", 128), ("wo1_b_rows", 128), ("wqkv_t", 384), ("bv_rows", 128), ("future", 128),
         ("select", 4 * DH), ("norm_g_rows", 128), ("norm_b_rows", 128), ("bg", 2 * E1), ("bu", 2 * E1),
         ("wq1_b", 1), ("bq_self", 1), ("bk_self", 1), ("norm_g", 1), ("norm_b", 1), ("slot_g", 1), ("slot_b", 1), ("scale", 1))

SIGNALS = """
start_in first_in second_in third_in ctxt_in0 ctxt_in1 ctxr_in mask0_in mask1_in0 mask1_in1 g_in0 g_in1 slots_in wg_in wu_in wd_in bd_in
ones_set dve_chain pool_chain mask0_ready spread_ready
var_ready rstd_ready xn_ready xnt_psum xnt_ready
fold_src fold_psum fold_ready qp_psum qp_ready row_psum xb_ready
mask1_ready s0_psum s0_masked s0_args s0_exp pt0_psum pt0_ready o0_psum o0_ready y0_psum x_ready
kp_psum kp_copied k_parts k_saved0 k_saved1 keys_in0 keys_in1 keys_in2 keys_in3 vp_psum v_copied v_ready
decay_exp decay_one decay_log v0_psum v0_ready st_psum sm_ready rd_psum rd_ready ro_psum
h0_psum rl_psum logits_max router_exp gates_ready gelu0_ready hw_ready ht_psum ht_ready f0_psum
q1_psum q_parts qr_psum queries_ready q_saved0 q_saved1 queries_in0 queries_in1
scores_psum scores_masked exp_ready pt_psum pt_copied pg_dve pg_pool pv_psum heads_copied heads_psum
at_ready att_psum att_ready wo_psum
q2_psum k2_psum v2_psum q2_ready k2_ready v2_ready gain_ready cs_psum cs_masked cs_exp pst_psum pst_ready ys_psum
se_rstd se_ready se_psum set_ready xf_ready xft_ready
ln_psum ln_max combine_exp ls_psum ls_max dispatch_exp dispatch_ready dt_psum dt_dve dt_act ct_psum ct_dve ct_act
sl_psum slots_ready g_psum u_psum gate_ready hmid_ready eo_psum eo_ready y_psum out_ready out_saved
""".split()


def columns(packed, names):
    views, at = {}, 0
    for name, n in names:
        views[name] = packed[:, at:at + n]
        at += n
    return views


def build(nc, a, out, k_dram, q_dram):
    with ExitStack() as ctx:
        def sb(name, shape, dt=F32):
            return ctx.enter_context(nc.sbuf_tensor(name, shape, dt))

        s = {name: ctx.enter_context(nc.semaphore(name)) for name in SIGNALS}
        keys_in = [s[f"keys_in{i}"] for i in range(RING)]

        start = sb("start", [128, sum(n for _, n in START)])
        first = sb("first", [128, sum(n for _, n in FIRST)])
        second = sb("second", [128, T])
        third = sb("third", [128, sum(n for _, n in THIRD)])
        w = {**columns(start, START), **columns(first, FIRST), **columns(second, SECOND), **columns(third, THIRD)}
        ident = w["ident"]
        ones = sb("ones", [128, 128])
        minus_half = sb("minus_half", [128, 8])
        ctx_t = sb("ctx_t", [128, B, T])
        ctx_r = sb("ctx_r", [128, B, C, D])
        g_t = sb("g_t", [128, B, C, N])
        mask1 = sb("mask1", [128, B, T])
        k_parts = sb("k_parts", [128, PARTS, B, T], BF16)
        keys = sb("keys", [ROWS, RING, T], BF16)
        queries = sb("queries", [ROWS, B, HEADS, N], BF16)
        v = sb("v", [128, B, C, D])
        lg = sb("lg", [128, 2, T])
        pg = sb("pg", [128, 2, T])
        pc = sb("pc", [128, 2, 512])
        se_t = sb("se_t", [128, NS])
        ring = [lg[:, 0, :], lg[:, 1, :], second[:, :]]
        mask0 = g_t[:, 1].rearrange("p c n -> p (c n)")
        k_full = [pc[:, :, :].rearrange("p a n -> p (a n)"), se_t[:, :]]
        se = se_t[:, :].rearrange("p (k d) -> p k d", d=D)
        spread = sb("spread", [128, 4, 5 * PARTS * DH], BF16)
        wg = ctx_t[:, :, :].rearrange("p b t -> p (b t)").rearrange("p (e f) -> p e f", e=E1)
        wu = ctx_r[:, :, :, :].rearrange("p b c d -> p (b c d)").rearrange("p (e f) -> p e f", e=E1)
        kw = k_parts[:, :, :, :].rearrange("p a b t -> p (a b t)").bitcast(F32)
        wd = kw[:, 0:E1 * 2 * D].rearrange("p (e k o) -> p e k o", e=E1, k=2)
        bd = kw[:, E1 * 2 * D:E1 * 2 * D + PAIRS * D].rearrange("p (k o) -> p k o", k=PAIRS)

        x = [w["x"].rearrange("p (b d) -> p b d", b=B)] + [sb(f"x{i}", [128, B, D])[:, :, :] for i in range(1, 6)]
        xb = sb("xb", [128, B, D])
        xn = sb("xn", [128, B, D])
        xnt = sb("xnt", [128, B, N + 2])
        stats = sb("stats", [128, 8, 6])
        mv = sb("mv", [128, 8, 2])
        ve = sb("ve", [128, 8])
        rstd = sb("rstd", [128, 8])
        folds = sb("folds", [128, 388])
        wob = sb("wob", [128, 128])
        t0 = sb("t0", [128, B * N])
        t1 = sb("t1", [128, B * N])
        t2 = sb("t2", [128, B * N])
        q_split = sb("q_split", [128, PARTS, B * N], BF16)
        heads_sb = sb("heads_sb", [128, 256])
        cols = sb("cols", [128, 96])
        m0 = cols[:, 0:4]
        flag, nflag, bias0, m0c, den0, rinv0 = (cols[:, 4 + 2 * i:6 + 2 * i] for i in range(6))
        rowc = cols[:, 16:18]
        bqbk = cols[:, 18:19]
        alpha, lgam, e1col = cols[:, 19:20], cols[:, 20:21], cols[:, 21:22]
        m2, den2, rinv2 = cols[:, 22:24], cols[:, 24:26], cols[:, 26:28]
        m_c, den_c, rinv_c = cols[:, 28:30], cols[:, 30:32], cols[:, 32:34]
        sg, sbias = cols[:, 34:35], cols[:, 35:36]
        scratch = cols[:, 78:79]
        mn = cols[:, 72:78]
        d_max, d_sum = cols[:, 40:56], cols[:, 56:72]
        den1 = sb("den1", [128, ITEMS])
        rinv1 = sb("rinv1", [128, ITEMS])
        router = sb("router", [128, 8, B * E0])
        versus = sb("versus", [128, 3, B * E0 * E0])

        ps = ctx.enter_context(nc.psum_tensor("ps", [128, 8, 512], F32))

        def wide(slot):
            return ps[:, 2 * slot:2 * slot + 2, :].rearrange("p a n -> p (a n)")

        combine = lg[:, 0, :].rearrange("p (b k n) -> p b k n", b=B, k=PAIRS)
        combine_t = lg[:, 1, :].rearrange("p (b k n) -> p b k n", b=B, k=PAIRS)
        dispatch_t = pg[:, 0, :].rearrange("p (k n) -> p k n", k=16)
        dispatch = pg[:, 1, :].rearrange("p (b n) -> p b n", b=B)
        slots_t = mask1[:, 0, :].rearrange("p (e b n) -> p e b n", e=E1, b=B)
        hmid = mask1[:, 1, 0:1024].rearrange("p (s k n) -> p s k n", s=4, k=2)
        eo = mask1[:, 1, 1024:1536].rearrange("p (s b n) -> p s b n", s=2, b=B)
        gate_h = mask1[:, 1, 1536:2048].rearrange("p (s k n) -> p s k n", s=2, k=2)
        hid = lg[:, 0, 0:1024]
        hid_t = lg[:, 1, 0:1024].rearrange("p (b k n) -> p b k n", b=B, k=4)

        def dispatch_group(g):
            return dispatch.rearrange("p b (k n) -> p k b n", n=128)[:, 2 * g:2 * g + 2]

        def bank_group(g):
            return ps[:, 4 + g, :].rearrange("p (k b n) -> p k b n", k=2, b=B)

        def xt(b):
            return xnt[:, b, 1:N + 1]

        xt2 = xnt[:, :, 1:N + 1]
        block = ctx.enter_context(nc.Block())

        @block.sync
        def _(sp):
            sp.dma_start(start[:, :], a["start"]).then_inc(s["start_in"], 16)
            sp.dma_start(first[:, :], a["first"]).then_inc(s["first_in"], 16)
            sp.dma_start(ctx_t[:, 0, :], a["ctx_t"][:, 0, :]).then_inc(s["ctxt_in0"], 16)
            sp.dma_start(mask0.bitcast(I32), a["mask0"]).then_inc(s["mask0_in"], 16)
            sp.dma_start(ctx_t[:, 1, :], a["ctx_t"][:, 1, :]).then_inc(s["ctxt_in1"], 16)
            sp.dma_start(second[:, 0:sum(n for _, n in SECOND)], a["second"]).then_inc(s["second_in"], 16)
            sp.dma_start(ctx_r[:, :, :, :], a["ctx_r"]).then_inc(s["ctxr_in"], 16)
            sp.dma_start(third[:, :], a["third"]).then_inc(s["third_in"], 16)

            def load_mask(b):
                sp.dma_start(mask1[:, b, :].bitcast(I32), a["mask1"][:, b, :]).then_inc(s[f"mask1_in{b}"], 16)

            def load_group(b):
                sp.dma_start(g_t[:, b], a["g_t"][:, b]).then_inc(s[f"g_in{b}"], 16)

            def save_keys(b):
                sp.wait_ge(s["k_parts"], 2 * b + 2)
                for p in range(PARTS):
                    sp.dma_start(k_dram[b, :, p], k_parts[:, p, b, :]).then_inc(s[f"k_saved{b}"], 16)

            def load_keys(i):
                b, h = i // HEADS, i % HEADS
                if i >= RING:
                    sp.wait_ge(s["scores_psum"], 2 * (i - RING) + 2)
                sp.dma_start(keys[:, i % RING, :], k_dram[b, h].rearrange("p d t -> (p d) t").unsqueeze(0)
                             .to_broadcast([PARTS, PARTS * DH, T])).then_inc(keys_in[i % RING], 16)

            load_mask(0)
            load_group(0)
            load_mask(1)
            sp.wait_ge(s["s0_masked"], 4)
            load_group(1)
            save_keys(0)
            sp.wait_ge(s["k_saved0"], 16 * PARTS)
            for i in range(RING):
                load_keys(i)
            save_keys(1)
            def save_queries(b):
                for r in range(PARTS):
                    sp.dma_start(q_dram[r, b].rearrange("d h n -> h d n"), q_split[:, r, b * N:(b + 1) * N])                      .then_inc(s[f"q_saved{b}"], 16)

            def load_queries(b, heads, signal):
                sp.wait_ge(s[f"q_saved{b}"], 16 * PARTS)
                for r in range(PARTS):
                    sp.dma_start(queries[PARTS * DH * r:PARTS * DH * (r + 1), b, heads, :].rearrange("r h n -> r (h n)"),
                                 q_dram[r, b][:, heads].rearrange("d h n -> d (h n)").unsqueeze(0)
                                 .to_broadcast([PARTS, DH, (heads.stop - heads.start) * N])).then_inc(signal, 16)

            sp.wait_ge(s["q_parts"], PARTS)
            save_queries(0)
            load_queries(0, slice(HEADS // 2, HEADS), s["queries_in0"])
            save_queries(1)
            sp.wait_ge(s["k_saved1"], 16 * PARTS)
            sp.wait_ge(s["vp_psum"], 4)
            sp.wait_ge(s["o0_psum"], 2)
            half_e = [slice(0, E1 // 2), slice(E1 // 2, E1)]
            extra = [(se, a["slots"], "slots_in")]
            extra += [(wg[:, h], a["wg"][:, h], "wg_in") for h in half_e]
            extra += [(wu[:, h], a["wu"][:, h], "wu_in") for h in half_e]
            extra += [(wd[:, h], a["wd"][:, h], "wd_in") for h in half_e]
            extra += [(bd, a["bd"], "bd_in")]
            for i in range(RING, ITEMS):
                load_keys(i)
                if i == RING:
                    load_queries(1, slice(0, HEADS), s["queries_in1"])
                if i % 3 == 0 and i // 3 - 2 < len(extra):
                    to, frm, signal = extra[i // 3 - 2]
                    sp.dma_start(to, frm).then_inc(s[signal], 16)
            sp.wait_ge(s["out_ready"], 2)
            sp.dma_start(out.rearrange("b n d -> n b d"), x[4]).then_inc(s["out_saved"], 16)
            sp.wait_ge(s["out_saved"], 16)

        @block.gpsimd
        def _(pool):
            chain = [0]

            def link(ins):
                chain[0] += 1
                ins.then_inc(s["pool_chain"], 1)
                pool.wait_ge(s["pool_chain"], chain[0])

            def inverse_root(k, n=B):
                pool.wait_ge(s["var_ready"], k + 1)
                pool.tensor_tensor(rstd[:, 0:n], ve[:, 0:n], minus_half[:, 0:n], ALU.pow).then_inc(s["rstd_ready"], 1)

            link(pool.memset(minus_half[:, :], -0.5))
            pool.memset(ones[:, :], 1.0).then_inc(s["ones_set"], 1)
            pool.memset(xnt[:, :, 0:1], 0.0).then_inc(s["ones_set"], 1)
            link(pool.memset(spread[:, :, :], 0.0))
            inverse_root(0)
            pool.wait_ge(s["mask0_in"], 16)
            pool.tensor_scalar(mask0, mask0.bitcast(I32), -MASKED, MASKED, ALU.mult, ALU.add).then_inc(s["mask0_ready"], 1)

            def split(kb):
                b, half = kb // 2, kb % 2
                part = [k_parts[:, p, b, half * HALF:(half + 1) * HALF] for p in range(PARTS)]
                rest = k_full[kb % 2]
                pool.wait_ge(s["kp_copied"], kb + 1)
                link(pool.tensor_tensor(rest, rest, part[0], ALU.subtract))
                link(pool.tensor_scalar(part[1], rest, 1.0, 0.0, ALU.mult, ALU.add))
                pool.tensor_tensor(part[2], rest, part[1], ALU.subtract).then_inc(s["k_parts"], 1)

            def widen_mask(b):
                pool.wait_ge(s[f"mask1_in{b}"], 16)
                pool.tensor_scalar(mask1[:, b, :], mask1[:, b, :].bitcast(I32), -MASKED, MASKED, ALU.mult, ALU.add)\
                    .then_inc(s["mask1_ready"], 1)

            def bias_values(vb):
                b, half = vb // 2, vb % 2
                pool.wait_ge(s["v_copied"], vb + 1)
                rows = v[:, b, half * 8:half * 8 + 8, :]
                pool.tensor_tensor(rows, rows, w["wv1_b_rows"].unsqueeze(1).to_broadcast([128, 8, D]), ALU.add)\
                    .then_inc(s["v_ready"], 1)

            pool.wait_ge(s["third_in"], 16)
            pool.tensor_scalar(spread[:, :, 2 * PARTS * DH:3 * PARTS * DH].rearrange("q n (p d) -> q n p d", p=PARTS),
                               w["select"].rearrange("q (n d) -> q n d", n=4).unsqueeze(2)
                               .to_broadcast([128, 4, PARTS, DH]), 1.0, 0.0, ALU.mult, ALU.add).then_inc(s["spread_ready"], 1)
            split(0)
            inverse_root(1)
            split(1)
            inverse_root(2)
            split(2)
            split(3)
            widen_mask(0)
            inverse_root(3)
            bias_values(0)
            bias_values(1)
            bias_values(2)
            bias_values(3)
            widen_mask(1)
            for i in range(ITEMS):
                b = i // HEADS
                if i % HEADS == 0:
                    pool.wait_ge(s[f"g_in{b}"], 16)
                for n, q in enumerate((1, 3)):
                    pool.wait_ge(s["pt_copied"], 2 * i + n + 1)
                    if n == 0 and i >= 2:
                        pool.wait_ge(s["pv_psum"], i - 1)
                    g = g_t[:, b].rearrange("p c n -> p (c n)")[:, q * 512:(q + 1) * 512]
                    pool.tensor_tensor(pg[:, i % 2, q * 512:(q + 1) * 512], pc[:, n, :], g, ALU.mult)\
                        .then_inc(s["pg_pool"], 1)
                if i == SE_ITEM + 8:
                    inverse_root(4, 8)
            inverse_root(5)
            inverse_root(6)

        @block.scalar
        def _(act):
            act.wait_ge(s["first_in"], 16)
            act.activation(e1col, w["decay"], ACT.Exp, scale=-1.0).then_inc(s["decay_exp"], 1)
            act.wait_ge(s["decay_one"], 1)
            act.activation(lgam, e1col, ACT.Ln).then_inc(s["decay_log"], 1)
            act.activation(alpha, w["log_alpha"], ACT.Exp).then_inc(s["decay_exp"], 1)
            for b in range(B):
                act.wait_ge(s["s0_args"], b + 1)
                act.activation(lg[:, b, :], lg[:, b, :], ACT.Exp, bias=bias0[:, b:b + 1], scale=nflag[:, b:b + 1],
                               accum_out=den0[:, b:b + 1]).then_inc(s["s0_exp"], 1)
            act.wait_ge(s["second_in"], 16)
            act.wait_ge(s["decay_one"], 2)
            act.activation(w["steps"], w["steps"], ACT.Exp, scale=lgam).then_inc(s["decay_log"], 1)
            def copy_keys(kb):
                b, half = kb // 2, kb % 2
                act.wait_ge(s["kp_psum"], kb + 1)
                if kb >= 2:
                    act.wait_ge(s["k_parts"], kb - 1)
                act.activation(k_full[kb % 2], wide(kb % 2), ACT.Identity, bias=w["wk1_b"])
                act.activation(k_parts[:, 0, b, half * HALF:(half + 1) * HALF], wide(kb % 2), ACT.Identity,
                               bias=w["wk1_b"]).then_inc(s["kp_copied"], 1)

            def copy_values(vb):
                b, half = vb // 2, vb % 2
                act.wait_ge(s["vp_psum"], vb + 1)
                act.activation(v[:, b, half * 8:half * 8 + 8, :].rearrange("p c d -> p (c d)"), wide(vb % 2), ACT.Copy)\
                   .then_inc(s["v_copied"], 1)

            for kb in range(4):
                copy_keys(kb)
            act.wait_ge(s["logits_max"], 1)
            act.activation(router[:, 2, :], router[:, 1, :], ACT.Exp).then_inc(s["router_exp"], 1)
            act.wait_ge(s["h0_psum"], 1)
            act.activation(hid, ps[:, 4:6, :].rearrange("p a n -> p (a n)"), ACT.Gelu).then_inc(s["gelu0_ready"], 1)
            for vb in range(3):
                copy_values(vb)
            act.activation(scratch, alpha, ACT.Exp)
            copy_values(3)

            def copy_queries(g):
                act.wait_ge(s["qr_psum"], g + 1)
                act.activation(queries[:, 0, 4 * g:4 * g + 4, :].rearrange("r h n -> r (h n)"), ps[0:ROWS, 4 + g, :],
                               ACT.Copy).then_inc(s["queries_ready"], 1)

            copy_queries(0)
            copy_queries(1)
            def exponentials(i):
                act.wait_ge(s["scores_masked"], 2 * i + 2)
                act.activation(ring[i % 3], ring[i % 3], ACT.Exp, bias=mn[:, 2 * (i % 3) + 1:2 * (i % 3) + 2],
                               scale=-1.0, accum_out=den1[:, i:i + 1]).then_inc(s["exp_ready"], 1)

            def copy_quarter(i, n):
                act.wait_ge(s["pt_psum"], 4 * i + 2 * n + 2)
                if i > 0:
                    act.wait_ge(s["pg_pool"], 2 * (i - 1) + n + 1)
                act.activation(pc[:, n, :], ps[:, 7 if n else 5, :], ACT.Copy).then_inc(s["pt_copied"], 1)

            def copy_heads(g):
                act.wait_ge(s["pv_psum"], 2 * g + 2)
                if g:
                    act.wait_ge(s["heads_psum"], g)
                act.activation(heads_sb[:, :], ps[:, 6, 0:256], ACT.Copy).then_inc(s["heads_copied"], 1)

            exponentials(0)
            for i in range(ITEMS):
                if i % 2 and i >= 3:
                    copy_heads((i - 3) // 2)
                if i + 1 < ITEMS:
                    exponentials(i + 1)
                copy_quarter(i, 0)
                copy_quarter(i, 1)
            copy_heads(ITEMS // 2 - 1)
            act.wait_ge(s["se_psum"], 1)
            act.wait_ge(s["gain_ready"], 2)
            act.activation(se_t[:, :], wide(0), ACT.Identity, scale=sg, bias=sbias).then_inc(s["set_ready"], 1)
            act.wait_ge(s["k2_psum"], 1)
            act.activation(t1[:, :], ps[:, 5, 0:256], ACT.Identity, bias=w["bk_self"]).then_inc(s["k2_ready"], 1)
            for b in range(B):
                act.wait_ge(s["cs_masked"], b + 1)
                act.activation(lg[:, 0, b * N:(b + 1) * N], lg[:, 0, b * N:(b + 1) * N], ACT.Exp, bias=m2[:, b:b + 1],
                               scale=-1.0, accum_out=den2[:, b:b + 1]).then_inc(s["cs_exp"], 1)
            for g in range(4):
                act.wait_ge(s["ls_max"], g + 1)
                for t in range(4 * g, 4 * g + 4):
                    ins = act.activation(dispatch_t[:, t, :], ps[:, 4 + g, (t % 4) * N:(t % 4 + 1) * N], ACT.Exp,
                                         bias=d_max[:, t:t + 1], accum_out=d_sum[:, t:t + 1])
                ins.then_inc(s["dispatch_exp"], 1)
            for g in (2, 3):
                act.wait_ge(s["dt_psum"], g + 1)
                act.activation(dispatch_group(g), bank_group(g), ACT.Copy).then_inc(s["dt_act"], 1)
            for b in range(B):
                act.wait_ge(s["ln_max"], b + 1)
                act.activation(combine[:, b, :, :], wide(b).rearrange("p (k n) -> p k n", k=PAIRS), ACT.Exp,
                               bias=m_c[:, b:b + 1], accum_out=den_c[:, b:b + 1]).then_inc(s["combine_exp"], 1)
            act.activation(scratch, alpha, ACT.Gelu)

            def gate(e):
                act.wait_ge(s["g_psum"], e + 1)
                if e >= 2:
                    act.wait_ge(s["hmid_ready"], 2 * (e - 1))
                for k in range(2):
                    act.activation(gate_h[:, e % 2, k, :], ps[:, 4 + e % 2, k * 128:(k + 1) * 128], ACT.Gelu,
                                   bias=w["bg"][:, 2 * e + k:2 * e + k + 1]).then_inc(s["gate_ready"], 1)

            gate(0)
            gate(1)
            act.wait_ge(s["ct_psum"], 2)
            act.activation(combine_t[:, 1], wide(1).rearrange("p (k n) -> p k n", k=PAIRS), ACT.Copy).then_inc(s["ct_act"], 1)
            for e in range(2, E1):
                gate(e)

        @block.vector
        def _(dve):
            chain = [0]

            def link(ins):
                chain[0] += 1
                ins.then_inc(s["dve_chain"], 1)
                dve.wait_ge(s["dve_chain"], chain[0])

            def step(ins):
                chain[0] += 1
                ins.then_inc(s["dve_chain"], 1)

            def normalise(xin, xout, k, between=None):
                for b in range(B):
                    step(dve.bn_stats(stats[:, b, :], xin[:, b, :]))
                dve.wait_ge(s["dve_chain"], chain[0])
                for b in range(B):
                    step(dve.bn_aggr(mv[:, b, :], stats[:, b, :]))
                dve.wait_ge(s["dve_chain"], chain[0])
                dve.tensor_scalar(ve[:, 0:B], mv[:, 0:B, 1:2].rearrange("p b o -> p (b o)"), EPS, None, ALU.add)\
                   .then_inc(s["var_ready"], 1)
                if between:
                    between()
                dve.wait_ge(s["rstd_ready"], k + 1)
                for b in range(B):
                    dve.tensor_scalar(xout[:, b, :], xin[:, b, :], mv[:, b, 0:1], rstd[:, b:b + 1],
                                      ALU.subtract, ALU.mult).then_inc(s["xn_ready"], 1)

            def keep_transpose(k):
                dve.wait_ge(s["xnt_psum"], k + 1)
                dve.tensor_copy(xt2, ps[:, 6, 0:256].rearrange("p (b n) -> p b n", b=B)).then_inc(s["xnt_ready"], 1)

            dve.wait_ge(s["start_in"], 16)

            def fold_sources():
                dve.wait_ge(s["first_in"], 16)
                dve.tensor_tensor(t2[:, 0:1], w["bq"], w["bk"], ALU.mult).then_inc(s["fold_src"], 1)
                dve.tensor_scalar(wob[:, :], w["wo"], w["bv"], None, ALU.mult).then_inc(s["fold_src"], 1)

            normalise(x[0], xn, 0, fold_sources)
            dve.wait_ge(s["fold_psum"], 1)
            dve.tensor_copy(folds[:, 0:387], ps[:, 7, 0:387]).then_inc(s["fold_ready"], 1)
            dve.wait_ge(s["ones_set"], 2)
            keep_transpose(0)
            dve.wait_ge(s["decay_exp"], 1)
            dve.tensor_scalar(e1col, e1col, 1.0, None, ALU.add).then_inc(s["decay_one"], 1)
            dve.wait_ge(s["fold_ready"], 1)
            dve.wait_ge(s["qp_psum"], 1)
            dve.tensor_scalar(t0[:, :], ps[:, 4, 0:256], folds[:, 384:385], -S0_SCALE, ALU.add, ALU.mult)\
               .then_inc(s["qp_ready"], 1)
            dve.wait_ge(s["row_psum"], 1)
            link(dve.tensor_scalar(rowc, ps[:, 5, 0:2], folds[:, 386:387], -S0_SCALE, ALU.add, ALU.mult))
            dve.wait_ge(s["mask0_ready"], 1)
            for b in range(B):
                for half in range(2):
                    u = 2 * b + half
                    dve.wait_ge(s["s0_psum"], u + 1)
                    dve.tensor_tensor_reduce(lg[:, b, half * HALF:(half + 1) * HALF], wide(half),
                                             mask0[:, half * HALF:(half + 1) * HALF], 1.0,
                                             FAR if half == 0 else m0[:, u - 1:u], ALU.add, ALU.min, m0[:, u:u + 1])\
                       .then_inc(s["s0_masked"], 1)
                    dve.wait_ge(s["s0_masked"], u + 1)
                m, f, o = m0[:, u:u + 1], flag[:, b:b + 1], slice(b, b + 1)
                step(dve.tensor_tensor(m0c[:, o], m, rowc[:, o], ALU.add))
                step(dve.tensor_scalar(f, m, 0.5 * MASKED, None, ALU.is_lt))
                link(dve.tensor_scalar(nflag[:, o], m, 0.5 * MASKED, -1.0, ALU.is_lt, ALU.mult))
                dve.scalar_tensor_tensor(out=bias0[:, o], in0=m0c[:, o], scalar=rowc[:, o], in1=f,
                                         op0=ALU.subtract, op1=ALU.mult).then_inc(s["s0_args"], 1)
            dve.wait_ge(s["decay_log"], 1)
            dve.tensor_scalar(lgam, lgam, -1.0, None, ALU.mult).then_inc(s["decay_one"], 1)
            link(dve.tensor_tensor(xb[:, :, :], x[0], w["bo_rows"].unsqueeze(1).to_broadcast([128, B, D]), ALU.add))
            link(dve.tensor_tensor(xb[:, :, :], xb[:, :, :],
                                   folds[:, 256:384].unsqueeze(1).to_broadcast([128, B, D]), ALU.add))
            for b in range(B):
                for q in range(4):
                    t = 4 * b + q
                    dve.wait_ge(s["pt0_psum"], t + 1)
                    dve.tensor_copy(pg[:, b, q * 512:(q + 1) * 512], ps[:, 4 + t % 2, :]).then_inc(s["pt0_ready"], 1)
                link(dve.reciprocal(rinv0[:, b:b + 1], den0[:, b:b + 1]))

            def end_cross_attention(b):
                dve.wait_ge(s["y0_psum"], b + 1)
                link(dve.scalar_tensor_tensor(out=x[1][:, b, :], in0=ps[:, 7, b * N:(b + 1) * N],
                                              scalar=rinv0[:, b:b + 1], in1=xb[:, b, :], op0=ALU.mult, op1=ALU.add))

            for b in range(B):
                dve.wait_ge(s["o0_psum"], b + 1)
                dve.tensor_copy(t1[:, b * N:(b + 1) * N], ps[:, 6, b * N:(b + 1) * N]).then_inc(s["o0_ready"], 1)
                end_cross_attention(b)

            def zero_future():
                dve.wait_ge(s["decay_log"], 2)
                link(dve.tensor_tensor(w["steps"], w["steps"], w["causal"], ALU.mult))

            normalise(x[1], xn, 1, zero_future)
            keep_transpose(1)

            dve.wait_ge(s["v0_psum"], 1)
            dve.tensor_copy(t0[:, :], ps[:, 7, 0:256]).then_inc(s["v0_ready"], 1)
            dve.wait_ge(s["st_psum"], 1)
            dve.tensor_tensor(t1[:, :].rearrange("p (b n) -> p b n", b=B), ps[:, 4, 0:256].rearrange("p (b n) -> p b n", b=B),
                              w["steps"].unsqueeze(1).to_broadcast([128, B, N]), ALU.mult).then_inc(s["sm_ready"], 1)
            dve.wait_ge(s["rd_psum"], 1)
            dve.tensor_copy(t2[:, :], ps[:, 5, 0:256]).then_inc(s["rd_ready"], 1)
            dve.wait_ge(s["ro_psum"], 1)
            link(dve.scalar_tensor_tensor(out=xb[:, :, :].rearrange("p b d -> p (b d)"), in0=ps[:, 6, 0:256], scalar=alpha,
                                          in1=xn[:, :, :].rearrange("p b d -> p (b d)"), op0=ALU.mult, op1=ALU.add))
            link(dve.tensor_tensor(x[2][:, :, :], x[1][:, :, :], xb[:, :, :], ALU.add))

            normalise(x[2], xn, 2)
            keep_transpose(2)
            l, shifted, ex, rank, wts, gates = (router[:, i, :] for i in (0, 1, 2, 3, 4, 5))
            pair, top = router[:, 6, 0:B], router[:, 7, 0:B]

            def by_batch(t):
                return t.rearrange("p (b e) -> p b e", b=B)

            def over_rest(t):
                return t.unsqueeze(2).to_broadcast([128, B, E0])

            dve.wait_ge(s["rl_psum"], 1)
            link(dve.tensor_copy(l, ps[:, 7, 0:16]))
            link(dve.tensor_reduce(top, by_batch(l), AX_X, ALU.max))
            dve.tensor_tensor(by_batch(shifted), by_batch(l), over_rest(top), ALU.subtract).then_inc(s["logits_max"], 1)
            me = by_batch(l).unsqueeze(3).to_broadcast([128, B, E0, E0])
            cube = [versus[:, i, :].rearrange("p (b e j) -> p b e j", b=B, e=E0) for i in range(3)]
            for b in range(B):
                other = by_batch(l)[:, b, :].unsqueeze(1).to_broadcast([128, E0, E0])
                link(dve.tensor_tensor(cube[0][:, b], other, me[:, b], ALU.is_gt))
                link(dve.tensor_tensor(cube[1][:, b], other, me[:, b], ALU.is_equal))
                link(dve.tensor_tensor(cube[1][:, b], cube[1][:, b], w["lower"].rearrange("p (e j) -> p e j", e=E0), ALU.mult))
            link(dve.tensor_tensor(versus[:, 2, :], versus[:, 0, :], versus[:, 1, :], ALU.add))
            link(dve.tensor_reduce(rank, versus[:, 2, :].rearrange("p (e j) -> p e j", j=E0), AX_X, ALU.add))
            dve.wait_ge(s["router_exp"], 1)
            link(dve.scalar_tensor_tensor(out=wts, in0=rank, scalar=1.5, in1=ex, op0=ALU.is_lt, op1=ALU.mult))
            link(dve.tensor_reduce(pair, by_batch(wts), AX_X, ALU.add))
            link(dve.reciprocal(pair, pair))
            link(dve.tensor_tensor(by_batch(gates), by_batch(wts), over_rest(pair), ALU.mult))
            dve.wait_ge(s["gelu0_ready"], 1)
            dve.tensor_tensor(hid.rearrange("p (g i) -> p g i", i=I0), hid.rearrange("p (g i) -> p g i", i=I0),
                              gates.unsqueeze(2).to_broadcast([128, B * E0, I0]), ALU.mult).then_inc(s["hw_ready"], 1)
            for b in range(B):
                dve.wait_ge(s["ht_psum"], b + 1)
                dve.tensor_copy(lg[:, 1, b * 512:(b + 1) * 512], ps[:, 6 + b, :]).then_inc(s["ht_ready"], 1)
            dve.wait_ge(s["f0_psum"], 1)
            link(dve.tensor_tensor(x[3][:, :, :].rearrange("p b d -> p (b d)"), ps[:, 4, 0:256],
                                   x[2][:, :, :].rearrange("p b d -> p (b d)"), ALU.add))

            dve.wait_ge(s["third_in"], 16)

            def next_bias():
                dve.tensor_tensor(sg, w["slot_g"], w["scale"], ALU.mult).then_inc(s["gain_ready"], 1)
                dve.tensor_tensor(sbias, w["slot_b"], w["scale"], ALU.mult).then_inc(s["gain_ready"], 1)

            normalise(x[3], xn, 3, next_bias)
            keep_transpose(3)
            link(dve.tensor_tensor(xb[:, :, :], x[3][:, :, :], w["wo1_b_rows"].unsqueeze(1).to_broadcast([128, B, D]), ALU.add))
            dve.wait_ge(s["q1_psum"], 1)
            link(dve.tensor_scalar(t0[:, :], ps[:, 5, 0:256], w["wq1_b"], -S1_SCALE, ALU.add, ALU.mult))
            for p in range(PARTS - 1):
                dve.tensor_copy(q_split[:, p, :], t0[:, :]).then_inc(s["q_parts"], 1)
                dve.wait_ge(s["q_parts"], p + 1)
                if p == 0:
                    link(dve.tensor_tensor(t0[:, :], t0[:, :], q_split[:, p, :], ALU.subtract))
            dve.tensor_tensor(q_split[:, 2, :], t0[:, :], q_split[:, 1, :], ALU.subtract).then_inc(s["q_parts"], 1)

            def mask_scores(i, half):
                b, slot = i // HEADS, 2 * (i % 3) + half
                if i % HEADS == 0:
                    dve.wait_ge(s["mask1_ready"], b + 1)
                dve.wait_ge(s["scores_psum"], 2 * i + half + 1)
                if half == 0 and i >= 3:
                    dve.wait_ge(s["pt_psum"], 4 * (i - 2))
                if half:
                    dve.wait_ge(s["scores_masked"], 2 * i + 1)
                dve.tensor_tensor_reduce(ring[i % 3][:, half * HALF:(half + 1) * HALF], wide(half),
                                         mask1[:, b, half * HALF:(half + 1) * HALF], 1.0,
                                         mn[:, slot - 1:slot] if half else FAR, ALU.add, ALU.min, mn[:, slot:slot + 1])\
                   .then_inc(s["scores_masked"], 1)

            def by_group(i, n):
                q = 2 * n
                if i % HEADS == 0:
                    dve.wait_ge(s[f"g_in{i // HEADS}"], 16)
                dve.wait_ge(s["pt_psum"], 4 * i + q + 1)
                if n == 0 and i >= 2:
                    dve.wait_ge(s["pv_psum"], i - 1)
                g = g_t[:, i // HEADS].rearrange("p c n -> p (c n)")[:, q * 512:(q + 1) * 512]
                dve.tensor_tensor(pg[:, i % 2, q * 512:(q + 1) * 512], ps[:, 4, :], g, ALU.mult)\
                   .then_inc(s["pg_dve"], 1)

            def slot_embeddings(k):
                if k < 8:
                    if k == 0:
                        dve.wait_ge(s["slots_in"], 16)
                    link(dve.bn_stats(stats[:, k, :], se[:, k, :]))
                    link(dve.bn_aggr(mv[:, k, :], stats[:, k, :]))
                    if k == 7:
                        dve.tensor_scalar(ve[:, :], mv[:, :, 1:2].rearrange("p b o -> p (b o)"), EPS, None, ALU.add)\
                           .then_inc(s["var_ready"], 1)
                elif k >= 10:
                    dve.wait_ge(s["rstd_ready"], 5)
                    for t in range(2 * (k - 10), 2 * (k - 10) + 2):
                        dve.tensor_scalar(se[:, t, :], se[:, t, :], mv[:, t, 0:1], rstd[:, t:t + 1],
                                          ALU.subtract, ALU.mult).then_inc(s["se_ready"], 1)

            mask_scores(0, 0)
            mask_scores(0, 1)
            mask_scores(1, 0)
            mask_scores(1, 1)
            for n in range(2):
                by_group(0, n)
                mask_scores(2, n)
            for i in range(1, ITEMS):
                for n in range(2):
                    if i + 2 < ITEMS:
                        mask_scores(i + 2, n)
                    by_group(i, n)
                if i >= SE_ITEM:
                    slot_embeddings(i - SE_ITEM)
            dve.wait_ge(s["exp_ready"], ITEMS)
            link(dve.reciprocal(rinv1[:, :], den1[:, :]))
            dve.wait_ge(s["heads_psum"], ITEMS // 2)
            dve.tensor_tensor(t0[:, :].rearrange("p (i d) -> p i d", d=DH), ps[:, 6, 256:512].rearrange("p (i d) -> p i d", d=DH),
                              rinv1[:, :].unsqueeze(2).to_broadcast([128, ITEMS, DH]), ALU.mult).then_inc(s["at_ready"], 1)
            dve.wait_ge(s["att_psum"], 1)
            dve.tensor_copy(t1[:, :], ps[:, 4, 0:256]).then_inc(s["att_ready"], 1)
            dve.wait_ge(s["wo_psum"], 1)
            link(dve.tensor_tensor(x[4][:, :, :].rearrange("p b d -> p (b d)"), ps[:, 5, 0:256],
                                   xb[:, :, :].rearrange("p b d -> p (b d)"), ALU.add))

            normalise(x[4], xn, 5)
            keep_transpose(4)
            dve.wait_ge(s["q2_psum"], 1)
            dve.tensor_scalar(t0[:, :], ps[:, 7, 0:256], w["bq_self"], -S0_SCALE, ALU.add, ALU.mult).then_inc(s["q2_ready"], 1)
            dve.wait_ge(s["cs_psum"], 1)
            for b in range(B):
                dve.tensor_tensor_reduce(lg[:, 0, b * N:(b + 1) * N], ps[:, 4, b * N:(b + 1) * N], w["future"], 1.0, FAR,
                                         ALU.add, ALU.min, m2[:, b:b + 1]).then_inc(s["cs_masked"], 1)
            dve.wait_ge(s["v2_psum"], 1)
            dve.tensor_tensor(t2[:, :].rearrange("p (b n) -> p b n", b=B), ps[:, 3, 0:256].rearrange("p (b n) -> p b n", b=B),
                              w["bv_rows"].unsqueeze(1).to_broadcast([128, B, D]), ALU.add).then_inc(s["v2_ready"], 1)
            dve.wait_ge(s["pst_psum"], 1)
            dve.tensor_copy(t1[:, :], ps[:, 5, 0:256]).then_inc(s["pst_ready"], 1)
            link(dve.reciprocal(rinv2, den2))
            dve.wait_ge(s["ys_psum"], 1)
            for b in range(B):
                link(dve.scalar_tensor_tensor(out=x[5][:, b, :], in0=ps[:, 6, b * N:(b + 1) * N], scalar=rinv2[:, b:b + 1],
                                              in1=x[4][:, b, :], op0=ALU.mult, op1=ALU.add))

            normalise(x[5], xn, 6)
            dve.wait_ge(s["xnt_psum"], 6)
            dve.tensor_scalar(t0[:, :], ps[:, 6, 0:256], w["norm_g"], w["norm_b"], ALU.mult, ALU.add).then_inc(s["xft_ready"], 1)
            link(dve.tensor_tensor(xb[:, :, :], xn[:, :, :], w["norm_g_rows"].unsqueeze(1).to_broadcast([128, B, D]), ALU.mult))
            dve.tensor_tensor(xb[:, :, :], xb[:, :, :], w["norm_b_rows"].unsqueeze(1).to_broadcast([128, B, D]), ALU.add)\
               .then_inc(s["xf_ready"], 1)
            for g in range(4):
                dve.wait_ge(s["ls_psum"], g + 1)
                dve.tensor_reduce(d_max[:, 4 * g:4 * g + 4], ps[:, 4 + g, :].rearrange("p (t n) -> p t n", n=N), AX_X, ALU.max,
                                  negate=True).then_inc(s["ls_max"], 1)
            def scale_dispatch(g):
                dve.wait_ge(s["dispatch_exp"], g + 1)
                group = slice(4 * g, 4 * g + 4)
                link(dve.reciprocal(d_sum[:, group], d_sum[:, group]))
                dve.tensor_tensor(dispatch_t[:, group, :], dispatch_t[:, group, :],
                                  d_sum[:, group].unsqueeze(2).to_broadcast([128, 4, N]), ALU.mult)\
                   .then_inc(s["dispatch_ready"], 1)

            def keep_dispatch(g):
                dve.wait_ge(s["dt_psum"], g + 1)
                dve.tensor_copy(dispatch_group(g), bank_group(g)).then_inc(s["dt_dve"], 1)

            def combine_maximum(b):
                dve.wait_ge(s["ln_psum"], b + 1)
                dve.tensor_reduce(m_c[:, b:b + 1], wide(b), AX_X, ALU.max, negate=True).then_inc(s["ln_max"], 1)

            scale_dispatch(0)
            scale_dispatch(1)
            keep_dispatch(0)
            scale_dispatch(2)
            keep_dispatch(1)
            scale_dispatch(3)
            combine_maximum(0)
            combine_maximum(1)
            for n in range(2):
                dve.wait_ge(s["sl_psum"], n + 1)
                dve.tensor_copy(slots_t[:, n * PAIRS:(n + 1) * PAIRS, :, :].rearrange("p e b n -> p b e n"),
                                wide(2 + n).rearrange("p (b e n) -> p b e n", b=B, e=PAIRS)).then_inc(s["slots_ready"], 1)
            dve.wait_ge(s["combine_exp"], 2)
            link(dve.reciprocal(rinv_c, den_c))
            dve.wait_ge(s["bd_in"], 16)

            def by_gate(e):
                dve.wait_ge(s["u_psum"], e + 1)
                if e >= 4:
                    dve.wait_ge(s["eo_psum"], e // 2 - 1)
                for k in range(2):
                    dve.wait_ge(s["gate_ready"], 2 * e + k + 1)
                    dve.scalar_tensor_tensor(out=hmid[:, e % 4, k, :], in0=ps[:, 6 + e % 2, k * 128:(k + 1) * 128],
                                             scalar=w["bu"][:, 2 * e + k:2 * e + k + 1], in1=gate_h[:, e % 2, k, :],
                                             op0=ALU.add, op1=ALU.mult).then_inc(s["hmid_ready"], 1)

            def add_down_bias(p):
                dve.wait_ge(s["eo_psum"], p + 1)
                if p >= 2:
                    dve.wait_ge(s["y_psum"], p - 1)
                dve.tensor_tensor(eo[:, p % 2], ps[:, 2 + p % 2, 0:256].rearrange("p (b n) -> p b n", b=B),
                                  bd[:, p, :].unsqueeze(1).to_broadcast([128, B, D]), ALU.add).then_inc(s["eo_ready"], 1)

            by_gate(0)
            by_gate(1)
            dve.wait_ge(s["ct_psum"], 1)
            dve.tensor_copy(combine_t[:, 0], wide(0).rearrange("p (k n) -> p k n", k=PAIRS)).then_inc(s["ct_dve"], 1)
            for p in range(1, PAIRS):
                by_gate(2 * p)
                add_down_bias(p - 1)
                by_gate(2 * p + 1)
            add_down_bias(PAIRS - 1)
            dve.wait_ge(s["y_psum"], PAIRS)
            for b in range(B):
                dve.scalar_tensor_tensor(out=x[4][:, b, :], in0=ps[:, b, 0:128], scalar=rinv_c[:, b:b + 1],
                                         in1=x[5][:, b, :], op0=ALU.mult, op1=ALU.add).then_inc(s["out_ready"], 1)

        @block.tensor
        def _(pe):
            mm, tp = pe.matmul, pe.transpose

            def transpose_rows(k, ready, src=xn):
                for b in range(B):
                    pe.wait_ge(s["xn_ready"], ready + b + 1)
                    ins = tp(ps[:, 6, b * N:(b + 1) * N], src[:, b, :], ident)
                ins.then_inc(s["xnt_psum"], 1)

            def keep_busy(n, bank):
                for _ in range(n):
                    mm(ps[:, bank, 0:128], ones[:, :], ones[:, :], start=True, stop=True)

            pe.wait_ge(s["ones_set"], 1)
            keep_busy(WARM_UP, 0)
            pe.wait_ge(s["first_in"], 16)
            mm(ps[:, 7, 0:128], w["wq_t"], w["wk_t"], start=True, stop=True)
            mm(ps[:, 7, 128:256], w["wv_t"], w["wo"], start=True, stop=True)
            mm(ps[:, 7, 384:385], w["wk_t"], w["bq"], start=True, stop=True)
            mm(ps[:, 7, 385:386], w["wq_t"], w["bk"], start=True, stop=True)
            pe.wait_ge(s["fold_src"], 2)
            mm(ps[:, 7, 256:384], ones[:, :], wob[:, :], start=True, stop=True)
            mm(ps[:, 7, 386:387], ones[:, :], t2[:, 0:1], start=True, stop=True).then_inc(s["fold_psum"], 1)
            keep_busy(F0, 0)
            transpose_rows(0, 0)
            keep_busy(F1, 0)
            pe.wait_ge(s["fold_ready"], 1)
            pe.wait_ge(s["xnt_ready"], 1)
            mm(ps[:, 4, 0:256], folds[:, 0:128], xt2, start=True, stop=True).then_inc(s["qp_psum"], 1)
            for b in range(B):
                ins = mm(ps[:, 5, b:b + 1], xt(b), folds[:, 385:386], start=True, stop=True)
            ins.then_inc(s["row_psum"], 1)
            keep_busy(F2, 0)
            pe.wait_ge(s["qp_ready"], 1)
            for b in range(B):
                pe.wait_ge(s[f"ctxt_in{b}"], 16)
                for half in range(2):
                    if b:
                        pe.wait_ge(s["s0_masked"], half + 1)
                    for n in range(2):
                        ins = mm(ps[:, 2 * half + n, :], t0[:, b * N:(b + 1) * N],
                                 ctx_t[:, b, half * HALF + n * 512:half * HALF + (n + 1) * 512], start=True, stop=True)
                    ins.then_inc(s["s0_psum"], 1)

            def project_keys(kb):
                b, half = kb // 2, kb % 2
                if kb < 2:
                    pe.wait_ge(s["s0_masked"], 3 + kb)
                else:
                    pe.wait_ge(s["kp_copied"], kb - 1)
                for n in range(2):
                    ins = mm(ps[:, 2 * half + n, :], w["wk1"],
                             ctx_t[:, b, half * HALF + n * 512:half * HALF + (n + 1) * 512], start=True, stop=True)
                ins.then_inc(s["kp_psum"], 1)

            def project_values(vb):
                b, half = vb // 2, vb % 2
                if vb < 2:
                    pe.wait_ge(s["kp_copied"], 3 + vb)
                else:
                    pe.wait_ge(s["v_copied"], vb - 1)
                for c in range(8):
                    t = (half * 8 + c) * 128
                    ins = mm(ps[:, 2 * half + c // 4, (c % 4) * 128:(c % 4 + 1) * 128], ctx_t[:, b, t:t + 128], w["wv1"],
                             start=True, stop=True)
                ins.then_inc(s["vp_psum"], 1)

            def transpose_first(b, q):
                t = 4 * b + q
                if q == 0:
                    pe.wait_ge(s["s0_exp"], b + 1)
                if t >= 2:
                    pe.wait_ge(s["pt0_ready"], t - 1)
                for n in range(4):
                    c = 4 * q + n
                    ins = tp(ps[:, 4 + t % 2, n * 128:(n + 1) * 128], lg[:, b, c * 128:(c + 1) * 128], ident)
                ins.then_inc(s["pt0_psum"], 1)

            def weigh_context(b, q):
                if b and q == 0:
                    pe.wait_ge(s["o0_ready"], 1)
                pe.wait_ge(s["pt0_ready"], 4 * b + q + 1)
                for c in range(4 * q, 4 * q + 4):
                    ins = mm(ps[:, 6, b * N:(b + 1) * N], ctx_r[:, b, c, :], pg[:, b, c * 128:(c + 1) * 128],
                             start=(c == 0), stop=(c == C - 1))
                if q == 3:
                    ins.then_inc(s["o0_psum"], 1)

            def project_context(b):
                pe.wait_ge(s["o0_ready"], b + 1)
                mm(ps[:, 7, b * N:(b + 1) * N], t1[:, b * N:(b + 1) * N], folds[:, 128:256], start=True, stop=True)\
                    .then_inc(s["y0_psum"], 1)

            pe.wait_ge(s["second_in"], 16)
            project_keys(0)
            for q in range(4):
                transpose_first(0, q)
            pe.wait_ge(s["ctxr_in"], 16)
            for q in range(4):
                weigh_context(0, q)
                transpose_first(1, q)
            project_context(0)
            for q in range(4):
                weigh_context(1, q)
            project_keys(1)
            project_context(1)
            project_keys(2)
            transpose_rows(1, 2)
            pe.wait_ge(s["xnt_ready"], 2)
            for b in range(B):
                ins = mm(ps[:, 7, b * N:(b + 1) * N], xt(b), w["ww_t"], start=True, stop=True)
            ins.then_inc(s["v0_psum"], 1)
            for b in range(B):
                ins = mm(ps[:, 4, b * N:(b + 1) * N], xnt[:, b, 0:N], xt(b), start=True, stop=True)
            ins.then_inc(s["st_psum"], 1)
            pe.wait_ge(s["v0_ready"], 1)
            pe.wait_ge(s["sm_ready"], 1)
            for b in range(B):
                ins = mm(ps[:, 5, b * N:(b + 1) * N], t0[:, b * N:(b + 1) * N], t1[:, b * N:(b + 1) * N], start=True, stop=True)
            ins.then_inc(s["rd_psum"], 1)
            pe.wait_ge(s["rd_ready"], 1)
            for b in range(B):
                ins = mm(ps[:, 6, b * N:(b + 1) * N], t2[:, b * N:(b + 1) * N], w["wr_t"], start=True, stop=True)
            ins.then_inc(s["ro_psum"], 1)
            project_keys(3)
            transpose_rows(2, 4)
            pe.wait_ge(s["xnt_ready"], 3)
            for b in range(B):
                ins = mm(ps[:, 7, b * E0:(b + 1) * E0], xt(b), w["wgate_t"], start=True, stop=True)
            ins.then_inc(s["rl_psum"], 1)
            for b in range(B):
                ins = mm(ps[:, 4 + b, :], xt(b), w["wfc_t"], start=True, stop=True)
            ins.then_inc(s["h0_psum"], 1)
            project_values(0)
            project_values(1)
            pe.wait_ge(s["hw_ready"], 1)
            for b in range(B):
                for k in range(4):
                    at = b * 512 + k * 128
                    ins = tp(ps[:, 6 + b, k * 128:(k + 1) * 128], lg[:, 0, at:at + 128], ident)
                ins.then_inc(s["ht_psum"], 1)
            for b in range(B):
                pe.wait_ge(s["ht_ready"], b + 1)
                for k in range(4):
                    ins = mm(ps[:, 4, b * N:(b + 1) * N], hid_t[:, b, k, :], w["wproj_t"][:, k * 128:(k + 1) * 128],
                             start=(k == 0), stop=(k == 3))
            ins.then_inc(s["f0_psum"], 1)
            project_values(2)
            transpose_rows(3, 6)
            pe.wait_ge(s["xnt_ready"], 4)
            pe.wait_ge(s["third_in"], 16)
            mm(ps[:, 5, 0:256], w["wq1"], xt2, start=True, stop=True).then_inc(s["q1_psum"], 1)
            project_values(3)

            def spread_queries(g):
                rows = slice(32 * g, 32 * g + 32)
                for j in range(4):
                    for r in range(PARTS):
                        if g == 0 and j == 0:
                            pe.wait_ge(s["q_parts"], r + 1)
                        at = (PARTS - 1 - r) * PARTS * DH
                        ins = mm(ps[0:ROWS, 4 + g, j * N:(j + 1) * N], spread[rows, j, at:at + ROWS],
                                 q_split[rows, r, 0:N], start=(r == 0), stop=(r == PARTS - 1))
                ins.then_inc(s["qr_psum"], 1)

            def scores(i, half):
                b, h = i // HEADS, i % HEADS
                if half == 0:
                    pe.wait_ge(keys_in[i % RING], 16 * (i // RING + 1))
                    if i == 0:
                        pe.wait_ge(s["queries_ready"], 1)
                    if i == 4:
                        pe.wait_ge(s["queries_ready"], 2)
                    if i == HEADS // 2:
                        pe.wait_ge(s["queries_in0"], 16 * PARTS)
                    if i == HEADS:
                        pe.wait_ge(s["queries_in1"], 16 * PARTS)
                if i >= 1:
                    pe.wait_ge(s["scores_masked"], 2 * i + half - 1)
                for n in range(2):
                    at = half * HALF + n * 512
                    ins = mm(ps[:, 2 * half + n, :], queries[:, b, h, :], keys[:, i % RING, at:at + 512],
                             start=True, stop=True)
                ins.then_inc(s["scores_psum"], 1)

            def transpose_quarter(i, q):
                bank = (4, 5, 4, 7)[q]
                if q == 0:
                    pe.wait_ge(s["exp_ready"], i + 1)
                if bank == 4 and (i or q):
                    pe.wait_ge(s["pg_dve"], 2 * i + q // 2)
                elif bank != 4 and i:
                    pe.wait_ge(s["pt_copied"], 2 * (i - 1) + q // 2 + 1)
                for n in range(4):
                    c = 4 * q + n
                    ins = tp(ps[:, bank, n * 128:(n + 1) * 128], ring[i % 3][:, c * 128:(c + 1) * 128], ident)
                ins.then_inc(s["pt_psum"], 1)

            def weigh_values(i, n):
                b, h = i // HEADS, i % HEADS
                if n == 0 and i % HEADS == 0:
                    pe.wait_ge(s["v_ready"], 2 * b + 2)
                if n == 0 and i % 2 == 0 and i:
                    pe.wait_ge(s["heads_copied"], i // 2)
                for q in range(2 * n, 2 * n + 2):
                    pe.wait_ge(s["pg_pool" if q % 2 else "pg_dve"], 2 * i + q // 2 + 1)
                    for j in range(4):
                        c = 4 * q + j
                        ins = mm(ps[32 * j:32 * j + 32, 6, (h % 2) * 128:(h % 2 + 1) * 128],
                                 v[:, b, c, 32 * (h // 4):32 * (h // 4) + 32], pg[:, i % 2, c * 128:(c + 1) * 128],
                                 start=(q == 0), stop=(q == 3))
                if n:
                    ins.then_inc(s["pv_psum"], 1)

            def gather_heads(g):
                pe.wait_ge(s["heads_copied"], g + 1)
                for n in range(2):
                    i = 2 * g + n
                    ins = mm(ps[:, 6, 256 + i * DH:256 + (i + 1) * DH], heads_sb[:, n * 128:(n + 1) * 128],
                             w["select"][:, (i % 4) * DH:(i % 4 + 1) * DH], start=True, stop=True)
                ins.then_inc(s["heads_psum"], 1)

            pe.wait_ge(s["spread_ready"], 1)
            spread_queries(0)
            pe.wait_ge(s["v_copied"], 4)
            scores(0, 0)
            scores(0, 1)
            spread_queries(1)
            scores(1, 0)
            scores(1, 1)
            transpose_quarter(0, 0)
            pe.wait_ge(s["queries_ready"], 2)
            transpose_quarter(0, 1)
            scores(2, 0)
            transpose_quarter(0, 2)
            transpose_quarter(0, 3)
            scores(2, 1)
            scores(3, 0)
            scores(3, 1)
            for i in range(1, ITEMS):
                transpose_quarter(i, 0)
                transpose_quarter(i, 1)
                weigh_values(i - 1, 0)
                if i + 3 < ITEMS:
                    scores(i + 3, 0)
                transpose_quarter(i, 2)
                transpose_quarter(i, 3)
                weigh_values(i - 1, 1)
                if i + 3 < ITEMS:
                    scores(i + 3, 1)
                if i % 2 and i >= 3:
                    gather_heads((i - 3) // 2)
            for n in range(2):
                weigh_values(ITEMS - 1, n)
            gather_heads(ITEMS // 2 - 1)
            pe.wait_ge(s["se_ready"], 8)
            for k in range(8):
                ins = tp(ps[:, k // 4, (k % 4) * 128:(k % 4 + 1) * 128], se[:, k, :], ident)
            ins.then_inc(s["se_psum"], 1)
            pe.wait_ge(s["at_ready"], 1)
            for b in range(B):
                ins = tp(ps[:, 4, b * N:(b + 1) * N], t0[:, b * N:(b + 1) * N], ident)
            ins.then_inc(s["att_psum"], 1)
            pe.wait_ge(s["att_ready"], 1)
            for b in range(B):
                ins = mm(ps[:, 5, b * N:(b + 1) * N], t1[:, b * N:(b + 1) * N], w["wo1"], start=True, stop=True)
            ins.then_inc(s["wo_psum"], 1)
            keep_busy(F3, 2)
            transpose_rows(4, 8)
            pe.wait_ge(s["xnt_ready"], 5)
            mm(ps[:, 7, 0:256], w["wqkv_t"][:, 0:128], xt2, start=True, stop=True).then_inc(s["q2_psum"], 1)
            mm(ps[:, 5, 0:256], w["wqkv_t"][:, 128:256], xt2, start=True, stop=True).then_inc(s["k2_psum"], 1)
            pe.wait_ge(s["q2_ready"], 1)
            pe.wait_ge(s["k2_ready"], 1)
            for b in range(B):
                ins = mm(ps[:, 4, b * N:(b + 1) * N], t0[:, b * N:(b + 1) * N], t1[:, b * N:(b + 1) * N], start=True, stop=True)
            ins.then_inc(s["cs_psum"], 1)
            for b in range(B):
                ins = mm(ps[:, 3, b * N:(b + 1) * N], xt(b), w["wqkv_t"][:, 256:384], start=True, stop=True)
            ins.then_inc(s["v2_psum"], 1)
            keep_busy(F4, 2)
            for b in range(B):
                pe.wait_ge(s["cs_exp"], b + 1)
                ins = tp(ps[:, 5, b * N:(b + 1) * N], lg[:, 0, b * N:(b + 1) * N], ident)
            ins.then_inc(s["pst_psum"], 1)
            pe.wait_ge(s["pst_ready"], 1)
            pe.wait_ge(s["v2_ready"], 1)
            for b in range(B):
                ins = mm(ps[:, 6, b * N:(b + 1) * N], t1[:, b * N:(b + 1) * N], t2[:, b * N:(b + 1) * N], start=True, stop=True)
            ins.then_inc(s["ys_psum"], 1)
            keep_busy(F5, 2)
            transpose_rows(5, 10)
            pe.wait_ge(s["xft_ready"], 1)
            pe.wait_ge(s["set_ready"], 1)
            for k in range(8):
                ins = mm(ps[:, 4 + k // 2, (k % 2) * 256:(k % 2 + 1) * 256], se_t[:, k * 128:(k + 1) * 128], t0[:, :],
                         start=True, stop=True)
                if k % 2:
                    ins.then_inc(s["ls_psum"], 1)

            def combine_logits(b):
                for n in range(2):
                    ins = mm(ps[:, 2 * b + n, :], t0[:, b * N:(b + 1) * N], se_t[:, n * 512:(n + 1) * 512], start=True, stop=True)
                ins.then_inc(s["ln_psum"], 1)

            def transpose_dispatch(g):
                pe.wait_ge(s["dispatch_ready"], g + 1)
                for t in range(4):
                    ins = tp(ps[:, 4 + g, t * 128:(t + 1) * 128], dispatch_t[:, 4 * g + t, :], ident)
                ins.then_inc(s["dt_psum"], 1)

            def fill_slots(n):
                for b in range(B):
                    ins = mm(ps[:, 4 + 2 * n + b, :], xb[:, b, :], dispatch[:, b, n * 512:(n + 1) * 512], start=True, stop=True)
                ins.then_inc(s["sl_psum"], 1)

            def up_gate(e):
                if e >= 2:
                    pe.wait_ge(s["gate_ready"], 2 * (e - 1))
                for k in range(2):
                    ins = mm(ps[:, 4 + e % 2, k * 128:(k + 1) * 128], wg[:, e, k * 128:(k + 1) * 128], slots_t[:, e, :, :],
                             start=True, stop=True)
                ins.then_inc(s["g_psum"], 1)

            def up_linear(e):
                if e >= 2:
                    pe.wait_ge(s["hmid_ready"], 2 * (e - 1))
                for k in range(2):
                    ins = mm(ps[:, 6 + e % 2, k * 128:(k + 1) * 128], wu[:, e, k * 128:(k + 1) * 128], slots_t[:, e, :, :],
                             start=True, stop=True)
                ins.then_inc(s["u_psum"], 1)

            def up(e):
                up_gate(e)
                up_linear(e)

            def down(p):
                if p >= 2:
                    pe.wait_ge(s["eo_ready"], p - 1)
                pe.wait_ge(s["hmid_ready"], 4 * p + 4)
                for b in range(B):
                    for k in range(2):
                        for j in range(2):
                            e = 2 * p + j
                            ins = mm(ps[64 * j:64 * j + 64, 2 + p % 2, b * N:(b + 1) * N],
                                     hmid[:, e % 4, k, b * SLOTS:(b + 1) * SLOTS], wd[:, e, k, :], start=(k == 0), stop=(k == 1))
                ins.then_inc(s["eo_psum"], 1)

            def back(p):
                pe.wait_ge(s["eo_ready"], p + 1)
                for b in range(B):
                    ins = mm(ps[:, b, 0:128], combine_t[:, b, p, :], eo[:, p % 2, b, :], start=(p == 0), stop=(p == PAIRS - 1))
                ins.then_inc(s["y_psum"], 1)

            combine_logits(0)
            transpose_dispatch(0)
            transpose_dispatch(1)
            combine_logits(1)
            transpose_dispatch(2)
            pe.wait_ge(s["xf_ready"], 1)
            pe.wait_ge(s["dt_dve"], 2)
            fill_slots(0)
            transpose_dispatch(3)
            pe.wait_ge(s["dt_act"], 2)
            fill_slots(1)
            for name in ("wg_in", "wu_in", "wd_in"):
                pe.wait_ge(s[name], 32)
            pe.wait_ge(s["slots_ready"], 1)
            up_gate(0)
            up_gate(1)
            pe.wait_ge(s["slots_ready"], 2)
            up_linear(0)
            up_linear(1)
            pe.wait_ge(s["combine_exp"], 2)
            for b in range(B):
                for k in range(PAIRS):
                    ins = tp(ps[:, 2 * b + k // 4, (k % 4) * 128:(k % 4 + 1) * 128], combine[:, b, k, :], ident)
                ins.then_inc(s["ct_psum"], 1)
            up(2)
            pe.wait_ge(s["ct_dve"], 1)
            pe.wait_ge(s["ct_act"], 1)
            down(0)
            up(3)
            for p in range(1, PAIRS):
                if p + 1 < PAIRS:
                    up(2 * p + 2)
                down(p)
                back(p - 1)
                if p + 1 < PAIRS:
                    up(2 * p + 3)
            back(PAIRS - 1)


def kernel(**inputs):
    import numpy as np
    import concourse.bacc as bacc
    from concourse.bass_utils import run_bass_kernel_spmd as run

    i = {name: np.asarray(value) for name, value in inputs.items()}

    def rows(vector):
        return np.broadcast_to(vector.reshape(1, -1), (128, vector.size))

    def col(vector):
        return vector.reshape(128, 1)

    f = np.float32
    j, p = np.arange(N)[:, None], np.arange(N)[None, :]
    e, o = np.arange(E0)[:, None], np.arange(E0)[None, :]
    select = np.zeros((128, 4, DH), f)
    for n in range(4):
        for g in range(4):
            for d in range(DH):
                select[32 * g + DH * n + d, n, d] = 1
    qkv_b = i["L1_attn_b_qkv"]
    parts = {
        "ident": np.eye(128, dtype=f), "x": i["x"].transpose(1, 0, 2).reshape(N, B * D),
        "wq_t": i["L0_xattn_Wq"].T, "wk_t": i["L0_xattn_Wk"].T, "wv_t": i["L0_xattn_Wv"].T, "wo": i["L0_xattn_Wo"],
        "bo_rows": rows(i["L0_xattn_bo"]), "bq": col(i["L0_xattn_bq"]), "bk": col(i["L0_xattn_bk"]),
        "bv": col(i["L0_xattn_bv"]), "decay": rows(i["L0_attn_decay"]), "log_alpha": rows(i["L0_attn_log_alpha"]),
        "wk1": i["L1_xattn_wk_k"], "wk1_b": col(i["L1_xattn_wk_b"]), "wv1": i["L1_xattn_wv_k"],
        "wv1_b_rows": rows(i["L1_xattn_wv_b"]),
        "steps": np.maximum(p - 1 - j, 0).astype(f), "causal": (p > j).astype(f),
        "ww_t": i["L0_attn_W_write"].T, "wr_t": i["L0_attn_W_read"].T,
        "wgate_t": i["L0_ffn_w_gate"].T, "lower": rows((o < e).astype(f).reshape(-1)),
        "wfc_t": i["L0_ffn_w_fc"].reshape(E0 * I0, D).T,
        "wproj_t": i["L0_ffn_w_proj"].transpose(0, 2, 1).reshape(4, 128, D).transpose(1, 0, 2).reshape(128, 4 * D),
        "wq1": i["L1_xattn_wq_k"], "wo1": i["L1_xattn_wo_k"], "wo1_b_rows": rows(i["L1_xattn_wo_b"]),
        "wqkv_t": i["L1_attn_W_qkv"].T, "bv_rows": rows(qkv_b[256:384]),
        "future": np.where(p > j, f(CAUSAL), f(0)).astype(f), "select": select.reshape(128, 4 * DH),
        "norm_g_rows": rows(i["L1_ffn_norm_g"]), "norm_b_rows": rows(i["L1_ffn_norm_b"]),
        "bg": i["L1_ffn_bg"].reshape(2 * E1, 128).T, "bu": i["L1_ffn_bu"].reshape(2 * E1, 128).T,
        "wq1_b": col(i["L1_xattn_wq_b"]), "bq_self": col(qkv_b[0:128]), "bk_self": col(qkv_b[128:256]),
        "norm_g": col(i["L1_ffn_norm_g"]), "norm_b": col(i["L1_ffn_norm_b"]), "slot_g": col(i["L1_ffn_slot_g"]),
        "slot_b": col(i["L1_ffn_slot_b"]), "scale": rows(i["L1_ffn_scale"]),
    }
    c = i["ctx_1024"]
    arrays = {
        "start": np.concatenate([parts[n] for n, _ in START], axis=1),
        "first": np.concatenate([parts[n] for n, _ in FIRST], axis=1),
        "second": np.concatenate([parts[n] for n, _ in SECOND], axis=1),
        "third": np.concatenate([parts[n] for n, _ in THIRD], axis=1),
        "ctx_t": c.transpose(2, 0, 1), "ctx_r": c.reshape(B, C, 128, D).transpose(2, 0, 1, 3),
        "g_t": i["fside_BxSxS2_0"].reshape(B, N, C, 128).transpose(3, 0, 2, 1),
        "mask0": i["mask_1xSxS2_if1"][0], "mask1": i["mask_BxSxS2_ik1"].transpose(1, 0, 2),
        "slots": i["L1_ffn_slot_embeds"].reshape(8, 128, D).transpose(1, 0, 2),
        "wg": i["L1_ffn_Wg"].transpose(1, 0, 2), "wu": i["L1_ffn_Wu"].transpose(1, 0, 2),
        "wd": i["L1_ffn_Wd"].reshape(E1, 2, 128, D).transpose(2, 0, 1, 3),
        "bd": np.broadcast_to(i["L1_ffn_bd"].reshape(PAIRS, 2, 1, D).transpose(1, 2, 0, 3), (2, SLOTS, PAIRS, D))
              .reshape(128, PAIRS, D),
    }
    nc = bacc.Bacc("TRN2", target_bir_lowering=False, num_devices=1)
    feeds, aps = {}, {}
    for name, array in arrays.items():
        feeds[f"in_{name}"] = array = np.ascontiguousarray(array)
        aps[name] = nc.dram_tensor(f"in_{name}", array.shape, mybir.dt.from_np(array.dtype), kind="ExternalInput").ap()
    out = nc.dram_tensor("out_0", (B, N, D), F32, kind="ExternalOutput").ap()
    q_dram = nc.dram_tensor("q_dram", (PARTS, B, DH, HEADS, N), BF16, kind="Internal").ap()
    k_dram = nc.dram_tensor("k_dram", (B, HEADS, PARTS, DH, T), BF16, kind="Internal").ap()
    build(nc, aps, out, k_dram, q_dram)
    r = run(nc, [feeds], core_ids=[0])
    return r.results[0]["out_0"]
```

```python
from contextlib import ExitStack

import concourse.bass as bass
from concourse import mybir

ALU = mybir.AluOpType
ACT = mybir.ActivationFunctionType
AX_X = mybir.AxisListType.X
F32 = mybir.dt.float32
BF16 = mybir.dt.bfloat16
I32 = mybir.dt.int32

B, N, D, T = 2, 128, 128, 2048
C = T // 128
HALF = T // 2
HEADS, DH = 16, 8
PARTS = 3
ROWS = PARTS * PARTS * DH
E0, I0 = 8, 64
E1, SLOTS, F1 = 16, 64, 256
NS = E1 * SLOTS
PAIRS = E1 // 2
EPS = 1e-5
MASKED = 1e9
CAUSAL = 1e30
FAR = 3e38
ITEMS = B * HEADS
PAIRS_OF_HEADS = ITEMS // 2
BUSY = {"loads": 10, "transposed rows": 2, "first queries": 2, "first exponentials": 5,
        "self attention's rows": 8, "soft mixture's rows": 12}
QUARTER_BANKS = (4, 5, 4, 7)
LATE = ITEMS - 2
RING = 4
S0_SCALE = float(D) ** -0.5
S1_SCALE = float(DH) ** -0.5

START = (("ident", 128), ("x", B * D))
FIRST = (("wq_t", 128), ("wk_t", 128), ("wv_t", 128), ("wo", 128), ("bo_rows", 128),
         ("bq", 1), ("bk", 1), ("bv", 1), ("decay", 1), ("log_alpha", 1), ("wk1_b", 1))
SECOND = (("wk1", 128), ("wv1", 128), ("steps", 128), ("causal", 128), ("ww", 128), ("wr_t", 128),
          ("wgate_t", E0), ("lower", E0 * E0), ("wfc_t", E0 * I0), ("wproj_t", E0 * I0))
THIRD = (("wv1_b_rows", 128), ("wq1", 128), ("wo1", 128), ("wo1_b_rows", 128), ("wqkv_t", 384), ("bv_rows", 128), ("future", 128),
         ("select", 4 * DH), ("norm_g_rows", 128), ("norm_b_rows", 128), ("bg", 2 * E1), ("bu", 2 * E1),
         ("wq1_b", 1), ("bq_self", 1), ("bk_self", 1), ("norm_g", 1), ("norm_b", 1), ("slot_g", 1), ("slot_b", 1), ("scale", 1))

SIGNALS = """
start_in first_in second_in third_in ctxt_in0 ctxt_in1 ctxr_in mask0_in mask1_in0 mask1_in1 g_in0 g_in1 slots_in wg_in wu_in wd_in bd_in
ones_set dve_chain pool_chain spread_ready
var_ready rstd_ready xn_ready xnt_psum xnt_ready
fold_src fold_psum fold_ready qp_psum qp_ready row_psum
mask1_ready s0_psum s0_masked s0_args s0_exp pt0_psum pt0_ready o0_psum o0_ready y0_psum
kp_psum kp_copied k_parts k_saved0 k_saved1 keys_in0 keys_in1 keys_in2 keys_in3 vp_psum v_copied v_ready
decay_exp decay_one decay_log rw_psum rw_ready v0_psum v0_ready st_psum sm_ready ro_psum
h0_psum rl_psum logits_max router_exp gelu0_ready hw_ready ht_psum ht_dve ht_act f0_psum
q1_psum q_parts qr_psum queries_ready q_saved0 q_saved1 queries_in0 queries_in1
scores_psum scores_masked exp_ready pt_psum pt_copied pg_dve pg_pool pg_late pv_psum heads_copied heads_psum
at_ready att_psum att_ready wo_psum
q2_psum k2_psum v2_psum q2_ready k2_ready v2_ready gain_ready cs_psum cs_masked cs_exp pst_psum pst_ready ys_psum
se_var se_root se_shift se_ready se_psum set_ready xf_ready xft_ready
ln_psum ln_max combine_exp ls_psum ls_max dispatch_exp dispatch_ready dt_psum dt_dve dt_act ct_psum ct_dve ct_act
sl_psum slots_ready g_psum u_psum gate_ready hmid_ready eo_psum eo_ready y_psum out_ready out_saved
""".split()


def columns(packed, names):
    views, at = {}, 0
    for name, n in names:
        views[name] = packed[:, at:at + n]
        at += n
    return views


def build(nc, a, out, k_dram, q_dram):
    with ExitStack() as ctx:
        def sb(name, shape, dt=F32):
            return ctx.enter_context(nc.sbuf_tensor(name, shape, dt))

        s = {name: ctx.enter_context(nc.semaphore(name)) for name in SIGNALS}
        keys_in = [s[f"keys_in{i}"] for i in range(RING)]

        start = sb("start", [128, sum(n for _, n in START)])
        first = sb("first", [128, sum(n for _, n in FIRST)])
        second = sb("second", [128, T])
        third = sb("third", [128, sum(n for _, n in THIRD)])
        w = {**columns(start, START), **columns(first, FIRST), **columns(second, SECOND), **columns(third, THIRD)}
        ident = w["ident"]
        ones = sb("ones", [128, 128])
        minus_half = sb("minus_half", [128, 8])
        ctx_t = sb("ctx_t", [128, B, T])
        ctx_r = sb("ctx_r", [128, B, C, D])
        g_t = sb("g_t", [128, B, C, N])
        mask1 = sb("mask1", [128, B, T])
        k_parts = sb("k_parts", [128, PARTS, B, T], BF16)
        keys = sb("keys", [ROWS, RING, T], BF16)
        queries = sb("queries", [ROWS, B, HEADS, N], BF16)
        v = sb("v", [128, B, C, D])
        lg = sb("lg", [128, 2, T])
        pg = sb("pg", [128, 2, T])
        pc = sb("pc", [128, 2, 512])
        se_t = sb("se_t", [128, NS])
        ring = [lg[:, 0, :], lg[:, 1, :], second[:, :]]
        mask0 = g_t[:, 1].rearrange("p c n -> p (c n)")
        k_full = [pc[:, :, :].rearrange("p a n -> p (a n)"), v[:, 1, 0:8].rearrange("p c d -> p (c d)")]
        se = v[:, 1, 8:16]
        spread = sb("spread", [128, 4, 5 * PARTS * DH], BF16)
        wg = ctx_t[:, :, :].rearrange("p b t -> p (b t)").rearrange("p (e f) -> p e f", e=E1)
        wu = ctx_r[:, :, :, :].rearrange("p b c d -> p (b c d)").rearrange("p (e f) -> p e f", e=E1)
        kw = k_parts[:, :, :, :].rearrange("p a b t -> p (a b t)").bitcast(F32)
        wd = g_t[:, :, :, :].rearrange("p b c n -> p (b c n)").rearrange("p (e k o) -> p e k o", e=E1, k=2)
        bd = kw[:, 2 * T:2 * T + PAIRS * D].rearrange("p (k o) -> p k o", k=PAIRS)
        weights = [t.rearrange("p (c h n) -> p c h n", c=C, h=2)
                   for t in (pg[:, :, :].rearrange("p a t -> p (a t)"), kw[:, 0:2 * T])]

        x = [w["x"].rearrange("p (b d) -> p b d", b=B)] + [sb(f"x{i}", [128, B, D])[:, :, :] for i in range(1, 6)]
        xb = sb("xb", [128, B, D])
        xn = sb("xn", [128, B, D])
        xnt = sb("xnt", [128, B, N + 2])
        stats = sb("stats", [128, 8, 6])
        mv = sb("mv", [128, B, 2])
        ve = sb("ve", [128, B])
        rstd = sb("rstd", [128, B])
        se_mv = sb("se_mv", [128, 8, 2])
        se_ve = sb("se_ve", [128, 8])
        se_rstd = sb("se_rstd", [128, 8])
        se_shift = sb("se_shift", [128, 8])
        folds = sb("folds", [128, 388])
        wob = sb("wob", [128, 128])
        write_read = sb("write_read", [128, 128])
        t0 = sb("t0", [128, B * N])
        t1 = sb("t1", [128, B * N])
        t2 = sb("t2", [128, B * N])
        q_split = sb("q_split", [128, PARTS, B * N], BF16)
        heads_sb = sb("heads_sb", [128, 256])
        cols = sb("cols", [128, 96])
        m0 = cols[:, 0:4]
        flag, nflag, bias0, m0c, den0, rinv0 = (cols[:, 4 + 2 * i:6 + 2 * i] for i in range(6))
        rowc = cols[:, 16:18]
        bqbk = cols[:, 18:19]
        alpha, lgam, e1col = cols[:, 19:20], cols[:, 20:21], cols[:, 21:22]
        m2, den2, rinv2 = cols[:, 22:24], cols[:, 24:26], cols[:, 26:28]
        m_c, den_c, rinv_c = cols[:, 28:30], cols[:, 30:32], cols[:, 32:34]
        sg, sbias = cols[:, 34:35], cols[:, 35:36]
        scratch = cols[:, 78:79]
        mn = cols[:, 72:78]
        d_max, d_sum = cols[:, 40:56], cols[:, 56:72]
        den1 = sb("den1", [128, ITEMS])
        rinv1 = sb("rinv1", [128, ITEMS])
        router = sb("router", [128, 8, B * E0])
        versus = sb("versus", [128, 3, B * E0 * E0])

        ps = ctx.enter_context(nc.psum_tensor("ps", [128, 8, 512], F32))

        def wide(slot):
            return ps[:, 2 * slot:2 * slot + 2, :].rearrange("p a n -> p (a n)")

        combine = lg[:, 0, :].rearrange("p (b k n) -> p b k n", b=B, k=PAIRS)
        combine_t = lg[:, 1, :].rearrange("p (b k n) -> p b k n", b=B, k=PAIRS)
        dispatch_t = pg[:, 0, :].rearrange("p (k n) -> p k n", k=16)
        dispatch = pg[:, 1, :].rearrange("p (b n) -> p b n", b=B)
        slots_t = mask1[:, 0, :].rearrange("p (e b n) -> p e b n", e=E1, b=B)
        hmid = mask1[:, 1, 0:1024].rearrange("p (s k n) -> p s k n", s=4, k=2)
        eo = mask1[:, 1, 1024:1536].rearrange("p (s b n) -> p s b n", s=2, b=B)
        gate_h = mask1[:, 1, 1536:2048].rearrange("p (s k n) -> p s k n", s=2, k=2)
        hid = lg[:, 0, 0:1024]
        hid_t = lg[:, 1, 0:1024].rearrange("p (b k n) -> p b k n", b=B, k=4)

        def dispatch_group(g):
            return dispatch.rearrange("p b (k n) -> p k b n", n=128)[:, 2 * g:2 * g + 2]

        def bank_group(g):
            return ps[:, 4 + g, :].rearrange("p (k b n) -> p k b n", k=2, b=B)

        def xt(b):
            return xnt[:, b, 1:N + 1]

        xt2 = xnt[:, :, 1:N + 1]
        block = ctx.enter_context(nc.Block())

        @block.sync
        def _(sp):
            sp.dma_start(start[:, :], a["start"]).then_inc(s["start_in"], 16)
            sp.dma_start(first[:, :], a["first"]).then_inc(s["first_in"], 16)
            sp.dma_start(ctx_t[:, 0, :], a["ctx_t"][:, 0, :]).then_inc(s["ctxt_in0"], 16)
            sp.dma_start(mask0.bitcast(I32), a["mask0"]).then_inc(s["mask0_in"], 16)
            sp.dma_start(ctx_t[:, 1, :], a["ctx_t"][:, 1, :]).then_inc(s["ctxt_in1"], 16)
            sp.dma_start(second[:, 0:sum(n for _, n in SECOND)], a["second"]).then_inc(s["second_in"], 16)
            sp.dma_start(ctx_r[:, :, :, :], a["ctx_r"]).then_inc(s["ctxr_in"], 16)
            sp.dma_start(se, a["slots"]).then_inc(s["slots_in"], 16)
            sp.dma_start(third[:, :], a["third"]).then_inc(s["third_in"], 16)

            def load_mask(b):
                sp.dma_start(mask1[:, b, :].bitcast(I32), a["mask1"][:, b, :]).then_inc(s[f"mask1_in{b}"], 16)

            def load_group(b):
                sp.dma_start(g_t[:, b], a["g_t"][:, b]).then_inc(s[f"g_in{b}"], 16)

            def save_keys(b):
                sp.wait_ge(s["k_parts"], 2 * b + 2)
                for p in range(PARTS):
                    sp.dma_start(k_dram[b, :, p], k_parts[:, p, b, :]).then_inc(s[f"k_saved{b}"], 16)

            def load_keys(i):
                b, h = i // HEADS, i % HEADS
                if i >= RING:
                    sp.wait_ge(s["scores_psum"], 2 * (i - RING) + 2)
                sp.dma_start(keys[:, i % RING, :], k_dram[b, h].rearrange("p d t -> (p d) t").unsqueeze(0)
                             .to_broadcast([PARTS, PARTS * DH, T])).then_inc(keys_in[i % RING], 16)

            load_mask(0)
            load_group(0)
            load_mask(1)
            sp.wait_ge(s["s0_masked"], 4)
            load_group(1)
            save_keys(0)
            sp.wait_ge(s["k_saved0"], 16 * PARTS)
            for i in range(RING):
                load_keys(i)
            save_keys(1)
            def save_queries(b):
                for r in range(PARTS):
                    sp.dma_start(q_dram[r, b].rearrange("d h n -> h d n"), q_split[:, r, b * N:(b + 1) * N])\
                      .then_inc(s[f"q_saved{b}"], 16)

            def load_queries(b, heads, signal):
                sp.wait_ge(s[f"q_saved{b}"], 16 * PARTS)
                for r in range(PARTS):
                    sp.dma_start(queries[PARTS * DH * r:PARTS * DH * (r + 1), b, heads, :].rearrange("r h n -> r (h n)"),
                                 q_dram[r, b][:, heads].rearrange("d h n -> d (h n)").unsqueeze(0)
                                 .to_broadcast([PARTS, DH, (heads.stop - heads.start) * N])).then_inc(signal, 16)

            sp.wait_ge(s["q_parts"], PARTS)
            save_queries(0)
            load_queries(0, slice(HEADS // 2, HEADS), s["queries_in0"])
            save_queries(1)
            sp.wait_ge(s["k_saved1"], 16 * PARTS)
            sp.wait_ge(s["vp_psum"], 4)
            sp.wait_ge(s["o0_psum"], 2)
            half_e = [slice(0, E1 // 2), slice(E1 // 2, E1)]
            extra = [(wg[:, h], a["wg"][:, h], "wg_in") for h in half_e]
            extra += [(wu[:, h], a["wu"][:, h], "wu_in") for h in half_e]
            extra += [(bd, a["bd"], "bd_in"), (wd[:, half_e[0]], a["wd"][:, half_e[0]], "wd_in")]
            for i in range(RING, ITEMS):
                load_keys(i)
                if i == RING:
                    load_queries(1, slice(0, HEADS), s["queries_in1"])
                if i % 3 == 0 and i // 3 - 3 in range(len(extra)):
                    to, frm, signal = extra[i // 3 - 3]
                    if signal == "wd_in":
                        sp.wait_ge(s["pg_dve"], 2 * HEADS)
                        sp.wait_ge(s["pg_pool"], 2 * HEADS)
                    sp.dma_start(to, frm).then_inc(s[signal], 16)
            sp.wait_ge(s["pg_dve"], 2 * ITEMS)
            sp.wait_ge(s["pg_pool"], 2 * LATE)
            sp.wait_ge(s["pg_late"], 2 * (ITEMS - LATE))
            sp.dma_start(wd[:, half_e[1]], a["wd"][:, half_e[1]]).then_inc(s["wd_in"], 16)
            sp.wait_ge(s["out_ready"], 2)
            sp.dma_start(out.rearrange("b n d -> n b d"), x[4]).then_inc(s["out_saved"], 16)
            sp.wait_ge(s["out_saved"], 16)

        @block.gpsimd
        def _(pool):
            chain = [0]

            def link(ins):
                chain[0] += 1
                ins.then_inc(s["pool_chain"], 1)
                pool.wait_ge(s["pool_chain"], chain[0])

            def inverse_root(k):
                pool.wait_ge(s["var_ready"], k + 1)
                pool.tensor_tensor(rstd[:, :], ve[:, :], minus_half[:, 0:B], ALU.pow).then_inc(s["rstd_ready"], 1)

            link(pool.memset(minus_half[:, :], -0.5))
            pool.memset(ones[:, :], 1.0).then_inc(s["ones_set"], 1)
            pool.memset(xnt[:, :, 0:1], 0.0).then_inc(s["ones_set"], 1)
            link(pool.memset(spread[:, :, :], 0.0))
            inverse_root(0)

            def split(kb):
                b, half = kb // 2, kb % 2
                part = [k_parts[:, p, b, half * HALF:(half + 1) * HALF] for p in range(PARTS)]
                rest = k_full[kb % 2]
                pool.wait_ge(s["kp_copied"], kb + 1)
                link(pool.tensor_tensor(rest, rest, part[0], ALU.subtract))
                link(pool.tensor_scalar(part[1], rest, 1.0, 0.0, ALU.mult, ALU.add))
                pool.tensor_tensor(part[2], rest, part[1], ALU.subtract).then_inc(s["k_parts"], 1)

            def widen_mask(b):
                pool.wait_ge(s[f"mask1_in{b}"], 16)
                pool.tensor_scalar(mask1[:, b, :], mask1[:, b, :].bitcast(I32), -MASKED, MASKED, ALU.mult, ALU.add)\
                    .then_inc(s["mask1_ready"], 1)

            def bias_values(vb):
                b, half = vb // 2, vb % 2
                pool.wait_ge(s["v_copied"], vb + 1)
                rows = v[:, b, half * 8:half * 8 + 8, :]
                pool.tensor_tensor(rows, rows, w["wv1_b_rows"].unsqueeze(1).to_broadcast([128, 8, D]), ALU.add)\
                    .then_inc(s["v_ready"], 1)

            pool.wait_ge(s["third_in"], 16)
            pool.tensor_scalar(spread[:, :, 2 * PARTS * DH:3 * PARTS * DH].rearrange("q n (p d) -> q n p d", p=PARTS),
                               w["select"].rearrange("q (n d) -> q n d", n=4).unsqueeze(2)
                               .to_broadcast([128, 4, PARTS, DH]), 1.0, 0.0, ALU.mult, ALU.add).then_inc(s["spread_ready"], 1)
            split(0)
            pool.wait_ge(s["se_var"], 1)
            pool.tensor_tensor(se_rstd[:, :], se_ve[:, :], minus_half[:, :], ALU.pow).then_inc(s["se_root"], 1)
            inverse_root(1)
            split(1)
            inverse_root(2)
            split(2)
            split(3)
            inverse_root(3)
            widen_mask(0)
            bias_values(0)
            bias_values(1)
            bias_values(2)
            bias_values(3)
            widen_mask(1)
            for i in range(LATE):
                b = i // HEADS
                if i % HEADS == 0:
                    pool.wait_ge(s[f"g_in{b}"], 16)
                for n, q in enumerate((1, 3)):
                    pool.wait_ge(s["pt_copied"], 2 * i + n + 1)
                    if n == 0 and i == 2:
                        pool.wait_ge(s["k_saved1"], 16 * PARTS)
                    if n == 0 and i % 2 == 0 and i >= 4:
                        pool.wait_ge(s["pv_psum"], i // 2 - 1)
                    pool.tensor_tensor(weights[i // 2 % 2][:, 4 * q:4 * q + 4, i % 2, :],
                                       pc[:, n, :].rearrange("p (c n) -> p c n", c=4), g_t[:, b, 4 * q:4 * q + 4, :], ALU.mult)\
                        .then_inc(s["pg_pool"], 1)
            inverse_root(4)
            inverse_root(5)

        @block.scalar
        def _(act):
            act.wait_ge(s["first_in"], 16)
            act.activation(e1col, w["decay"], ACT.Exp, scale=-1.0).then_inc(s["decay_exp"], 1)
            act.wait_ge(s["decay_one"], 1)
            act.activation(lgam, e1col, ACT.Ln).then_inc(s["decay_log"], 1)
            act.activation(alpha, w["log_alpha"], ACT.Exp).then_inc(s["decay_exp"], 1)
            act.wait_ge(s["fold_psum"], 2)
            act.activation(folds[:, 128:384], ps[:, 7, 128:384], ACT.Copy).then_inc(s["fold_ready"], 1)
            for b in range(B):
                act.wait_ge(s["s0_args"], b + 1)
                act.activation(lg[:, b, :], lg[:, b, :], ACT.Exp, bias=bias0[:, b:b + 1], scale=nflag[:, b:b + 1],
                               accum_out=den0[:, b:b + 1]).then_inc(s["s0_exp"], 1)
            act.wait_ge(s["second_in"], 16)
            act.wait_ge(s["decay_one"], 2)
            act.activation(w["steps"], w["steps"], ACT.Exp, scale=lgam).then_inc(s["decay_log"], 1)
            def copy_keys(kb):
                b, half = kb // 2, kb % 2
                act.wait_ge(s["kp_psum"], kb + 1)
                if kb >= 2:
                    act.wait_ge(s["k_parts"], kb - 1)
                act.activation(k_full[kb % 2], wide(kb % 2), ACT.Identity, bias=w["wk1_b"])
                act.activation(k_parts[:, 0, b, half * HALF:(half + 1) * HALF], wide(kb % 2), ACT.Identity,
                               bias=w["wk1_b"]).then_inc(s["kp_copied"], 1)

            def copy_values(vb):
                b, half = vb // 2, vb % 2
                act.wait_ge(s["vp_psum"], vb + 1)
                if vb == 2:
                    act.wait_ge(s["k_parts"], 4)
                act.activation(v[:, b, half * 8:half * 8 + 8, :].rearrange("p c d -> p (c d)"), wide(vb % 2), ACT.Copy)\
                   .then_inc(s["v_copied"], 1)

            copy_keys(0)
            copy_keys(1)
            act.wait_ge(s["rw_psum"], 1)
            act.activation(write_read[:, :], ps[:, 5, 0:128], ACT.Copy).then_inc(s["rw_ready"], 1)
            act.wait_ge(s["v0_psum"], 1)
            act.activation(t0[:, :], ps[:, 7, 0:256], ACT.Copy).then_inc(s["v0_ready"], 1)
            act.wait_ge(s["se_shift"], 1)
            for t in range(8):
                ins = act.activation(se[:, t, :], se[:, t, :], ACT.Identity, scale=se_rstd[:, t:t + 1],
                                     bias=se_shift[:, t:t + 1])
            ins.then_inc(s["se_ready"], 1)
            copy_keys(2)
            act.wait_ge(s["se_psum"], 1)
            act.wait_ge(s["gain_ready"], 2)
            act.activation(se_t[:, :], wide(2), ACT.Identity, scale=sg, bias=sbias).then_inc(s["set_ready"], 1)
            act.wait_ge(s["logits_max"], 1)
            act.activation(router[:, 2, :], router[:, 1, :], ACT.Exp).then_inc(s["router_exp"], 1)
            act.wait_ge(s["h0_psum"], 1)
            act.activation(hid, ps[:, 4:6, :].rearrange("p a n -> p (a n)"), ACT.Gelu).then_inc(s["gelu0_ready"], 1)
            copy_keys(3)
            act.wait_ge(s["ht_psum"], 2)
            act.activation(lg[:, 1, 512:1024], ps[:, 7, :], ACT.Copy).then_inc(s["ht_act"], 1)
            copy_values(0)
            copy_values(1)
            copy_values(2)
            act.activation(scratch, alpha, ACT.Exp)
            copy_values(3)

            def copy_queries(g):
                act.wait_ge(s["qr_psum"], g + 1)
                act.activation(queries[:, 0, 4 * g:4 * g + 4, :], ps[0:ROWS, 4:8, g * N:(g + 1) * N], ACT.Copy).then_inc(s["queries_ready"], 1)

            copy_queries(0)
            copy_queries(1)
            def exponentials(i):
                act.wait_ge(s["scores_masked"], 2 * i + 2)
                act.activation(ring[i % 3], ring[i % 3], ACT.Exp, bias=mn[:, 2 * (i % 3) + 1:2 * (i % 3) + 2],
                               scale=-1.0, accum_out=den1[:, i:i + 1]).then_inc(s["exp_ready"], 1)

            def copy_quarter(i, n):
                act.wait_ge(s["pt_psum"], 4 * i + 2 * n + 2)
                if i > 0:
                    act.wait_ge(s["pg_pool"], 2 * (i - 1) + n + 1)
                act.activation(pc[:, n, :], ps[:, QUARTER_BANKS[2 * n + 1], :], ACT.Copy).then_inc(s["pt_copied"], 1)

            def copy_heads(g):
                act.wait_ge(s["pv_psum"], g + 1)
                if g:
                    act.wait_ge(s["heads_psum"], g)
                act.activation(heads_sb[:, :], ps[:, 0 if g == PAIRS_OF_HEADS - 1 else 6, 0:256], ACT.Copy)\
                   .then_inc(s["heads_copied"], 1)

            exponentials(0)
            for i in range(ITEMS):
                if i % 2 == 0 and i >= 4:
                    copy_heads(i // 2 - 2)
                if i + 1 < ITEMS:
                    exponentials(i + 1)
                if i < LATE:
                    copy_quarter(i, 0)
                    copy_quarter(i, 1)
            copy_heads(PAIRS_OF_HEADS - 2)
            copy_heads(PAIRS_OF_HEADS - 1)
            act.wait_ge(s["k2_psum"], 1)
            act.activation(t1[:, :], ps[:, 5, 0:256], ACT.Identity, bias=w["bk_self"]).then_inc(s["k2_ready"], 1)
            for b in range(B):
                act.wait_ge(s["cs_masked"], b + 1)
                act.activation(lg[:, 0, b * N:(b + 1) * N], lg[:, 0, b * N:(b + 1) * N], ACT.Exp, bias=m2[:, b:b + 1],
                               scale=-1.0, accum_out=den2[:, b:b + 1]).then_inc(s["cs_exp"], 1)
            for g in range(4):
                act.wait_ge(s["ls_max"], g + 1)
                for t in range(4 * g, 4 * g + 4):
                    ins = act.activation(dispatch_t[:, t, :], ps[:, 4 + g, (t % 4) * N:(t % 4 + 1) * N], ACT.Exp,
                                         bias=d_max[:, t:t + 1], accum_out=d_sum[:, t:t + 1])
                ins.then_inc(s["dispatch_exp"], 1)
            for g in (2, 3):
                act.wait_ge(s["dt_psum"], g + 1)
                act.activation(dispatch_group(g), bank_group(g), ACT.Copy).then_inc(s["dt_act"], 1)
            for b in range(B):
                act.wait_ge(s["ln_max"], b + 1)
                act.activation(combine[:, b, :, :], wide(b).rearrange("p (k n) -> p k n", k=PAIRS), ACT.Exp,
                               bias=m_c[:, b:b + 1], accum_out=den_c[:, b:b + 1]).then_inc(s["combine_exp"], 1)
            act.activation(scratch, alpha, ACT.Gelu)

            def gate(e):
                act.wait_ge(s["g_psum"], e + 1)
                if e >= 2:
                    act.wait_ge(s["hmid_ready"], 2 * (e - 1))
                for k in range(2):
                    act.activation(gate_h[:, e % 2, k, :], ps[:, 4 + e % 2, k * 128:(k + 1) * 128], ACT.Gelu,
                                   bias=w["bg"][:, 2 * e + k:2 * e + k + 1]).then_inc(s["gate_ready"], 1)

            gate(0)
            gate(1)
            act.wait_ge(s["ct_psum"], 2)
            act.activation(combine_t[:, 1], wide(1).rearrange("p (k n) -> p k n", k=PAIRS), ACT.Copy).then_inc(s["ct_act"], 1)
            for e in range(2, E1):
                gate(e)

        @block.vector
        def _(dve):
            chain = [0]

            def link(ins):
                chain[0] += 1
                ins.then_inc(s["dve_chain"], 1)
                dve.wait_ge(s["dve_chain"], chain[0])

            def step(ins):
                chain[0] += 1
                ins.then_inc(s["dve_chain"], 1)

            def normalise(xin, xout, k, between=None):
                for b in range(B):
                    step(dve.bn_stats(stats[:, b, :], xin[:, b, :]))
                dve.wait_ge(s["dve_chain"], chain[0])
                for b in range(B):
                    step(dve.bn_aggr(mv[:, b, :], stats[:, b, :]))
                dve.wait_ge(s["dve_chain"], chain[0])
                dve.tensor_scalar(ve[:, 0:B], mv[:, 0:B, 1:2].rearrange("p b o -> p (b o)"), EPS, None, ALU.add)\
                   .then_inc(s["var_ready"], 1)
                if between:
                    between()
                dve.wait_ge(s["rstd_ready"], k + 1)
                for b in range(B):
                    dve.tensor_scalar(xout[:, b, :], xin[:, b, :], mv[:, b, 0:1], rstd[:, b:b + 1],
                                      ALU.subtract, ALU.mult).then_inc(s["xn_ready"], 1)

            def keep_transpose(k):
                dve.wait_ge(s["xnt_psum"], k + 1)
                dve.tensor_copy(xt2, ps[:, 6, 0:256].rearrange("p (b n) -> p b n", b=B)).then_inc(s["xnt_ready"], 1)

            dve.wait_ge(s["start_in"], 16)

            def fold_sources():
                dve.wait_ge(s["first_in"], 16)
                dve.tensor_tensor(t2[:, 0:1], w["bq"], w["bk"], ALU.mult).then_inc(s["fold_src"], 1)
                dve.tensor_scalar(wob[:, :], w["wo"], w["bv"], None, ALU.mult).then_inc(s["fold_src"], 1)

            normalise(x[0], xn, 0, fold_sources)
            dve.wait_ge(s["fold_psum"], 1)
            dve.tensor_copy(folds[:, 384:387], ps[:, 7, 384:387]).then_inc(s["fold_ready"], 1)
            dve.tensor_copy(folds[:, 0:128], ps[:, 7, 0:128]).then_inc(s["fold_ready"], 1)
            dve.wait_ge(s["ones_set"], 2)
            keep_transpose(0)
            dve.wait_ge(s["decay_exp"], 1)
            dve.tensor_scalar(e1col, e1col, 1.0, None, ALU.add).then_inc(s["decay_one"], 1)
            dve.wait_ge(s["fold_ready"], 2)
            dve.wait_ge(s["qp_psum"], 1)
            dve.tensor_scalar(t0[:, :], ps[:, 4, 0:256], folds[:, 384:385], -S0_SCALE, ALU.add, ALU.mult)\
               .then_inc(s["qp_ready"], 1)
            dve.wait_ge(s["row_psum"], 1)
            link(dve.tensor_scalar(rowc, ps[:, 5, 0:2], folds[:, 386:387], -S0_SCALE, ALU.add, ALU.mult))
            dve.wait_ge(s["mask0_in"], 16)
            for half in range(2):
                row = mask0[:, half * HALF:(half + 1) * HALF]
                link(dve.tensor_scalar(row, row.bitcast(I32), 0, MASKED, ALU.is_equal, ALU.mult))
            for b in range(B):
                for half in range(2):
                    u = 2 * b + half
                    dve.wait_ge(s["s0_psum"], u + 1)
                    dve.tensor_tensor_reduce(lg[:, b, half * HALF:(half + 1) * HALF], wide(half),
                                             mask0[:, half * HALF:(half + 1) * HALF], 1.0,
                                             FAR if half == 0 else m0[:, u - 1:u], ALU.add, ALU.min, m0[:, u:u + 1])\
                       .then_inc(s["s0_masked"], 1)
                    dve.wait_ge(s["s0_masked"], u + 1)
                m, f, o = m0[:, u:u + 1], flag[:, b:b + 1], slice(b, b + 1)
                step(dve.tensor_tensor(m0c[:, o], m, rowc[:, o], ALU.add))
                step(dve.tensor_scalar(f, m, 0.5 * MASKED, None, ALU.is_lt))
                link(dve.tensor_scalar(nflag[:, o], m, 0.5 * MASKED, -1.0, ALU.is_lt, ALU.mult))
                dve.scalar_tensor_tensor(out=bias0[:, o], in0=m0c[:, o], scalar=rowc[:, o], in1=f,
                                         op0=ALU.subtract, op1=ALU.mult).then_inc(s["s0_args"], 1)
            dve.wait_ge(s["decay_log"], 1)
            dve.tensor_scalar(lgam, lgam, -1.0, None, ALU.mult).then_inc(s["decay_one"], 1)
            for b in range(B):
                for q in range(4):
                    t = 4 * b + q
                    dve.wait_ge(s["pt0_psum"], t + 1)
                    dve.tensor_copy(pg[:, b, q * 512:(q + 1) * 512], ps[:, 4 + t % 2, :]).then_inc(s["pt0_ready"], 1)
                link(dve.reciprocal(rinv0[:, b:b + 1], den0[:, b:b + 1]))

            def end_cross_attention(b):
                dve.wait_ge(s["y0_psum"], b + 1)
                link(dve.scalar_tensor_tensor(out=x[1][:, b, :], in0=ps[:, 7, b * N:(b + 1) * N],
                                              scalar=rinv0[:, b:b + 1], in1=xb[:, b, :], op0=ALU.mult, op1=ALU.add))

            for b in range(B):
                dve.wait_ge(s["o0_psum"], b + 1)
                dve.tensor_copy(t1[:, b * N:(b + 1) * N], ps[:, 6, b * N:(b + 1) * N]).then_inc(s["o0_ready"], 1)
                if b == 0:
                    dve.wait_ge(s["fold_ready"], 3)
                    link(dve.tensor_tensor(xb[:, :, :], x[0], w["bo_rows"].unsqueeze(1).to_broadcast([128, B, D]), ALU.add))
                    link(dve.tensor_tensor(xb[:, :, :], xb[:, :, :],
                                           folds[:, 256:384].unsqueeze(1).to_broadcast([128, B, D]), ALU.add))
                end_cross_attention(b)
                if b == 0:
                    dve.wait_ge(s["slots_in"], 16)
                    for t in range(8):
                        step(dve.bn_stats(stats[:, t, :], se[:, t, :]))
                    dve.wait_ge(s["dve_chain"], chain[0])
                    for t in range(8):
                        step(dve.bn_aggr(se_mv[:, t, :], stats[:, t, :]))
                    dve.wait_ge(s["dve_chain"], chain[0])
                    dve.tensor_scalar(se_ve[:, :], se_mv[:, :, 1:2].rearrange("p b o -> p (b o)"), EPS, None, ALU.add)\
                       .then_inc(s["se_var"], 1)
                    dve.wait_ge(s["third_in"], 16)
                    dve.tensor_tensor(sg, w["slot_g"], w["scale"], ALU.mult).then_inc(s["gain_ready"], 1)
                    dve.tensor_tensor(sbias, w["slot_b"], w["scale"], ALU.mult).then_inc(s["gain_ready"], 1)

            def zero_future():
                dve.wait_ge(s["decay_log"], 2)
                link(dve.tensor_tensor(w["steps"], w["steps"], w["causal"], ALU.mult))
                dve.wait_ge(s["se_root"], 1)
                dve.scalar_tensor_tensor(out=se_shift[:, :], in0=se_mv[:, :, 0:1].rearrange("p t o -> p (t o)"), scalar=-1.0,
                                         in1=se_rstd[:, :], op0=ALU.mult, op1=ALU.mult).then_inc(s["se_shift"], 1)

            normalise(x[1], xn, 1, zero_future)
            keep_transpose(1)

            dve.wait_ge(s["st_psum"], 1)
            dve.tensor_tensor(t1[:, :].rearrange("p (b n) -> p b n", b=B), ps[:, 4, 0:256].rearrange("p (b n) -> p b n", b=B),
                              w["steps"].unsqueeze(1).to_broadcast([128, B, N]), ALU.mult).then_inc(s["sm_ready"], 1)
            dve.wait_ge(s["ro_psum"], 1)
            link(dve.scalar_tensor_tensor(out=xb[:, :, :].rearrange("p b d -> p (b d)"), in0=ps[:, 6, 0:256], scalar=alpha,
                                          in1=xn[:, :, :].rearrange("p b d -> p (b d)"), op0=ALU.mult, op1=ALU.add))
            link(dve.tensor_tensor(x[2][:, :, :], x[1][:, :, :], xb[:, :, :], ALU.add))

            normalise(x[2], xn, 2)
            keep_transpose(2)
            l, shifted, ex, rank, wts, gates = (router[:, i, :] for i in (0, 1, 2, 3, 4, 5))
            pair, top = router[:, 6, 0:B], router[:, 7, 0:B]

            def by_batch(t):
                return t.rearrange("p (b e) -> p b e", b=B)

            def over_rest(t):
                return t.unsqueeze(2).to_broadcast([128, B, E0])

            dve.wait_ge(s["rl_psum"], 1)
            link(dve.tensor_copy(l, ps[:, 7, 0:16]))
            link(dve.tensor_reduce(top, by_batch(l), AX_X, ALU.max))
            dve.tensor_tensor(by_batch(shifted), by_batch(l), over_rest(top), ALU.subtract).then_inc(s["logits_max"], 1)
            me = by_batch(l).unsqueeze(3).to_broadcast([128, B, E0, E0])
            cube = [versus[:, i, :].rearrange("p (b e j) -> p b e j", b=B, e=E0) for i in range(3)]
            for b in range(B):
                other = by_batch(l)[:, b, :].unsqueeze(1).to_broadcast([128, E0, E0])
                step(dve.tensor_tensor(cube[1][:, b], other, me[:, b], ALU.is_equal))
                step(dve.tensor_tensor(cube[0][:, b], other, me[:, b], ALU.is_gt))
            dve.wait_ge(s["dve_chain"], chain[0])
            for b in range(B):
                step(dve.tensor_tensor(cube[1][:, b], cube[1][:, b], w["lower"].rearrange("p (e j) -> p e j", e=E0), ALU.mult))
            dve.wait_ge(s["dve_chain"], chain[0])
            link(dve.tensor_tensor(versus[:, 2, :], versus[:, 0, :], versus[:, 1, :], ALU.add))
            link(dve.tensor_reduce(rank, versus[:, 2, :].rearrange("p (e j) -> p e j", j=E0), AX_X, ALU.add))
            dve.wait_ge(s["router_exp"], 1)
            link(dve.scalar_tensor_tensor(out=wts, in0=rank, scalar=1.5, in1=ex, op0=ALU.is_lt, op1=ALU.mult))
            link(dve.tensor_reduce(pair, by_batch(wts), AX_X, ALU.add))
            link(dve.reciprocal(pair, pair))
            link(dve.tensor_tensor(by_batch(gates), by_batch(wts), over_rest(pair), ALU.mult))
            dve.wait_ge(s["gelu0_ready"], 1)
            for b in range(B):
                h = hid[:, b * 512:(b + 1) * 512].rearrange("p (g i) -> p g i", i=I0)
                dve.tensor_tensor(h, h, gates[:, b * E0:(b + 1) * E0].unsqueeze(2).to_broadcast([128, E0, I0]), ALU.mult)\
                   .then_inc(s["hw_ready"], 1)
            dve.wait_ge(s["ht_psum"], 1)
            dve.tensor_copy(lg[:, 1, 0:512], ps[:, 6, :]).then_inc(s["ht_dve"], 1)
            for b in range(B):
                dve.wait_ge(s["f0_psum"], b + 1)
                step(dve.tensor_tensor(x[3][:, b, :], ps[:, 4 + b, 0:128], x[2][:, b, :], ALU.add))
            dve.wait_ge(s["dve_chain"], chain[0])

            dve.wait_ge(s["third_in"], 16)

            normalise(x[3], xn, 3)
            keep_transpose(3)
            link(dve.tensor_tensor(xb[:, :, :], x[3][:, :, :], w["wo1_b_rows"].unsqueeze(1).to_broadcast([128, B, D]), ALU.add))
            dve.wait_ge(s["q1_psum"], 1)
            link(dve.tensor_scalar(t0[:, :], ps[:, 5, 0:256], w["wq1_b"], -S1_SCALE, ALU.add, ALU.mult))
            for p in range(PARTS - 1):
                dve.tensor_copy(q_split[:, p, :], t0[:, :]).then_inc(s["q_parts"], 1)
                dve.wait_ge(s["q_parts"], p + 1)
                if p == 0:
                    link(dve.tensor_tensor(t0[:, :], t0[:, :], q_split[:, p, :], ALU.subtract))
            dve.tensor_tensor(q_split[:, 2, :], t0[:, :], q_split[:, 1, :], ALU.subtract).then_inc(s["q_parts"], 1)

            def mask_scores(i, half):
                b, slot = i // HEADS, 2 * (i % 3) + half
                if i % HEADS == 0:
                    dve.wait_ge(s["mask1_ready"], b + 1)
                dve.wait_ge(s["scores_psum"], 2 * i + half + 1)
                if half == 0 and i >= 3:
                    dve.wait_ge(s["pt_psum"], 4 * (i - 2))
                if half:
                    dve.wait_ge(s["scores_masked"], 2 * i + 1)
                dve.tensor_tensor_reduce(ring[i % 3][:, half * HALF:(half + 1) * HALF], wide(half),
                                         mask1[:, b, half * HALF:(half + 1) * HALF], 1.0,
                                         mn[:, slot - 1:slot] if half else FAR, ALU.add, ALU.min, mn[:, slot:slot + 1])\
                   .then_inc(s["scores_masked"], 1)

            def by_group(i, q):
                if i % HEADS == 0:
                    dve.wait_ge(s[f"g_in{i // HEADS}"], 16)
                dve.wait_ge(s["pt_psum"], 4 * i + q + 1)
                if q == 0 and i == 2:
                    dve.wait_ge(s["k_saved1"], 16 * PARTS)
                if q == 0 and i % 2 == 0 and i >= 4:
                    dve.wait_ge(s["pv_psum"], i // 2 - 1)
                dve.tensor_tensor(weights[i // 2 % 2][:, 4 * q:4 * q + 4, i % 2, :],
                                  ps[:, QUARTER_BANKS[q], :].rearrange("p (c n) -> p c n", c=4),
                                  g_t[:, i // HEADS, 4 * q:4 * q + 4, :], ALU.mult)\
                   .then_inc(s["pg_late" if q % 2 else "pg_dve"], 1)

            mask_scores(0, 0)
            mask_scores(0, 1)
            mask_scores(1, 0)
            mask_scores(1, 1)
            for n in range(2):
                by_group(0, 2 * n)
                mask_scores(2, n)
            for i in range(1, ITEMS):
                for n in range(2):
                    if i + 2 < ITEMS:
                        mask_scores(i + 2, n)
                    by_group(i, 2 * n)
                    if i >= LATE:
                        by_group(i, 2 * n + 1)
            dve.wait_ge(s["exp_ready"], ITEMS)
            link(dve.reciprocal(rinv1[:, :], den1[:, :]))
            dve.wait_ge(s["heads_psum"], PAIRS_OF_HEADS)
            dve.tensor_tensor(t0[:, :].rearrange("p (i d) -> p i d", d=DH), ps[:, 6, 256:512].rearrange("p (i d) -> p i d", d=DH),
                              rinv1[:, :].unsqueeze(2).to_broadcast([128, ITEMS, DH]), ALU.mult).then_inc(s["at_ready"], 1)
            dve.wait_ge(s["att_psum"], 1)
            dve.tensor_copy(t1[:, :], ps[:, 4, 0:256]).then_inc(s["att_ready"], 1)
            dve.wait_ge(s["wo_psum"], 1)
            link(dve.tensor_tensor(x[4][:, :, :].rearrange("p b d -> p (b d)"), ps[:, 5, 0:256],
                                   xb[:, :, :].rearrange("p b d -> p (b d)"), ALU.add))

            normalise(x[4], xn, 4)
            keep_transpose(4)
            dve.wait_ge(s["q2_psum"], 1)
            dve.tensor_scalar(t0[:, :], ps[:, 7, 0:256], w["bq_self"], -S0_SCALE, ALU.add, ALU.mult).then_inc(s["q2_ready"], 1)
            dve.wait_ge(s["cs_psum"], 1)
            for b in range(B):
                dve.tensor_tensor_reduce(lg[:, 0, b * N:(b + 1) * N], ps[:, 4, b * N:(b + 1) * N], w["future"], 1.0, FAR,
                                         ALU.add, ALU.min, m2[:, b:b + 1]).then_inc(s["cs_masked"], 1)
            dve.wait_ge(s["v2_psum"], 1)
            dve.tensor_tensor(t2[:, :].rearrange("p (b n) -> p b n", b=B), ps[:, 3, 0:256].rearrange("p (b n) -> p b n", b=B),
                              w["bv_rows"].unsqueeze(1).to_broadcast([128, B, D]), ALU.add).then_inc(s["v2_ready"], 1)
            dve.wait_ge(s["pst_psum"], 1)
            dve.tensor_copy(t1[:, :], ps[:, 5, 0:256]).then_inc(s["pst_ready"], 1)
            link(dve.reciprocal(rinv2, den2))
            dve.wait_ge(s["ys_psum"], 1)
            for b in range(B):
                link(dve.scalar_tensor_tensor(out=x[5][:, b, :], in0=ps[:, 6, b * N:(b + 1) * N], scalar=rinv2[:, b:b + 1],
                                              in1=x[4][:, b, :], op0=ALU.mult, op1=ALU.add))

            normalise(x[5], xn, 5)
            dve.wait_ge(s["xnt_psum"], 6)
            dve.tensor_scalar(t0[:, :], ps[:, 6, 0:256], w["norm_g"], w["norm_b"], ALU.mult, ALU.add).then_inc(s["xft_ready"], 1)
            link(dve.tensor_tensor(xb[:, :, :], xn[:, :, :], w["norm_g_rows"].unsqueeze(1).to_broadcast([128, B, D]), ALU.mult))
            dve.tensor_tensor(xb[:, :, :], xb[:, :, :], w["norm_b_rows"].unsqueeze(1).to_broadcast([128, B, D]), ALU.add)\
               .then_inc(s["xf_ready"], 1)
            for g in range(4):
                dve.wait_ge(s["ls_psum"], g + 1)
                dve.tensor_reduce(d_max[:, 4 * g:4 * g + 4], ps[:, 4 + g, :].rearrange("p (t n) -> p t n", n=N), AX_X, ALU.max,
                                  negate=True).then_inc(s["ls_max"], 1)
            def scale_dispatch(g):
                dve.wait_ge(s["dispatch_exp"], g + 1)
                group = slice(4 * g, 4 * g + 4)
                link(dve.reciprocal(d_sum[:, group], d_sum[:, group]))
                dve.tensor_tensor(dispatch_t[:, group, :], dispatch_t[:, group, :],
                                  d_sum[:, group].unsqueeze(2).to_broadcast([128, 4, N]), ALU.mult)\
                   .then_inc(s["dispatch_ready"], 1)

            def keep_dispatch(g):
                dve.wait_ge(s["dt_psum"], g + 1)
                dve.tensor_copy(dispatch_group(g), bank_group(g)).then_inc(s["dt_dve"], 1)

            def combine_maximum(b):
                dve.wait_ge(s["ln_psum"], b + 1)
                dve.tensor_reduce(m_c[:, b:b + 1], wide(b), AX_X, ALU.max, negate=True).then_inc(s["ln_max"], 1)

            scale_dispatch(0)
            scale_dispatch(1)
            keep_dispatch(0)
            scale_dispatch(2)
            keep_dispatch(1)
            scale_dispatch(3)
            combine_maximum(0)
            combine_maximum(1)
            for n in range(2):
                dve.wait_ge(s["sl_psum"], n + 1)
                dve.tensor_copy(slots_t[:, n * PAIRS:(n + 1) * PAIRS, :, :].rearrange("p e b n -> p b e n"),
                                wide(2 + n).rearrange("p (b e n) -> p b e n", b=B, e=PAIRS)).then_inc(s["slots_ready"], 1)
            dve.wait_ge(s["combine_exp"], 2)
            link(dve.reciprocal(rinv_c, den_c))
            dve.wait_ge(s["bd_in"], 16)

            def by_gate(e):
                dve.wait_ge(s["u_psum"], e + 1)
                if e >= 4:
                    dve.wait_ge(s["eo_psum"], e // 2 - 1)
                for k in range(2):
                    dve.wait_ge(s["gate_ready"], 2 * e + k + 1)
                    dve.scalar_tensor_tensor(out=hmid[:, e % 4, k, :], in0=ps[:, 6 + e % 2, k * 128:(k + 1) * 128],
                                             scalar=w["bu"][:, 2 * e + k:2 * e + k + 1], in1=gate_h[:, e % 2, k, :],
                                             op0=ALU.add, op1=ALU.mult).then_inc(s["hmid_ready"], 1)

            def add_down_bias(p):
                dve.wait_ge(s["eo_psum"], p + 1)
                if p >= 2:
                    dve.wait_ge(s["y_psum"], p - 1)
                dve.tensor_tensor(eo[:, p % 2], ps[:, 2 + p % 2, 0:256].rearrange("p (b n) -> p b n", b=B),
                                  bd[:, p, :].unsqueeze(1).to_broadcast([128, B, D]), ALU.add).then_inc(s["eo_ready"], 1)

            dve.wait_ge(s["ct_psum"], 1)
            dve.tensor_copy(combine_t[:, 0], wide(0).rearrange("p (k n) -> p k n", k=PAIRS)).then_inc(s["ct_dve"], 1)
            by_gate(0)
            by_gate(1)
            for p in range(1, PAIRS):
                by_gate(2 * p)
                add_down_bias(p - 1)
                by_gate(2 * p + 1)
            add_down_bias(PAIRS - 1)
            dve.wait_ge(s["y_psum"], PAIRS)
            for b in range(B):
                dve.scalar_tensor_tensor(out=x[4][:, b, :], in0=ps[:, b, 0:128], scalar=rinv_c[:, b:b + 1],
                                         in1=x[5][:, b, :], op0=ALU.mult, op1=ALU.add).then_inc(s["out_ready"], 1)

        @block.tensor
        def _(pe):
            mm, tp = pe.matmul, pe.transpose

            def transpose_rows(k, ready, src=xn):
                for b in range(B):
                    pe.wait_ge(s["xn_ready"], ready + b + 1)
                    ins = tp(ps[:, 6, b * N:(b + 1) * N], src[:, b, :], ident)
                ins.then_inc(s["xnt_psum"], 1)

            def keep_busy(beside, bank):
                for _ in range(BUSY[beside]):
                    mm(ps[:, bank, 0:128], ones[:, :], ones[:, :], start=True, stop=True)

            pe.wait_ge(s["ones_set"], 1)
            keep_busy("loads", 0)
            pe.wait_ge(s["first_in"], 16)
            mm(ps[:, 7, 0:128], w["wq_t"], w["wk_t"], start=True, stop=True)
            mm(ps[:, 7, 384:385], w["wk_t"], w["bq"], start=True, stop=True)
            mm(ps[:, 7, 385:386], w["wq_t"], w["bk"], start=True, stop=True)
            pe.wait_ge(s["fold_src"], 2)
            mm(ps[:, 7, 386:387], ones[:, :], t2[:, 0:1], start=True, stop=True).then_inc(s["fold_psum"], 1)
            transpose_rows(0, 0)
            keep_busy("transposed rows", 0)
            pe.wait_ge(s["fold_ready"], 2)
            pe.wait_ge(s["xnt_ready"], 1)
            mm(ps[:, 4, 0:256], folds[:, 0:128], xt2, start=True, stop=True).then_inc(s["qp_psum"], 1)
            for b in range(B):
                ins = mm(ps[:, 5, b:b + 1], xt(b), folds[:, 385:386], start=True, stop=True)
            ins.then_inc(s["row_psum"], 1)
            keep_busy("first queries", 0)
            pe.wait_ge(s["qp_ready"], 1)
            for b in range(B):
                pe.wait_ge(s[f"ctxt_in{b}"], 16)
                for half in range(2):
                    if b:
                        pe.wait_ge(s["s0_masked"], half + 1)
                    for n in range(2):
                        ins = mm(ps[:, 2 * half + n, :], t0[:, b * N:(b + 1) * N],
                                 ctx_t[:, b, half * HALF + n * 512:half * HALF + (n + 1) * 512], start=True, stop=True)
                    ins.then_inc(s["s0_psum"], 1)
                if b == 0:
                    mm(ps[:, 7, 128:256], w["wv_t"], w["wo"], start=True, stop=True)
                    mm(ps[:, 7, 256:384], ones[:, :], wob[:, :], start=True, stop=True).then_inc(s["fold_psum"], 1)

            def project_keys(kb):
                b, half = kb // 2, kb % 2
                if kb < 2:
                    pe.wait_ge(s["s0_masked"], 3 + kb)
                else:
                    pe.wait_ge(s["kp_copied"], kb - 1)
                for n in range(2):
                    ins = mm(ps[:, 2 * half + n, :], w["wk1"],
                             ctx_t[:, b, half * HALF + n * 512:half * HALF + (n + 1) * 512], start=True, stop=True)
                ins.then_inc(s["kp_psum"], 1)

            def project_values(vb):
                b, half = vb // 2, vb % 2
                if vb < 2:
                    pe.wait_ge(s["kp_copied"], 3 + vb)
                else:
                    pe.wait_ge(s["v_copied"], vb - 1)
                for c in range(8):
                    t = (half * 8 + c) * 128
                    ins = mm(ps[:, 2 * half + c // 4, (c % 4) * 128:(c % 4 + 1) * 128], ctx_t[:, b, t:t + 128], w["wv1"],
                             start=True, stop=True)
                ins.then_inc(s["vp_psum"], 1)

            def transpose_first(b, q):
                t = 4 * b + q
                if q == 0:
                    pe.wait_ge(s["s0_exp"], b + 1)
                if t >= 2:
                    pe.wait_ge(s["pt0_ready"], t - 1)
                for n in range(4):
                    c = 4 * q + n
                    ins = tp(ps[:, 4 + t % 2, n * 128:(n + 1) * 128], lg[:, b, c * 128:(c + 1) * 128], ident)
                ins.then_inc(s["pt0_psum"], 1)

            def weigh_context(b, q):
                if b and q == 0:
                    pe.wait_ge(s["o0_ready"], 1)
                pe.wait_ge(s["pt0_ready"], 4 * b + q + 1)
                for c in range(4 * q, 4 * q + 4):
                    ins = mm(ps[:, 6, b * N:(b + 1) * N], ctx_r[:, b, c, :], pg[:, b, c * 128:(c + 1) * 128],
                             start=(c == 0), stop=(c == C - 1))
                if q == 3:
                    ins.then_inc(s["o0_psum"], 1)

            def project_context(b):
                pe.wait_ge(s["o0_ready"], b + 1)
                pe.wait_ge(s["fold_ready"], 3)
                mm(ps[:, 7, b * N:(b + 1) * N], t1[:, b * N:(b + 1) * N], folds[:, 128:256], start=True, stop=True)\
                    .then_inc(s["y0_psum"], 1)

            transpose_first(0, 0)
            transpose_first(0, 1)
            pe.wait_ge(s["second_in"], 16)
            project_keys(0)
            transpose_first(0, 2)
            transpose_first(0, 3)
            pe.wait_ge(s["ctxr_in"], 16)
            for q in range(4):
                weigh_context(0, q)
                transpose_first(1, q)
            project_context(0)
            for q in range(4):
                weigh_context(1, q)
            project_keys(1)
            project_context(1)
            mm(ps[:, 5, 0:128], w["ww"], w["wr_t"], start=True, stop=True).then_inc(s["rw_psum"], 1)
            project_keys(2)
            transpose_rows(1, 2)
            pe.wait_ge(s["xnt_ready"], 2)
            pe.wait_ge(s["rw_ready"], 1)
            for b in range(B):
                ins = mm(ps[:, 7, b * N:(b + 1) * N], xt(b), write_read[:, :], start=True, stop=True)
            ins.then_inc(s["v0_psum"], 1)
            for b in range(B):
                ins = mm(ps[:, 4, b * N:(b + 1) * N], xnt[:, b, 0:N], xt(b), start=True, stop=True)
            ins.then_inc(s["st_psum"], 1)
            pe.wait_ge(s["v0_ready"], 1)
            pe.wait_ge(s["sm_ready"], 1)
            for b in range(B):
                ins = mm(ps[:, 6, b * N:(b + 1) * N], t1[:, b * N:(b + 1) * N], t0[:, b * N:(b + 1) * N], start=True, stop=True)
            ins.then_inc(s["ro_psum"], 1)
            project_keys(3)
            pe.wait_ge(s["se_ready"], 1)
            for k in range(8):
                ins = tp(ps[:, 4 + k // 4, (k % 4) * 128:(k % 4 + 1) * 128], se[:, k, :], ident)
            ins.then_inc(s["se_psum"], 1)
            transpose_rows(2, 4)
            pe.wait_ge(s["xnt_ready"], 3)
            for b in range(B):
                ins = mm(ps[:, 7, b * E0:(b + 1) * E0], xt(b), w["wgate_t"], start=True, stop=True)
            ins.then_inc(s["rl_psum"], 1)
            pe.wait_ge(s["set_ready"], 1)
            for b in range(B):
                ins = mm(ps[:, 4 + b, :], xt(b), w["wfc_t"], start=True, stop=True)
            ins.then_inc(s["h0_psum"], 1)
            project_values(0)
            for b in range(B):
                pe.wait_ge(s["hw_ready"], b + 1)
                for k in range(4):
                    at = b * 512 + k * 128
                    ins = tp(ps[:, 6 + b, k * 128:(k + 1) * 128], lg[:, 0, at:at + 128], ident)
                ins.then_inc(s["ht_psum"], 1)
            for b in range(B):
                pe.wait_ge(s["ht_act" if b else "ht_dve"], 1)
                for k in range(4):
                    ins = mm(ps[:, 4 + b, 0:N], hid_t[:, b, k, :], w["wproj_t"][:, k * 128:(k + 1) * 128],
                             start=(k == 0), stop=(k == 3))
                ins.then_inc(s["f0_psum"], 1)
            project_values(1)
            project_values(2)
            transpose_rows(3, 6)
            pe.wait_ge(s["xnt_ready"], 4)
            pe.wait_ge(s["third_in"], 16)
            mm(ps[:, 5, 0:256], w["wq1"], xt2, start=True, stop=True).then_inc(s["q1_psum"], 1)
            project_values(3)

            def spread_queries(g):
                rows = slice(32 * g, 32 * g + 32)
                for r in range(PARTS):
                    if g == 0:
                        pe.wait_ge(s["q_parts"], r + 1)
                    at = (PARTS - 1 - r) * PARTS * DH
                    for j in range(4):
                        ins = mm(ps[0:ROWS, 4 + j, g * N:(g + 1) * N], spread[rows, j, at:at + ROWS],
                                 q_split[rows, r, 0:N], start=(r == 0), stop=(r == PARTS - 1))
                ins.then_inc(s["qr_psum"], 1)

            def scores(i, half):
                b, h = i // HEADS, i % HEADS
                if half == 0:
                    pe.wait_ge(keys_in[i % RING], 16 * (i // RING + 1))
                    if i == 0:
                        pe.wait_ge(s["queries_ready"], 1)
                    if i == 4:
                        pe.wait_ge(s["queries_ready"], 2)
                    if i == HEADS // 2:
                        pe.wait_ge(s["queries_in0"], 16 * PARTS)
                    if i == HEADS:
                        pe.wait_ge(s["queries_in1"], 16 * PARTS)
                if i >= 1:
                    pe.wait_ge(s["scores_masked"], 2 * i + half - 1)
                for n in range(2):
                    at = half * HALF + n * 512
                    ins = mm(ps[:, 2 * half + n, :], queries[:, b, h, :], keys[:, i % RING, at:at + 512],
                             start=True, stop=True)
                ins.then_inc(s["scores_psum"], 1)

            def transpose_quarter(i, q):
                bank = QUARTER_BANKS[q]
                if q == 0:
                    pe.wait_ge(s["exp_ready"], i + 1)
                if bank == 4 and (i or q):
                    pe.wait_ge(s["pg_dve"], 2 * i + q // 2)
                elif bank != 4 and i > LATE:
                    pe.wait_ge(s["pg_late"], 2 * (i - 1 - LATE) + q // 2 + 1)
                elif bank != 4 and i:
                    pe.wait_ge(s["pt_copied"], 2 * (i - 1) + q // 2 + 1)
                for n in range(4):
                    c = 4 * q + n
                    ins = tp(ps[:, bank, n * 128:(n + 1) * 128], ring[i % 3][:, c * 128:(c + 1) * 128], ident)
                ins.then_inc(s["pt_psum"], 1)

            def weigh_values(g, q):
                i = 2 * g
                b, h = i // HEADS, i % HEADS
                if q == 0 and h == 0:
                    pe.wait_ge(s["v_ready"], 2 * b + 2)
                last = g == PAIRS_OF_HEADS - 1
                if q == 0 and g and not last:
                    pe.wait_ge(s["heads_copied"], g)
                if q % 2 == 0:
                    pe.wait_ge(s["pg_dve"], 2 * (i + 1) + q // 2 + 1)
                elif i < LATE:
                    pe.wait_ge(s["pg_pool"], 2 * (i + 1) + q // 2 + 1)
                else:
                    pe.wait_ge(s["pg_late"], 2 * (i + 1 - LATE) + q // 2 + 1)
                for j in range(4):
                    c = 4 * q + j
                    ins = mm(ps[32 * j:32 * j + 32, 0 if last else 6, 0:256], v[:, b, c, 32 * (h // 4):32 * (h // 4) + 32],
                             weights[g % 2][:, c, :, :].rearrange("p h n -> p (h n)"), start=(q == 0), stop=(q == 3))
                if q == 3:
                    ins.then_inc(s["pv_psum"], 1)

            def gather_heads(g):
                pe.wait_ge(s["heads_copied"], g + 1)
                for n in range(2):
                    i = 2 * g + n
                    ins = mm(ps[:, 6, 256 + i * DH:256 + (i + 1) * DH], heads_sb[:, n * 128:(n + 1) * 128],
                             w["select"][:, (i % 4) * DH:(i % 4 + 1) * DH], start=True, stop=True)
                ins.then_inc(s["heads_psum"], 1)

            pe.wait_ge(s["spread_ready"], 1)
            spread_queries(0)
            pe.wait_ge(s["v_copied"], 4)
            scores(0, 0)
            scores(0, 1)
            spread_queries(1)
            scores(1, 0)
            scores(1, 1)
            pe.wait_ge(s["queries_ready"], 2)
            keep_busy("first exponentials", 6)
            transpose_quarter(0, 0)
            transpose_quarter(0, 1)
            scores(2, 0)
            transpose_quarter(0, 2)
            transpose_quarter(0, 3)
            scores(2, 1)
            scores(3, 0)
            for i in range(1, ITEMS):
                transpose_quarter(i, 0)
                transpose_quarter(i, 1)
                if i % 2 == 0 and i >= 4:
                    gather_heads(i // 2 - 2)
                if i == 1:
                    scores(3, 1)
                if i >= 2:
                    weigh_values(i // 2 - 1, 2 * (i % 2))
                if i + 3 < ITEMS:
                    scores(i + 3, 0)
                transpose_quarter(i, 2)
                transpose_quarter(i, 3)
                if i >= 2:
                    weigh_values(i // 2 - 1, 2 * (i % 2) + 1)
                if i + 3 < ITEMS:
                    scores(i + 3, 1)
            for q in range(4):
                weigh_values(PAIRS_OF_HEADS - 1, q)
                if q == 1:
                    gather_heads(PAIRS_OF_HEADS - 2)
            gather_heads(PAIRS_OF_HEADS - 1)
            pe.wait_ge(s["at_ready"], 1)
            for b in range(B):
                ins = tp(ps[:, 4, b * N:(b + 1) * N], t0[:, b * N:(b + 1) * N], ident)
            ins.then_inc(s["att_psum"], 1)
            pe.wait_ge(s["att_ready"], 1)
            for b in range(B):
                ins = mm(ps[:, 5, b * N:(b + 1) * N], t1[:, b * N:(b + 1) * N], w["wo1"], start=True, stop=True)
            ins.then_inc(s["wo_psum"], 1)
            keep_busy("self attention's rows", 2)
            transpose_rows(4, 8)
            pe.wait_ge(s["xnt_ready"], 5)
            mm(ps[:, 7, 0:256], w["wqkv_t"][:, 0:128], xt2, start=True, stop=True).then_inc(s["q2_psum"], 1)
            mm(ps[:, 5, 0:256], w["wqkv_t"][:, 128:256], xt2, start=True, stop=True).then_inc(s["k2_psum"], 1)
            pe.wait_ge(s["q2_ready"], 1)
            pe.wait_ge(s["k2_ready"], 1)
            for b in range(B):
                ins = mm(ps[:, 4, b * N:(b + 1) * N], t0[:, b * N:(b + 1) * N], t1[:, b * N:(b + 1) * N], start=True, stop=True)
            ins.then_inc(s["cs_psum"], 1)
            for b in range(B):
                ins = mm(ps[:, 3, b * N:(b + 1) * N], xt(b), w["wqkv_t"][:, 256:384], start=True, stop=True)
            ins.then_inc(s["v2_psum"], 1)
            for b in range(B):
                pe.wait_ge(s["cs_exp"], b + 1)
                ins = tp(ps[:, 5, b * N:(b + 1) * N], lg[:, 0, b * N:(b + 1) * N], ident)
            ins.then_inc(s["pst_psum"], 1)
            pe.wait_ge(s["pst_ready"], 1)
            pe.wait_ge(s["v2_ready"], 1)
            for b in range(B):
                ins = mm(ps[:, 6, b * N:(b + 1) * N], t1[:, b * N:(b + 1) * N], t2[:, b * N:(b + 1) * N], start=True, stop=True)
            ins.then_inc(s["ys_psum"], 1)
            keep_busy("soft mixture's rows", 2)
            transpose_rows(5, 10)
            pe.wait_ge(s["xft_ready"], 1)
            pe.wait_ge(s["set_ready"], 1)
            for k in range(8):
                ins = mm(ps[:, 4 + k // 2, (k % 2) * 256:(k % 2 + 1) * 256], se_t[:, k * 128:(k + 1) * 128], t0[:, :],
                         start=True, stop=True)
                if k % 2:
                    ins.then_inc(s["ls_psum"], 1)

            def combine_logits(b):
                for n in range(2):
                    ins = mm(ps[:, 2 * b + n, :], t0[:, b * N:(b + 1) * N], se_t[:, n * 512:(n + 1) * 512], start=True, stop=True)
                ins.then_inc(s["ln_psum"], 1)

            def transpose_dispatch(g):
                pe.wait_ge(s["dispatch_ready"], g + 1)
                for t in range(4):
                    ins = tp(ps[:, 4 + g, t * 128:(t + 1) * 128], dispatch_t[:, 4 * g + t, :], ident)
                ins.then_inc(s["dt_psum"], 1)

            def fill_slots(n):
                for b in range(B):
                    ins = mm(ps[:, 4 + 2 * n + b, :], xb[:, b, :], dispatch[:, b, n * 512:(n + 1) * 512], start=True, stop=True)
                ins.then_inc(s["sl_psum"], 1)

            def up_gate(e):
                if e >= 2:
                    pe.wait_ge(s["gate_ready"], 2 * (e - 1))
                for k in range(2):
                    ins = mm(ps[:, 4 + e % 2, k * 128:(k + 1) * 128], wg[:, e, k * 128:(k + 1) * 128], slots_t[:, e, :, :],
                             start=True, stop=True)
                ins.then_inc(s["g_psum"], 1)

            def up_linear(e):
                if e >= 2:
                    pe.wait_ge(s["hmid_ready"], 2 * (e - 1))
                for k in range(2):
                    ins = mm(ps[:, 6 + e % 2, k * 128:(k + 1) * 128], wu[:, e, k * 128:(k + 1) * 128], slots_t[:, e, :, :],
                             start=True, stop=True)
                ins.then_inc(s["u_psum"], 1)

            def up(e):
                up_gate(e)
                up_linear(e)

            def down(p):
                if p >= 2:
                    pe.wait_ge(s["eo_ready"], p - 1)
                pe.wait_ge(s["hmid_ready"], 4 * p + 4)
                for b in range(B):
                    for k in range(2):
                        for j in range(2):
                            e = 2 * p + j
                            ins = mm(ps[64 * j:64 * j + 64, 2 + p % 2, b * N:(b + 1) * N],
                                     hmid[:, e % 4, k, b * SLOTS:(b + 1) * SLOTS], wd[:, e, k, :], start=(k == 0), stop=(k == 1))
                ins.then_inc(s["eo_psum"], 1)

            def back(p):
                pe.wait_ge(s["eo_ready"], p + 1)
                for b in range(B):
                    ins = mm(ps[:, b, 0:128], combine_t[:, b, p, :], eo[:, p % 2, b, :], start=(p == 0), stop=(p == PAIRS - 1))
                ins.then_inc(s["y_psum"], 1)

            combine_logits(0)
            transpose_dispatch(0)
            transpose_dispatch(1)
            combine_logits(1)
            transpose_dispatch(2)
            transpose_dispatch(3)
            pe.wait_ge(s["xf_ready"], 1)
            pe.wait_ge(s["dt_dve"], 2)
            fill_slots(0)
            pe.wait_ge(s["dt_act"], 2)
            fill_slots(1)
            for name in ("wg_in", "wu_in", "wd_in"):
                pe.wait_ge(s[name], 32)
            pe.wait_ge(s["slots_ready"], 1)
            up_gate(0)
            up_gate(1)
            pe.wait_ge(s["combine_exp"], 2)
            for b in range(B):
                for k in range(PAIRS):
                    ins = tp(ps[:, 2 * b + k // 4, (k % 4) * 128:(k % 4 + 1) * 128], combine[:, b, k, :], ident)
                ins.then_inc(s["ct_psum"], 1)
            pe.wait_ge(s["slots_ready"], 2)
            up_linear(0)
            up_linear(1)
            up(2)
            pe.wait_ge(s["ct_dve"], 1)
            pe.wait_ge(s["ct_act"], 1)
            down(0)
            up(3)
            for p in range(1, PAIRS):
                if p + 1 < PAIRS:
                    up(2 * p + 2)
                down(p)
                back(p - 1)
                if p + 1 < PAIRS:
                    up(2 * p + 3)
            back(PAIRS - 1)


def kernel(**inputs):
    import numpy as np
    import concourse.bacc as bacc
    from concourse.bass_utils import run_bass_kernel_spmd as run

    i = {name: np.asarray(value) for name, value in inputs.items()}

    def rows(vector):
        return np.broadcast_to(vector.reshape(1, -1), (128, vector.size))

    def col(vector):
        return vector.reshape(128, 1)

    f = np.float32
    j, p = np.arange(N)[:, None], np.arange(N)[None, :]
    e, o = np.arange(E0)[:, None], np.arange(E0)[None, :]
    select = np.zeros((128, 4, DH), f)
    for n in range(4):
        for g in range(4):
            for d in range(DH):
                select[32 * g + DH * n + d, n, d] = 1
    qkv_b = i["L1_attn_b_qkv"]
    parts = {
        "ident": np.eye(128, dtype=f), "x": i["x"].transpose(1, 0, 2).reshape(N, B * D),
        "wq_t": i["L0_xattn_Wq"].T, "wk_t": i["L0_xattn_Wk"].T, "wv_t": i["L0_xattn_Wv"].T, "wo": i["L0_xattn_Wo"],
        "bo_rows": rows(i["L0_xattn_bo"]), "bq": col(i["L0_xattn_bq"]), "bk": col(i["L0_xattn_bk"]),
        "bv": col(i["L0_xattn_bv"]), "decay": rows(i["L0_attn_decay"]), "log_alpha": rows(i["L0_attn_log_alpha"]),
        "wk1": i["L1_xattn_wk_k"], "wk1_b": col(i["L1_xattn_wk_b"]), "wv1": i["L1_xattn_wv_k"],
        "wv1_b_rows": rows(i["L1_xattn_wv_b"]),
        "steps": np.maximum(p - 1 - j, 0).astype(f), "causal": (p > j).astype(f),
        "ww": i["L0_attn_W_write"], "wr_t": i["L0_attn_W_read"].T,
        "wgate_t": i["L0_ffn_w_gate"].T, "lower": rows((o < e).astype(f).reshape(-1)),
        "wfc_t": i["L0_ffn_w_fc"].reshape(E0 * I0, D).T,
        "wproj_t": i["L0_ffn_w_proj"].transpose(0, 2, 1).reshape(4, 128, D).transpose(1, 0, 2).reshape(128, 4 * D),
        "wq1": i["L1_xattn_wq_k"], "wo1": i["L1_xattn_wo_k"], "wo1_b_rows": rows(i["L1_xattn_wo_b"]),
        "wqkv_t": i["L1_attn_W_qkv"].T, "bv_rows": rows(qkv_b[256:384]),
        "future": np.where(p > j, f(CAUSAL), f(0)).astype(f), "select": select.reshape(128, 4 * DH),
        "norm_g_rows": rows(i["L1_ffn_norm_g"]), "norm_b_rows": rows(i["L1_ffn_norm_b"]),
        "bg": i["L1_ffn_bg"].reshape(2 * E1, 128).T, "bu": i["L1_ffn_bu"].reshape(2 * E1, 128).T,
        "wq1_b": col(i["L1_xattn_wq_b"]), "bq_self": col(qkv_b[0:128]), "bk_self": col(qkv_b[128:256]),
        "norm_g": col(i["L1_ffn_norm_g"]), "norm_b": col(i["L1_ffn_norm_b"]), "slot_g": col(i["L1_ffn_slot_g"]),
        "slot_b": col(i["L1_ffn_slot_b"]), "scale": rows(i["L1_ffn_scale"]),
    }
    c = i["ctx_1024"]
    arrays = {
        "start": np.concatenate([parts[n] for n, _ in START], axis=1),
        "first": np.concatenate([parts[n] for n, _ in FIRST], axis=1),
        "second": np.concatenate([parts[n] for n, _ in SECOND], axis=1),
        "third": np.concatenate([parts[n] for n, _ in THIRD], axis=1),
        "ctx_t": c.transpose(2, 0, 1), "ctx_r": c.reshape(B, C, 128, D).transpose(2, 0, 1, 3),
        "g_t": i["fside_BxSxS2_0"].reshape(B, N, C, 128).transpose(3, 0, 2, 1),
        "mask0": i["mask_1xSxS2_if1"][0], "mask1": i["mask_BxSxS2_ik1"].transpose(1, 0, 2),
        "slots": i["L1_ffn_slot_embeds"].reshape(8, 128, D).transpose(1, 0, 2),
        "wg": i["L1_ffn_Wg"].transpose(1, 0, 2), "wu": i["L1_ffn_Wu"].transpose(1, 0, 2),
        "wd": i["L1_ffn_Wd"].reshape(E1, 2, 128, D).transpose(2, 0, 1, 3),
        "bd": np.broadcast_to(i["L1_ffn_bd"].reshape(PAIRS, 2, 1, D).transpose(1, 2, 0, 3), (2, SLOTS, PAIRS, D))
              .reshape(128, PAIRS, D),
    }
    nc = bacc.Bacc("TRN2", target_bir_lowering=False, num_devices=1)
    feeds, aps = {}, {}
    for name, array in arrays.items():
        feeds[f"in_{name}"] = array = np.ascontiguousarray(array)
        aps[name] = nc.dram_tensor(f"in_{name}", array.shape, mybir.dt.from_np(array.dtype), kind="ExternalInput").ap()
    out = nc.dram_tensor("out_0", (B, N, D), F32, kind="ExternalOutput").ap()
    q_dram = nc.dram_tensor("q_dram", (PARTS, B, DH, HEADS, N), BF16, kind="Internal").ap()
    k_dram = nc.dram_tensor("k_dram", (B, HEADS, PARTS, DH, T), BF16, kind="Internal").ap()
    build(nc, aps, out, k_dram, q_dram)
    r = run(nc, [feeds], core_ids=[0])
    return r.results[0]["out_0"]
```
